# Optimizing a Trainium2 kernel written in Bass

```python
import numpy as np
import jax
import jax.numpy as jnp

def _softmax(x, axis=-1):
    return jax.nn.softmax(x, axis=axis)

def _gelu(x):
    return jax.nn.gelu(x, approximate=True)

def _silu(x):
    return jax.nn.silu(x)

def _sigmoid(x):
    return jax.nn.sigmoid(x)

def _layernorm(x, axis=-1, eps=1e-05):
    m = jnp.mean(x, axis=axis, keepdims=True)
    v = jnp.var(x, axis=axis, keepdims=True)
    return (x - m) / jnp.sqrt(v + eps)

def _scatter_add(tgt, idx, src, axis=0):
    return tgt.at[idx].add(src)

def _segment_sum(src, seg, n):
    return jax.ops.segment_sum(src, seg, n)
kernel_name = 'mk_perceiver_d2_seqx_r4_88741a'

def setup_inputs(seed: int=0):
    np.random.seed(seed)
    _w = jnp.asarray

    def _rec_inputs():
        import jax
        import jax.numpy as jnp
        _rk = jax.random.key(seed)
        x = -0.0003929 + 0.9999 * jax.random.normal(jax.random.fold_in(_rk, 1), (32, 64, 256), jnp.float32)
        _lenS = 64 - jax.random.randint(jax.random.fold_in(_rk, 7), (32,), 0, max(1, 64 // 4) + 1, jnp.int32)
        _lenS2 = 1601 - jax.random.randint(jax.random.fold_in(_rk, 8), (32,), 0, max(1, 1601 // 4) + 1, jnp.int32)
        _ctx_1024P = jax.random.normal(jax.random.fold_in(_rk, 11), (32, 16, 256), jnp.float32)
        _ctx_1024c = jax.random.dirichlet(jax.random.fold_in(_rk, 511), 0.3 * jnp.ones((16,), jnp.float32), (32, 1601))
        _ctx_1024t = jnp.einsum('bsk,bkd->bsd', _ctx_1024c, _ctx_1024P)
        _ctx_1024t = _ctx_1024t * jax.lax.rsqrt(jnp.mean(jnp.square(_ctx_1024t)) + 1e-12) * 0.953939
        ctx_1024 = 2.81802e-05 + 1.00001 * (_ctx_1024t + 0.3 * jax.random.normal(jax.random.fold_in(_rk, 611), (32, 1601, 256), jnp.float32))
        return (x, ctx_1024)
    x, ctx_1024 = _rec_inputs()

    def _L0_xattn_setup():
        import jax, jax.numpy as jnp
        import numpy as np
        IN_DIM = 256
        OUT_DIM = 256
        IN_Q_DIM = 256
        HID_Q_DIM = 256
        B, NQ, NK = (8, 512, 512)
        key = jax.random.key(seed)
        k1, k2, k3, k4, k5 = jax.random.split(key, 5)
        scale = 0.02
        return {'q': jax.random.normal(k1, (B, NQ, IN_Q_DIM), dtype=jnp.float32), 'y': jax.random.normal(k2, (B, NK, IN_DIM), dtype=jnp.float32), 'Wq': jax.random.normal(k3, (IN_Q_DIM, HID_Q_DIM), dtype=jnp.float32) * scale, 'Wk': jax.random.normal(k4, (IN_DIM, OUT_DIM), dtype=jnp.float32) * scale, 'Wv': jax.random.normal(k5, (IN_DIM, OUT_DIM), dtype=jnp.float32) * scale}
    _L0_xattn_all = _L0_xattn_setup()
    _L0_xattn_in = {k: v for k, v in _L0_xattn_all.items() if k in ('Wq', 'Wk', 'Wv')}
    del _L0_xattn_all

    def _L0_attn_setup():
        import jax, jax.numpy as jnp
        import numpy as np
        import math
        D_MODEL = 256
        D_QUERY = 64
        key = jax.random.key(seed)
        k1, k2, k3, k4 = jax.random.split(key, 4)
        X = jax.random.normal(k1, (4, 1024, D_MODEL), dtype=jnp.float32)
        Wq = jax.random.normal(k2, (D_MODEL, D_QUERY), dtype=jnp.float32) * (1.0 / math.sqrt(D_MODEL))
        Wk = jax.random.normal(k3, (D_MODEL, D_QUERY), dtype=jnp.float32) * (1.0 / math.sqrt(D_MODEL))
        Wv = jax.random.normal(k4, (D_MODEL, D_MODEL), dtype=jnp.float32) * (1.0 / math.sqrt(D_MODEL))
        return {'X': X, 'Wq': Wq, 'Wk': Wk, 'Wv': Wv}
    _L0_attn_all = _L0_attn_setup()
    _L0_attn_in = {k: v for k, v in _L0_attn_all.items() if k in ('Wq', 'Wk', 'Wv')}
    del _L0_attn_all

    def _L0_ffn_setup():
        import jax, jax.numpy as jnp
        import numpy as np
        B, S, D_MODEL, D_HIDDEN = (4, 512, 256, 1024)

        def act_quant(x):
            scale = 127.0 / jnp.clip(jnp.max(jnp.abs(x), axis=-1, keepdims=True), 1e-05)
            return jnp.clip(jnp.round(x * scale), -128, 127) / scale

        def weight_quant(w):
            scale = 1.0 / jnp.clip(jnp.mean(jnp.abs(w)), 1e-05)
            return jnp.clip(jnp.round(w * scale), -1, 1) / scale

        def bit_linear(x, w):
            xq = x + jax.lax.stop_gradient(act_quant(x) - x)
            wq = w + jax.lax.stop_gradient(weight_quant(w) - w)
            return jnp.einsum('bsd,hd->bsh', xq, wq)

        def depthwise_conv1d(x_bcl, w, b):
            y = jax.lax.conv_general_dilated(x_bcl, w, window_strides=(1,), padding=[(1, 1)], dimension_numbers=('NCH', 'OIH', 'NCH'), feature_group_count=x_bcl.shape[1])
            return y + b[None, :, None]
        key = jax.random.key(seed)
        ks = jax.random.split(key, 5)
        lim1 = 1.0 / np.sqrt(D_MODEL)
        lim2 = 1.0 / np.sqrt(D_HIDDEN)
        limc = 1.0 / np.sqrt(3.0)
        return {'x': jax.random.normal(ks[0], (B, S, D_MODEL), dtype=jnp.float32), 'w1': jax.random.uniform(ks[1], (D_HIDDEN, D_MODEL), jnp.float32, -lim1, lim1), 'conv_w': jax.random.uniform(ks[2], (D_HIDDEN, 1, 3), jnp.float32, -limc, limc), 'conv_b': jax.random.uniform(ks[3], (D_HIDDEN,), jnp.float32, -limc, limc), 'w2': jax.random.uniform(ks[4], (D_MODEL, D_HIDDEN), jnp.float32, -lim2, lim2)}
    _L0_ffn_all = _L0_ffn_setup()
    _L0_ffn_in = {k: v for k, v in _L0_ffn_all.items() if k in ('w1', 'conv_w', 'conv_b', 'w2')}
    del _L0_ffn_all

    def _L1_xattn_setup():
        import jax, jax.numpy as jnp
        import numpy as np
        DIM = 256
        HEADS = 16
        HEAD_DIM = DIM // HEADS
        SCALE = HEAD_DIM ** (-0.5)
        key = jax.random.key(seed)
        ks = jax.random.split(key, 6)
        B, Nq, Nkv = (2, 256, 512)
        s = DIM ** (-0.5)
        return {'x': jax.random.normal(ks[0], (B, Nq, DIM), jnp.float32), 'mem': jax.random.normal(ks[1], (B, Nkv, DIM), jnp.float32), 'W_kv': jax.random.normal(ks[2], (DIM, 2 * DIM), jnp.float32) * s, 'W_q': jax.random.normal(ks[3], (DIM, DIM), jnp.float32) * s, 'W_proj': jax.random.normal(ks[4], (DIM, DIM), jnp.float32) * s, 'b_proj': jax.random.normal(ks[5], (DIM,), jnp.float32) * 0.01}
    _L1_xattn_all = _L1_xattn_setup()
    _L1_xattn_in = {k: v for k, v in _L1_xattn_all.items() if k in ('W_kv', 'W_q', 'W_proj', 'b_proj')}
    del _L1_xattn_all

    def _L1_attn_setup():
        import jax, jax.numpy as jnp
        import numpy as np
        B, S, E, H = (4, 256, 256, 16)
        D = E // H
        NEG_INF = -1000000000.0

        def _xavier(key, shape, fan_in, fan_out):
            a = (6.0 / (fan_in + fan_out)) ** 0.5
            return jax.random.uniform(key, shape, jnp.float32, -a, a)
        key = jax.random.key(seed)
        kx, kq, kk, kv, ko = jax.random.split(key, 5)
        x = jax.random.normal(kx, (B, S, E), jnp.float32)
        Wq = _xavier(kq, (H, D, D), D, D)
        Wk = _xavier(kk, (H, D, D), D, D)
        Wv = _xavier(kv, (H, D, D), D, D)
        W_O = _xavier(ko, (E, E), E, E)
        return {'x': x, 'Wq': Wq, 'Wk': Wk, 'Wv': Wv, 'W_O': W_O}
    _L1_attn_all = _L1_attn_setup()
    _L1_attn_in = {k: v for k, v in _L1_attn_all.items() if k in ('Wq', 'Wk', 'Wv', 'W_O')}
    del _L1_attn_all

    def _L1_ffn_setup():
        import jax, jax.numpy as jnp
        import numpy as np
        TOP_K = 2
        key = jax.random.key(seed)
        ks = jax.random.split(key, 5)
        B, S, H, I, E = (4, 512, 256, 1024, 8)
        scale_hi = (2.0 / (H + I)) ** 0.5
        scale_he = (2.0 / (H + E)) ** 0.5
        return {'x': jax.random.normal(ks[0], (B, S, H), dtype=jnp.float32), 'router_w': jax.random.normal(ks[1], (E, H), dtype=jnp.float32) * scale_he, 'gate_w': jax.random.normal(ks[2], (E, I, H), dtype=jnp.float32) * scale_hi, 'up_w': jax.random.normal(ks[3], (E, I, H), dtype=jnp.float32) * scale_hi, 'down_w': jax.random.normal(ks[4], (E, H, I), dtype=jnp.float32) * scale_hi}
    _L1_ffn_all = _L1_ffn_setup()
    _L1_ffn_in = {k: v for k, v in _L1_ffn_all.items() if k in ('router_w', 'gate_w', 'up_w', 'down_w')}
    del _L1_ffn_all
    return {'x': x, 'ctx_1024': ctx_1024, 'L0_xattn_Wq': _L0_xattn_in['Wq'], 'L0_xattn_Wk': _L0_xattn_in['Wk'], 'L0_xattn_Wv': _L0_xattn_in['Wv'], 'L0_attn_Wq': _L0_attn_in['Wq'], 'L0_attn_Wk': _L0_attn_in['Wk'], 'L0_attn_Wv': _L0_attn_in['Wv'], 'L0_ffn_w1': _L0_ffn_in['w1'], 'L0_ffn_conv_w': _L0_ffn_in['conv_w'], 'L0_ffn_conv_b': _L0_ffn_in['conv_b'], 'L0_ffn_w2': _L0_ffn_in['w2'], 'L1_xattn_W_kv': _L1_xattn_in['W_kv'], 'L1_xattn_W_q': _L1_xattn_in['W_q'], 'L1_xattn_W_proj': _L1_xattn_in['W_proj'], 'L1_xattn_b_proj': _L1_xattn_in['b_proj'], 'L1_attn_Wq': _L1_attn_in['Wq'], 'L1_attn_Wk': _L1_attn_in['Wk'], 'L1_attn_Wv': _L1_attn_in['Wv'], 'L1_attn_W_O': _L1_attn_in['W_O'], 'L1_ffn_router_w': _L1_ffn_in['router_w'], 'L1_ffn_gate_w': _L1_ffn_in['gate_w'], 'L1_ffn_up_w': _L1_ffn_in['up_w'], 'L1_ffn_down_w': _L1_ffn_in['down_w']}

def reference(x, ctx_1024, L0_xattn_Wq, L0_xattn_Wk, L0_xattn_Wv, L0_attn_Wq, L0_attn_Wk, L0_attn_Wv, L0_ffn_w1, L0_ffn_conv_w, L0_ffn_conv_b, L0_ffn_w2, L1_xattn_W_kv, L1_xattn_W_q, L1_xattn_W_proj, L1_xattn_b_proj, L1_attn_Wq, L1_attn_Wk, L1_attn_Wv, L1_attn_W_O, L1_ffn_router_w, L1_ffn_gate_w, L1_ffn_up_w, L1_ffn_down_w):
    import jax
    import jax.numpy as jnp

    def _L0_xattn_ref(q, y, Wq, Wk, Wv):
        import jax, jax.numpy as jnp
        import numpy as np
        IN_DIM = 256
        OUT_DIM = 256
        IN_Q_DIM = 256
        HID_Q_DIM = 256
        B, NQ, NK = (8, 512, 512)
        q_proj = jnp.einsum('bnd,de->bne', q, Wq)
        k_proj = jnp.einsum('bmd,de->bme', y, Wk)
        v_proj = jnp.einsum('bme,ef->bmf', k_proj, Wv)
        scores = jnp.einsum('bne,bme->bnm', q_proj, k_proj) / jnp.sqrt(jnp.float32(OUT_DIM))
        attn = jax.nn.softmax(scores, axis=-1)
        return jnp.einsum('bnm,bmf->bnf', attn, v_proj)

    def _L0_attn_ref(X, Wq, Wk, Wv):
        import jax, jax.numpy as jnp
        import numpy as np
        import math
        D_MODEL = 256
        D_QUERY = 64
        B, T, _ = X.shape
        Q = X @ Wq
        K = X @ Wk
        V = X @ Wv
        scores = jnp.einsum('btd,bsd->bts', Q, K)
        causal = jnp.tril(jnp.ones((T, T), dtype=bool))
        scores = jnp.where(causal[None, :, :], scores, -jnp.inf)
        attn = jax.nn.softmax(scores / math.sqrt(D_QUERY), axis=2)
        return attn @ V

    def _L0_ffn_ref(x, w1, conv_w, conv_b, w2):
        import jax, jax.numpy as jnp
        import numpy as np
        B, S, D_MODEL, D_HIDDEN = (4, 512, 256, 1024)

        def act_quant(x):
            scale = 127.0 / jnp.clip(jnp.max(jnp.abs(x), axis=-1, keepdims=True), 1e-05)
            return jnp.clip(jnp.round(x * scale), -128, 127) / scale

        def weight_quant(w):
            scale = 1.0 / jnp.clip(jnp.mean(jnp.abs(w)), 1e-05)
            return jnp.clip(jnp.round(w * scale), -1, 1) / scale

        def bit_linear(x, w):
            xq = x + jax.lax.stop_gradient(act_quant(x) - x)
            wq = w + jax.lax.stop_gradient(weight_quant(w) - w)
            return jnp.einsum('bsd,hd->bsh', xq, wq)

        def depthwise_conv1d(x_bcl, w, b):
            y = jax.lax.conv_general_dilated(x_bcl, w, window_strides=(1,), padding=[(1, 1)], dimension_numbers=('NCH', 'OIH', 'NCH'), feature_group_count=x_bcl.shape[1])
            return y + b[None, :, None]
        h = bit_linear(x, w1)
        h = depthwise_conv1d(h.transpose(0, 2, 1), conv_w, conv_b)
        h = h.transpose(0, 2, 1)
        h = jax.nn.silu(h)
        return bit_linear(h, w2)

    def _L1_xattn_ref(x, mem, W_kv, W_q, W_proj, b_proj):
        import jax, jax.numpy as jnp
        import numpy as np
        DIM = 256
        HEADS = 16
        HEAD_DIM = DIM // HEADS
        SCALE = HEAD_DIM ** (-0.5)
        B, Nkv, C = mem.shape
        Nq = x.shape[1]
        kv = (mem @ W_kv).reshape(B, Nkv, 2, HEADS, HEAD_DIM)
        k = kv[:, :, 0].transpose(0, 2, 1, 3)
        v = kv[:, :, 1].transpose(0, 2, 1, 3)
        q = (x @ W_q).reshape(B, Nq, HEADS, HEAD_DIM).transpose(0, 2, 1, 3)
        attn = jnp.einsum('bhqd,bhkd->bhqk', q, k) * SCALE
        attn = jax.nn.softmax(attn, axis=-1)
        out = jnp.einsum('bhqk,bhkd->bhqd', attn, v)
        out = out.transpose(0, 2, 1, 3).reshape(B, Nq, C)
        return out @ W_proj + b_proj

    def _L1_attn_ref(x, Wq, Wk, Wv, W_O):
        import jax, jax.numpy as jnp
        import numpy as np
        B, S, E, H = (4, 256, 256, 16)
        D = E // H
        NEG_INF = -1000000000.0

        def _xavier(key, shape, fan_in, fan_out):
            a = (6.0 / (fan_in + fan_out)) ** 0.5
            return jax.random.uniform(key, shape, jnp.float32, -a, a)
        b, s, e = x.shape
        h = Wq.shape[0]
        d = e // h
        xh = x.reshape(b, s, h, d).transpose(0, 2, 1, 3)
        Q = jnp.einsum('bhsd,hde->bhse', xh, Wq)
        K = jnp.einsum('bhsd,hde->bhse', xh, Wk)
        V = jnp.einsum('bhsd,hde->bhse', xh, Wv)
        scale = 1.0 / jnp.sqrt(jnp.asarray(d, x.dtype))
        scores = jnp.einsum('bhsd,bhtd->bhst', Q, K) * scale
        causal = jnp.tril(jnp.ones((s, s), bool))
        scores = jnp.where(causal, scores, NEG_INF)
        attn = jax.nn.softmax(scores, axis=-1)
        out = jnp.einsum('bhst,bhtd->bhsd', attn, V)
        cat = out.transpose(0, 2, 1, 3).reshape(b, s, e)
        scrambled = cat.transpose(0, 2, 1).reshape(b, s, e)
        return scrambled @ W_O

    def _L1_ffn_ref(x, router_w, gate_w, up_w, down_w):
        import jax, jax.numpy as jnp
        import numpy as np
        TOP_K = 2
        B, S, H = x.shape
        E = router_w.shape[0]
        xf = x.reshape(-1, H)
        logits = xf @ router_w.T
        probs = jax.nn.softmax(logits, axis=-1)
        topk_p, topk_i = jax.lax.top_k(probs, TOP_K)
        topk_p = topk_p / topk_p.sum(axis=-1, keepdims=True)

        def body(out, inputs):
            e, gw, uw, dw = inputs
            sel = topk_i == e
            mask = sel.any(axis=-1)
            w_tok = (topk_p * sel).sum(axis=-1)
            cnt = mask.sum().astype(xf.dtype)
            mean_w = jnp.where(cnt > 0, w_tok.sum() / jnp.maximum(cnt, 1.0), 0.0)
            h = jax.nn.silu(xf @ gw.T) * (xf @ uw.T)
            eo = h @ dw.T
            out = out + mask[:, None].astype(xf.dtype) * eo * mean_w
            return (out, None)
        out0 = jnp.zeros_like(xf)
        out, _ = jax.lax.scan(body, out0, (jnp.arange(E), gate_w, up_w, down_w))
        return out.reshape(B, S, H)
    x = x + _L0_xattn_ref(_layernorm(x, axis=-1), ctx_1024, L0_xattn_Wq, L0_xattn_Wk, L0_xattn_Wv)
    x = x + _L0_attn_ref(_layernorm(x, axis=-1), L0_attn_Wq, L0_attn_Wk, L0_attn_Wv)
    x = x + _L0_ffn_ref(_layernorm(x, axis=-1), L0_ffn_w1, L0_ffn_conv_w, L0_ffn_conv_b, L0_ffn_w2)
    x = x + _L1_xattn_ref(_layernorm(x, axis=-1), ctx_1024, L1_xattn_W_kv, L1_xattn_W_q, L1_xattn_W_proj, L1_xattn_b_proj)
    x = x + _L1_attn_ref(_layernorm(x, axis=-1), L1_attn_Wq, L1_attn_Wk, L1_attn_Wv, L1_attn_W_O)
    x = x + _L1_ffn_ref(_layernorm(x, axis=-1), L1_ffn_router_w, L1_ffn_gate_w, L1_ffn_up_w, L1_ffn_down_w)
    return x

_drawn_inputs = setup_inputs


def setup_inputs(seed=0):
    import zlib

    import numpy as np

    out = dict(_drawn_inputs(seed))
    spreads = {}
    factors = {'L0_xattn_Wq': 8.0, 'L1_xattn_b_proj': 3.477}
    for name, (base, spread) in spreads.items():
        noise = np.random.default_rng([zlib.crc32(name.encode()), seed]).standard_normal(out[name].shape)
        drawn = base * np.exp(spread * noise) if base else spread * noise
        out[name] = jnp.asarray(drawn.astype(out[name].dtype))
    for name, factor in factors.items():
        out[name] = (out[name] * factor).astype(out[name].dtype)
    return out
```

```python
from contextlib import ExitStack

import concourse.bass as bass
from concourse import mybir

ALU = mybir.AluOpType
ACT = mybir.ActivationFunctionType
F32 = mybir.dt.float32
F32R = mybir.dt.float32r
BF16 = mybir.dt.bfloat16
AX = mybir.AxisListType.X

P = 128
B, S, D = 32, 64, 256
NK = 1601
NKP = NK + 1
TILES = B * S // P
KT = D // P
KEY_TILES = -(-NK // P)
LAST_KEYS = NK - (KEY_TILES - 1) * P
HEADS, HD = 16, 16
PAIRS = HEADS // 2
HPT = P // HD
HID = 1024
HT = HID // P
EXPERTS = 8
CHUNK = 512
CHUNKS = B * S // CHUNK
TPC = CHUNK // P
BPC = CHUNK // S
EPS = 1e-5
MASKED = -1e30
MAGIC = 12582912.0
KEY_CHUNKS = [(c, min(512, NK - c)) for c in range(0, NK, 512)]
KEY_CHUNKS_EVEN = [(c, min(512, NKP - c)) for c in range(0, NKP, 512)]
MAX_UNITS = 2 * PAIRS
K_PIECES = [("k", o, c) for o in range(KT) for c in range(len(KEY_CHUNKS_EVEN))]
V_PIECES = [("v", t, min(t + 2, KEY_TILES)) for t in range(0, KEY_TILES, 2)]
PIECES = K_PIECES + V_PIECES
PROBS = 3
QUARTERS = 4
HPQ = HEADS // QUARTERS

WEIGHTS = dict(sq=64, sk=64, sv=D, ck=D, cv=D, cq=D, cp=D, hq=P, hk=P, hv=P, router=EXPERTS)


def keys_of(t):
    return P if t < KEY_TILES - 1 else LAST_KEYS


class Tally:

    def __init__(self, **per):
        self.base, self.done, self.trip, self.per = 0, 0, None, per
        self.rate = 0

    def up(self, n=1):
        self.done += n
        return self.now()

    def now(self, less=0):
        fixed = self.base + self.done - less
        return fixed if self.trip is None else self.trip * self.rate + fixed

    def enter(self, phase, trip):
        self.base, self.done, self.trip, self.rate = self.base + self.done, 0, trip, self.per.get(phase, 0)

    def leave(self, phase, trips):
        assert self.done == self.rate, (phase, self.done, self.rate)
        self.base, self.done, self.trip = self.base + trips * self.rate, 0, None


def build(nc, io, out):
    ctx = ExitStack()
    with ctx:
        def sb(name, shape, dt=F32):
            return ctx.enter_context(nc.sbuf_tensor(name, shape, dt))

        def sem(name):
            return ctx.enter_context(nc.semaphore(name))

        x = sb("x", [P, TILES, D])
        ctxT = sb("ctxT", [P, 2, KT * NKP])
        ctxN = sb("ctxN", [P, 2, KEY_TILES, D])
        kT = sb("kT", [P, 2, KT * NKP])
        kTr = sb("kTr", [P, KT, NKP], F32R)
        probs = sb("probs", [P, PROBS, HEADS * S])
        probs_sum = sb("probs_sum", [P, HEADS * S])
        qbd = sb("qbd", [P, 2, KT, HPT * S])
        qbdr = sb("qbdr", [P, 2, KT, HPT * S], F32R)
        shift = sb("shift", [P, HEADS * S], BF16)
        ident = sb("ident", [P, P])
        identb = sb("identb", [P, P], BF16)
        ones = sb("ones", [P, P])
        onesb = sb("onesb", [P, P], BF16)
        head_of = sb("head_of", [P, HPT])
        parity = sb("parity", [P, 2])
        causal = sb("causal", [P, P])
        neghalf = sb("neghalf", [P, 1])
        eps = sb("eps", [P, 1])
        carrier_g = sb("carrier_g", [P, HT])
        carrier_v = sb("carrier_v", [P, 1])
        rank = sb("rank", [P, EXPERTS])
        xn = sb("xn", [P, D])
        xnT = sb("xnT", [P, KT, P])
        big = sb("big", [P, 4096])
        w = {n: sb("w_" + n, [P, KT, width]) for n, width in WEIGHTS.items()}
        fold = sb("fold", [P, KT, D])
        vout = sb("vout", [P, KT, D])
        wo = sb("wo", [P, 4, D])
        bias_p = sb("bias_p", [P, D])
        convw = sb("convw", [P, HT, 3])
        convb = sb("convb", [P, HT])
        w1q = sb("w1q", [P, KT, HID], BF16)
        w2q = sb("w2q", [P, HT, D], BF16)
        stat = sb("stat", [P, 6])
        mv = sb("mv", [P, 2])
        rstd = sb("rstd", [P, 2])
        small = sb("small", [P, 96])
        mpart = sb("mpart", [P, PAIRS, 2])
        m8 = sb("m8", [P, 40])
        sh8 = sb("sh8", [40, 2, P], BF16)
        attn_ch = sb("attn_ch", [P, KT, P])
        PS = ctx.enter_context(nc.psum_tensor("PS", [P, 8 * 512], F32))

        def bank(n, width=512, rows=slice(0, P), at=0):
            return PS[rows, 512 * n + at:512 * n + at + width]

        ctxTv = ctxT[:, :, :].rearrange("p b (k n) -> p b k n", k=KT)
        kTv = kT[:, :, :].rearrange("p b (k n) -> p b k n", k=KT)
        ctxNf = ctxN[:, :, :, :].rearrange("p b t n -> p (b t n)")
        probsA = big[:, 0:NK]
        probsAT = big[:, 1664:1664 + KEY_TILES * P].rearrange("p (t q) -> p t q", q=P)
        qkT = big[:, 3328:3584].rearrange("p (k t) -> p k t", k=KT)
        qk_s = kT[0:64, 0, 0:256]
        v_s = kT[:, 0, 256:512]
        s_s = kT[:, 0, 512:640]
        p_s = kT[:, 0, 640:768]
        pT_s = kT[:, 0, 768:896]
        hs = ctxNf[:, 0:HT * CHUNK].rearrange("p (j t) -> p j t", j=HT)
        hq = qbd[:, :, :, :].rearrange("p b k n -> p (b k n)").bitcast(BF16).rearrange("p (j t) -> p j t", j=HT)
        xq = big[:, 0:128].bitcast(BF16)
        xqT = big[:, 128:640].bitcast(BF16).rearrange("p (k t) -> p k t", k=KT)
        diag = big[:, 640:1152].rearrange("p (k t) -> p k t", k=TPC)
        rowscale = big[:, 1152:1664]
        hpad = [kT[:, 0, 600 * n:600 * n + BPC * (S + 2)].rearrange("p (b t) -> p b t", b=BPC) for n in range(3)]
        hacc = [kT[:, 1, 512 * n:512 * n + 512] for n in range(2)]
        hmax = big[:, 1664:2176]
        qT = big[:, 0:256].rearrange("p (k t) -> p k t", k=KT)
        sqT = big[:, 256:512].rearrange("p (k t) -> p k t", k=KT)
        skT = big[:, 512:768].rearrange("p (k t) -> p k t", k=KT)
        s4 = big[:, 768:1280].rearrange("p (h t) -> p h t", h=HPQ)
        skbd = big[:, 1280:3328].rearrange("p (k h t) -> p k h t", k=KT, h=HPT)
        v4 = big[:, 3328:3584]
        p4T = big[:, 3584:4096].rearrange("p (h t) -> p h t", h=HPQ)
        cat = sb("cat", [P, D])
        gates = sb("gates", [P, TILES, EXPERTS])
        weighed_sb = sb("weighed", [P, D])
        xnTall = big[:, :].rearrange("p (k t) -> p k t", k=KT)
        hM = ctxNf[:, 0:HT * CHUNK].rearrange("p (j t) -> p j t", j=HT)
        expert_w = [t[:, :, :].rearrange("p b n -> p (b n)")[:, 0:6144] for t in (ctxT, kT)]
        silu_g = [probs[:, n, 0:512] for n in range(2)]
        rt = probs_sum[:, :]
        logits, rp, ro1, ro2, rc = (rt[:, 128 * n:128 * n + 128].rearrange("p (t e) -> p t e", e=EXPERTS) for n in range(5))
        rsmall = qbd[:, 0, 0, :]

        S_ = {n: sem(n) for n in """
            weights_in consts_ready ctxT_in ctxN_in ctxB0_in ctxB1_in expert0_in expert1_in out_stored
            vec_step pool_step act_step ln_var ln_rstd xn_ready xn_ps xnT_ready
            fold_ps fold_ready tern_sum tern_ps
            qk_ps qk_ready scores_ps nmax_ready probsA_ready pT_ps pT_ready av_ps att_ready attT_ps attT_ready outA_ps x_done
            qkv_ps qkv_ready ss_ps snmax_ready sp_ready spT_ps spT_ready so_ps
            xq_ready xqT_ps xqT_ready diag_ready rows_ps rows_ready h_ps h_scaled conv_mid conv_done silu_done
            hmax_ready hmaxT_ps hq_ready o_ps
            proj_ps proj_sb kTr_ready mx_ps mx_red m8_ready m8T_ps shift_ready
            qB_ps qB_ready qbd_ready qbdr_ready sc_ps pr_ready pv_done sum_done den_ps attn_ready
            po_ps sqkv_ps sqkv_ready skbd_ready s4_ps s4_masked p4_ready p4T_ps p4T_ready o4_ps cat_ready wo_ps
            xT_all logits_ps logits_sb gates_ready rexp_in rexp_out rsum_ready rsum_ps g_ps u_ps silu_g_ready hM_ready eo_ps eo_added
            """.split()}
        s = type("Sems", (), S_)

        n_weights = [0]
        block = ctx.enter_context(nc.Block())
        NCONST = 22

        raw = ctxNf
        wqT_raw, wkT_raw, wv_raw = (raw[:, 512 * n:512 * n + 512].rearrange("p (k n) -> p k n", k=KT) for n in range(3))
        w1_raw = kT[:, 0, 0:KT * HID]
        w2_raw = kT[:, 1, 0:HT * D]
        loads = [(w[n][:, :, :], io["w_" + n]) for n in WEIGHTS] + [
            (wqT_raw, io["w_xqT"]), (wkT_raw, io["w_xkT"]), (wv_raw, io["w_xv"]),
            (w1_raw, io["w1T"]), (w2_raw, io["w2T"]), (wo[:, :, :], io["w_o"]),
            (bias_p[:, :], io["b_p"]), (convw[:, :, :], io["conv_w"]), (convb[:, :], io["conv_b"]),
            (x[:, :, :], io["x"])]
        WEIGHTS_IN = 16 * len(loads)
        XDONE_A = 2 * TILES
        XDONE_F = XDONE_A + TILES
        XDONE_B = XDONE_F + 3 * TILES
        XNT_READY_B = 4 * TILES

        @block.sync
        def _(sp):
            for dst, src in loads:
                sp.dma_start(dst, src).then_inc(s.weights_in, 16)

            def pair_of(src, i):
                return src[bass.ds(2 * i, 2), :, :].rearrange("b p n -> p b n")

            sp.dma_start(ctxT[:, :, :], pair_of(io["ctxT"], 0)).then_inc(s.ctxT_in, 16)
            sp.wait_ge(s.fold_ps, 2)
            nkeys = ctxN[:, :, :, :].rearrange("p b t n -> p b (t n)")
            sp.dma_start(nkeys, pair_of(io["ctxN"], 0)).then_inc(s.ctxN_in, 16)
            with sp.Fori(1, TILES) as i:
                sp.wait_ge(s.scores_ps, i)
                sp.dma_start(ctxT[:, :, :], pair_of(io["ctxT"], i)).then_inc(s.ctxT_in, 16)
                sp.wait_ge(s.av_ps, i)
                sp.dma_start(nkeys, pair_of(io["ctxN"], i)).then_inc(s.ctxN_in, 16)
            sp.wait_ge(s.scores_ps, TILES)
            for n in range(2):
                sp.dma_start(ctxT[:, n, :], io["ctxT"][n, :, :]).then_inc((s.ctxB0_in, s.ctxB1_in)[n], 16)
            with sp.Fori(1, TILES) as i:
                for n in range(2):
                    sp.wait_ge(s.proj_ps, i * (2 * len(PIECES)) + (n - 1) * len(PIECES))
                    sp.dma_start(ctxT[:, n, :], io["ctxT"][bass.ds(2 * i + n, 1), :, :].rearrange("b p n -> (b p) n"))\
                      .then_inc((s.ctxB0_in, s.ctxB1_in)[n], 16)
            sp.wait_ge(s.proj_ps, B * len(PIECES))
            sp.dma_start(expert_w[0], io["experts"][0, :, :]).then_inc(s.expert0_in, 16)
            sp.wait_ge(s.x_done, XDONE_B)
            sp.dma_start(expert_w[1], io["experts"][1, :, :]).then_inc(s.expert1_in, 16)
            with sp.Fori(1, EXPERTS // 2) as i:
                for n in range(2):
                    sp.wait_ge(s.eo_ps, i * (2 * CHUNKS * TPC) + (n - 1) * CHUNKS * TPC)
                    sp.dma_start(expert_w[n], io["experts"][bass.ds(2 * i + n, 1), :, :].rearrange("e p n -> (e p) n"))\
                      .then_inc((s.expert0_in, s.expert1_in)[n], 16)
            sp.wait_ge(s.eo_added, EXPERTS * CHUNKS * TPC)
            sp.dma_start(out, x[:, :, :]).then_inc(s.out_stored, 16)
            sp.wait_ge(s.out_stored, 16)

        @block.gpsimd
        def _(g):
            step = Tally(A=2 * 1, F=TPC * 1, B=2, M=1)
            var = Tally(A=2, F=TPC, B=2, M=1)

            g.memset(ident[:, :], 0.0).then_inc(s.consts_ready, 1)
            g.memset(ones[:, :], 1.0).then_inc(s.consts_ready, 1)
            g.memset(onesb[:, :], 1.0).then_inc(s.consts_ready, 1)
            g.memset(head_of[:, :], 1.0).then_inc(s.consts_ready, 1)
            g.memset(causal[:, :], 0.0).then_inc(s.consts_ready, 1)
            g.memset(neghalf[:, :], -0.5).then_inc(s.consts_ready, 1)
            g.memset(eps[:, :], EPS).then_inc(s.consts_ready, 1)
            g.memset(shift[:, :], 0.0).then_inc(s.consts_ready, 1)
            g.memset(m8[:, :], 0.0).then_inc(s.consts_ready, 1)
            for e in range(EXPERTS):
                g.memset(rank[:, e:e + 1], float(EXPERTS - e)).then_inc(s.consts_ready, 1)
            g.wait_ge(s.consts_ready, 17)
            g.affine_select(out=ident[:, :], in_=ident[:, :], compare_op=ALU.not_equal, fill=1.0, base=0,
                            pattern=[[-1, P]], channel_multiplier=1).then_inc(s.consts_ready, 1)
            g.affine_select(out=head_of[:, :], in_=head_of[:, :], compare_op=ALU.is_ge, fill=0.0, base=0,
                            pattern=[[-HD, HPT]], channel_multiplier=1).then_inc(s.consts_ready, 1)
            g.affine_select(out=causal[:, :], in_=causal[:, :], compare_op=ALU.is_ge, fill=MASKED, base=0,
                            pattern=[[-1, P]], channel_multiplier=1).then_inc(s.consts_ready, 1)
            g.wait_ge(s.consts_ready, 20)
            g.affine_select(out=head_of[:, :], in_=head_of[:, :], compare_op=ALU.is_ge, fill=0.0, base=HD - 1,
                            pattern=[[HD, HPT]], channel_multiplier=-1).then_inc(s.consts_ready, 1)
            g.wait_ge(s.consts_ready, 21)
            g.memset(causal[S:P, 0:S], MASKED).then_inc(s.consts_ready, 1)

            def rsqrt():
                g.wait_ge(s.ln_var, var.up())
                g.tensor_tensor(rstd[:, 0:1], mv[:, 1:2], eps[:, :], ALU.add).then_inc(s.pool_step, 1)
                g.wait_ge(s.pool_step, step.up())
                g.tensor_tensor(rstd[:, 1:2], rstd[:, 0:1], neghalf[:, :], ALU.pow).then_inc(s.ln_rstd, 1)

            def enter(phase, i):
                for t in (step, var):
                    t.enter(phase, i)

            def leave(phase, n):
                for t in (step, var):
                    t.leave(phase, n)

            with g.Fori(0, TILES) as i:
                enter("A", i)
                rsqrt()
                rsqrt()
            leave("A", TILES)
            hsc = Tally(F=HT)
            with g.Fori(0, CHUNKS) as c:
                enter("F", c)
                hsc.enter("F", c)
                for k in range(TPC):
                    rsqrt()
                for j in range(HT):
                    if j >= 2:
                        g.wait_ge(s.silu_done, c * HT + j - 1)
                    g.wait_ge(s.h_scaled, hsc.up())
                    g.tensor_tensor(carrier_g[:, j:j + 1], eps[:, :], eps[:, :], ALU.add)
                    g.tensor_scalar(hacc[j % 2].rearrange("p (b t) -> p b t", b=BPC), hpad[j % 3][:, :, 1:S + 1],
                                    convw[:, j, 1:2], convb[:, j:j + 1], ALU.mult, ALU.add).then_inc(s.conv_mid, 1)
            leave("F", CHUNKS)
            psb = Tally(B=2 * len(PIECES))
            mxp = Tally(B=2 * MAX_UNITS)
            qb = Tally(B=1)

            def round_keys(n):
                g.wait_ge(s.proj_sb, psb.up(len(PIECES)))
                g.tensor_tensor(carrier_g[:, 0:1], eps[:, :], eps[:, :], ALU.add)
                g.tensor_copy(kTr[:, :, :], kTv[:, n, :, :]).then_inc(s.kTr_ready, 1)

            def pool_pair(i, last):
                g.wait_ge(s.qB_ready, qb.up())
                for b in range(2):
                    for a in range(KT):
                        g.tensor_tensor(qbdr[:, b, a, :].rearrange("p (h q) -> p h q", h=HPT),
                                        qT[:, a, None, b * S:b * S + S].broadcast_to([P, HPT, S]),
                                        head_of[:, :, None].broadcast_to([P, HPT, S]), ALU.mult).then_inc(s.qbdr_ready, 1)
                for b in range(2):
                    if not (last and b == 1):
                        g.wait_ge(s.mx_ps, mxp.up(MAX_UNITS))
                        round_keys((b + 1) % 2)
                rsqrt()
                g.wait_ge(s.sqkv_ready, sqk.up(3))
                for a in range(KT):
                    g.tensor_tensor(skbd[:, a, :, :], skT[:, a, None, :].broadcast_to([P, HPT, P]),
                                    head_of[:, :, None].broadcast_to([P, HPT, P]), ALU.mult).then_inc(s.skbd_ready, 1)

            sqk = Tally(B=3)
            g.wait_ge(s.x_done, XDONE_F)
            round_keys(0)
            bt = (psb, mxp, qb, sqk)
            with g.Fori(0, TILES - 1) as i:
                enter("B", i)
                for t in bt:
                    t.enter("B", i)
                rsqrt()
                pool_pair(i, False)
            leave("B", TILES - 1)
            for t in bt:
                t.leave("B", TILES - 1)
            rsqrt()
            pool_pair(TILES - 1, True)
            xt = Tally(M=1)
            with g.Fori(0, TILES) as i:
                enter("M", i)
                xt.enter("M", i)
                rsqrt()
                g.wait_ge(s.xnT_ready, XNT_READY_B + xt.up())
                g.tensor_copy(xnTall[:, :, bass.ds(i * P, P)], xnT[:, :, :]).then_inc(s.xT_all, 1)

        @block.scalar
        def _(act):
            names = dict(xn_ps=dict(A=2, B=2, M=1), qk_ps=dict(A=1), nmax=dict(A=1), attT=dict(A=1), qkv=dict(A=1),
                         snmax=dict(A=1), spT=dict(A=1),
                         xqT=dict(F=TPC), rows=dict(F=2), conv=dict(F=HT),
                         proj=dict(B=2 * len(PIECES)), sc=dict(B=2 * KEY_TILES), pv=dict(B=2 * KEY_TILES),
                         qB=dict(B=1), sqkv=dict(B=1), s4=dict(B=QUARTERS), p4T=dict(B=QUARTERS))
            T = {k: Tally(**v) for k, v in names.items()}

            def enter(phase, i):
                for t in T.values():
                    t.enter(phase, i)

            def leave(phase, n):
                for t in T.values():
                    t.leave(phase, n)

            def copy_xnT():
                act.wait_ge(s.xn_ps, T["xn_ps"].up())
                act.copy(xnT[:, :, :].rearrange("p k t -> p (k t)"), bank(0, 256)).then_inc(s.xnT_ready, 1)

            act.wait_ge(s.consts_ready, NCONST)
            act.copy(identb[:, :], ident[:, :]).then_inc(s.consts_ready, 1)
            act.wait_ge(s.fold_ps, 1)
            act.copy(fold[:, :, :].rearrange("p k n -> p (k n)"), bank(0)).then_inc(s.fold_ready, 1)
            act.wait_ge(s.fold_ps, 2)
            act.copy(vout[:, :, :].rearrange("p k n -> p (k n)"), bank(1)).then_inc(s.fold_ready, 1)

            with act.Fori(0, TILES) as i:
                enter("A", i)
                copy_xnT()
                act.wait_ge(s.qk_ps, T["qk_ps"].up())
                act.copy(qkT.rearrange("p k t -> p (k t)"), bank(1, 256)).then_inc(s.qk_ready, 1)
                act.wait_ge(s.nmax_ready, T["nmax"].up())
                act.activation(probsA, PS[:, 2048:2048 + NK], ACT.Exp, bias=small[:, 1:2], scale=1 / 16,
                               accum_out=small[:, 2:3]).then_inc(s.probsA_ready, 1)
                act.wait_ge(s.attT_ps, T["attT"].up())
                act.copy(xnT[:, :, :].rearrange("p k t -> p (k t)"), bank(0, 256)).then_inc(s.attT_ready, 1)
                copy_xnT()
                act.wait_ge(s.qkv_ps, T["qkv"].up())
                act.copy(qk_s, bank(1, 256, slice(0, 64))).then_inc(s.qkv_ready, 1)
                act.copy(v_s, bank(2, 256)).then_inc(s.qkv_ready, 1)
                act.wait_ge(s.snmax_ready, T["snmax"].up())
                act.activation(p_s, s_s, ACT.Exp, bias=small[:, 5:6], scale=1 / 8,
                               accum_out=small[:, 6:7]).then_inc(s.sp_ready, 1)
                act.wait_ge(s.spT_ps, T["spT"].up())
                act.copy(pT_s, bank(4, P)).then_inc(s.spT_ready, 1)
            leave("A", TILES)

            with act.Fori(0, CHUNKS) as c:
                enter("F", c)
                for k in range(TPC):
                    act.wait_ge(s.xqT_ps, T["xqT"].up())
                    act.copy(xqT[:, :, k * P:k * P + P], bank(0, P).bitcast(BF16).rearrange("p (k t) -> p k t", k=KT))\
                       .then_inc(s.xqT_ready, 1)
                act.wait_ge(s.rows_ps, T["rows"].up())
                act.copy(rowscale, bank(1)).then_inc(s.rows_ready, 1)
                for j in range(HT):
                    act.wait_ge(s.conv_done, T["conv"].up())
                    act.activation(hs[:, j, :], hacc[j % 2], ACT.Silu).then_inc(s.silu_done, 1)
                act.wait_ge(s.rows_ps, T["rows"].up())
                act.copy(rowscale, bank(5)).then_inc(s.rows_ready, 1)
            leave("F", CHUNKS)

            def evac(piece, n):
                act.wait_ge(s.proj_ps, T["proj"].up())
                at = 5 + pieces_evac[0] % 2
                pieces_evac[0] += 1
                kind, a, b = piece
                if kind == "k":
                    c, width = KEY_CHUNKS_EVEN[b]
                    act.copy(kTv[:, n, a, c:c + width], bank(at, width)).then_inc(s.proj_sb, 1)
                elif b - a == 2:
                    act.copy(ctxN[:, n, a:b, :].rearrange("p t n -> p (t n)"), bank(at)).then_inc(s.proj_sb, 1)
                else:
                    act.copy(ctxN[0:LAST_KEYS, n, a, :], bank(at, D, slice(0, LAST_KEYS))).then_inc(s.proj_sb, 1)

            pieces_evac = [0]

            def act_pair(last):
                copy_xnT()
                act.wait_ge(s.qB_ps, T["qB"].up())
                act.mul(qT.rearrange("p k t -> p (k t)"), bank(7, 256), HD ** -0.5).then_inc(s.qB_ready, 1)
                for b in range(2):
                    if not (last and b == 1):
                        pieces_evac[0] = 0
                        for piece in PIECES:
                            evac(piece, (b + 1) % 2)
                    for t in range(KEY_TILES):
                        rows = slice(0, keys_of(t))
                        act.wait_ge(s.sc_ps, T["sc"].up())
                        if t >= PROBS:
                            act.wait_ge(s.sum_done, T["pv"].now() + t - PROBS + 1)
                        act.activation(probs[rows, t % PROBS, :], PS[rows, 1024 * (t % 2):1024 * (t % 2) + 1024],
                                       ACT.Exp).then_inc(s.pr_ready, 1)
                    T["pv"].up(KEY_TILES)
                copy_xnT()
                act.wait_ge(s.sqkv_ps, T["sqkv"].up())
                act.copy(sqT.rearrange("p k t -> p (k t)"), bank(7, 256)).then_inc(s.sqkv_ready, 1)
                act.copy(skT.rearrange("p k t -> p (k t)"), bank(7, 256, at=256)).then_inc(s.sqkv_ready, 1)
                act.copy(v4, bank(5, 256)).then_inc(s.sqkv_ready, 1)
                for q in range(QUARTERS):
                    act.wait_ge(s.s4_masked, T["s4"].up())
                    act.activation(s4, s4, ACT.Exp, scale=HD ** -0.5).then_inc(s.p4_ready, 1)
                    act.wait_ge(s.p4T_ps, T["p4T"].up())
                    act.copy(p4T.rearrange("p h t -> p (h t)"), bank(7)).then_inc(s.p4T_ready, 1)

            act.wait_ge(s.x_done, XDONE_F)
            pieces_evac[0] = 0
            for piece in PIECES:
                evac(piece, 0)
            with act.Fori(0, TILES - 1) as i:
                enter("B", i)
                act_pair(False)
            leave("B", TILES - 1)
            act_pair(True)

            with act.Fori(0, TILES) as i:
                enter("M", i)
                copy_xnT()
            leave("M", TILES)
            act.wait_ge(s.rexp_in, 1)
            act.activation(rp, logits, ACT.Exp).then_inc(s.rexp_out, 1)
            with act.Fori(0, EXPERTS // 2) as i:
                for n in range(2 * CHUNKS * HT):
                    act.wait_ge(s.g_ps, i * (2 * CHUNKS * HT) + n + 1)
                    if n >= 2:
                        act.wait_ge(s.hM_ready, i * (2 * CHUNKS * HT) + n - 1)
                    act.activation(silu_g[n % 2], bank(n % 2), ACT.Silu).then_inc(s.silu_g_ready, 1)

        @block.tensor
        def _(pe):
            names = dict(xn=dict(A=2, B=2, M=1), xnT=dict(A=2, B=2, M=1), qk=dict(A=1), probsA=dict(A=1), pT=dict(A=4),
                         att=dict(A=1), attT=dict(A=1), qkv=dict(A=2), sp=dict(A=1), spT=dict(A=1),
                         xq=dict(F=TPC), xqT=dict(F=TPC), diag=dict(F=2), h_scaled=dict(F=HT), hmax=dict(F=1), hq=dict(F=HT),
                         psb=dict(B=2 * len(PIECES)), mx=dict(B=2 * MAX_UNITS), m8=dict(B=2), shift=dict(B=4),
                         kTr=dict(B=2), qbd=dict(B=4), qbdr=dict(B=4), pr=dict(B=2 * KEY_TILES), sum=dict(B=2),
                         attn=dict(B=2), sqkv=dict(B=3), skbd=dict(B=2), s4m=dict(B=QUARTERS), p4=dict(B=QUARTERS), p4T=dict(B=QUARTERS),
                         cat=dict(B=QUARTERS), x_done=dict(A=2, F=TPC, B=3),
                         ctx=dict(A=16), ctxB=dict(B=16))
            T = {k: Tally(**v) for k, v in names.items()}

            def enter(phase, i):
                for t in T.values():
                    t.enter(phase, i)

            def leave(phase, n):
                for t in T.values():
                    t.leave(phase, n)

            pe.wait_ge(s.weights_in, WEIGHTS_IN)
            pe.wait_ge(s.consts_ready, NCONST + 1)
            for o in range(KT):
                for k in range(KT):
                    mm = pe.matmul(bank(0, D, at=o * D), wqT_raw[:, k, o * P:o * P + P], wkT_raw[:, k, :], start=k == 0, stop=k == KT - 1)
            mm.then_inc(s.fold_ps, 1)
            for o in range(KT):
                for k in range(KT):
                    mm = pe.matmul(bank(1, D, at=o * D), wkT_raw[:, k, o * P:o * P + P], wv_raw[:, k, :], start=k == 0, stop=k == KT - 1)
            mm.then_inc(s.fold_ps, 1)
            pe.wait_ge(s.tern_sum, 1)
            pe.matmul(bank(2, 2), ones[:, :], small[:, 0:2], start=True, stop=True).then_inc(s.tern_ps, 1)
            pe.wait_ge(s.fold_ready, 2)

            def transpose_xn():
                pe.wait_ge(s.xn_ready, T["xn"].up())
                for k in range(KT):
                    mm = pe.transpose(bank(0, P, at=k * P), xn[:, k * P:k * P + P], ident[:, :])
                mm.then_inc(s.xn_ps, 1)

            with pe.Fori(0, TILES) as i:
                enter("A", i)
                transpose_xn()
                pe.wait_ge(s.xnT_ready, T["xnT"].up())
                for o in range(KT):
                    for k in range(KT):
                        mm = pe.matmul(bank(1, P, at=o * P), fold[:, k, o * P:o * P + P], xnT[:, k, :], start=k == 0, stop=k == KT - 1)
                mm.then_inc(s.qk_ps, 1)
                pe.wait_ge(s.qk_ready, T["qk"].up())
                pe.wait_ge(s.ctxT_in, T["ctx"].up(16))
                for n, (c, width) in enumerate(KEY_CHUNKS):
                    for k in range(KT):
                        for b in range(2):
                            mm = pe.matmul(bank(4 + n, width, slice(b * S, b * S + S)), qkT[:, k, b * S:b * S + S],
                                           ctxTv[:, b, k, c:c + width], start=k == 0, stop=k == KT - 1)
                mm.then_inc(s.scores_ps, 1)
                pe.wait_ge(s.probsA_ready, T["probsA"].up())
                for t in range(KEY_TILES):
                    mm = pe.transpose(bank(t // 4, P, slice(0, keys_of(t)), (t % 4) * P), probsA[:, t * P:t * P + keys_of(t)], ident[:, :])
                    if t % 4 == 3 or t == KEY_TILES - 1:
                        mm.then_inc(s.pT_ps, 1)
                pe.wait_ge(s.ctxN_in, T["ctx"].now())
                for t in range(KEY_TILES):
                    if t % 4 == 0:
                        pe.wait_ge(s.pT_ready, T["pT"].up())
                    rows = slice(0, keys_of(t))
                    for b in range(2):
                        mm = pe.matmul(bank(4, D, slice(b * S, b * S + S)), probsAT[rows, t, b * S:b * S + S], ctxN[rows, b, t, :],
                                       start=t == 0, stop=t == KEY_TILES - 1)
                mm.then_inc(s.av_ps, 1)
                pe.wait_ge(s.att_ready, T["att"].up())
                for k in range(KT):
                    mm = pe.transpose(bank(0, P, at=k * P), xn[:, k * P:k * P + P], ident[:, :])
                mm.then_inc(s.attT_ps, 1)
                pe.wait_ge(s.attT_ready, T["attT"].up())
                for k in range(KT):
                    mm = pe.matmul(bank(1, D), xnT[:, k, :], vout[:, k, :], start=k == 0, stop=k == KT - 1)
                mm.then_inc(s.outA_ps, 1)
                transpose_xn()
                pe.wait_ge(s.xnT_ready, T["xnT"].up())
                for n, m in enumerate(("sq", "sk")):
                    for k in range(KT):
                        pe.matmul(bank(1, P, slice(0, 64), n * P), w[m][:, k, :], xnT[:, k, :], start=k == 0, stop=k == KT - 1)
                for k in range(KT):
                    mm = pe.matmul(bank(2, D), xnT[:, k, :], w["sv"][:, k, :], start=k == 0, stop=k == KT - 1)
                mm.then_inc(s.qkv_ps, 1)
                pe.wait_ge(s.qkv_ready, T["qkv"].up(2))
                pe.matmul(bank(3, P), qk_s[:, 0:P], qk_s[:, P:2 * P], start=True, stop=True).then_inc(s.ss_ps, 1)
                pe.wait_ge(s.sp_ready, T["sp"].up())
                pe.transpose(bank(4, P), p_s, ident[:, :]).then_inc(s.spT_ps, 1)
                pe.wait_ge(s.spT_ready, T["spT"].up())
                pe.matmul(bank(5, D), pT_s, v_s, start=True, stop=True).then_inc(s.so_ps, 1)
                T["x_done"].up(2)
            leave("A", TILES)

            with pe.Fori(0, CHUNKS) as c:
                enter("F", c)
                for k in range(TPC):
                    pe.wait_ge(s.xq_ready, T["xq"].up())
                    if k:
                        pe.wait_ge(s.xqT_ready, T["xqT"].up())
                    for a in range(KT):
                        mm = pe.transpose(bank(0, P).bitcast(BF16)[:, a * P:a * P + P], xq[:, a * P:a * P + P], identb[:, :])
                    mm.then_inc(s.xqT_ps, 1)
                pe.wait_ge(s.diag_ready, T["diag"].up())
                for k in range(TPC):
                    mm = pe.matmul(bank(1, P, at=k * P), ones[:, :], diag[:, k, :], start=True, stop=True)
                mm.then_inc(s.rows_ps, 1)
                pe.wait_ge(s.xqT_ready, T["xqT"].up())
                for j in range(HT):
                    if j >= 2:
                        pe.wait_ge(s.h_scaled, T["h_scaled"].up())
                    for a in range(KT):
                        mm = pe.matmul(bank(2 + j % 2), w1q[:, a, j * P:j * P + P], xqT[:, a, :], start=a == 0, stop=a == KT - 1)
                    mm.then_inc(s.h_ps, 1)
                T["h_scaled"].up(2)
                pe.wait_ge(s.hmax_ready, T["hmax"].up())
                for k in range(TPC):
                    mm = pe.transpose(bank(4, P, at=k * P), hmax[:, k * P:k * P + P], ident[:, :])
                mm.then_inc(s.hmaxT_ps, 1)
                pe.wait_ge(s.diag_ready, T["diag"].up())
                for k in range(TPC):
                    mm = pe.matmul(bank(5, P, at=k * P), ones[:, :], diag[:, k, :], start=True, stop=True)
                mm.then_inc(s.rows_ps, 1)
                pe.wait_ge(s.hq_ready, T["hq"].up(HT))
                for k in range(TPC):
                    if k >= 2:
                        pe.wait_ge(s.x_done, T["x_done"].up())
                    for j in range(HT):
                        mm = pe.matmul(bank(6 + k % 2, D), hq[:, j, k * P:k * P + P], w2q[:, j, :], start=j == 0, stop=j == HT - 1)
                    mm.then_inc(s.o_ps, 1)
                T["x_done"].up(2)
            leave("F", CHUNKS)

            count = [0]

            def project(piece, n):
                kind, a, b = piece
                at = 5 + count[0] % 2
                count[0] += 1
                if count[0] > 2:
                    pe.wait_ge(s.proj_sb, T["psb"].now() + count[0] - 2)
                if kind == "k":
                    c, width = KEY_CHUNKS_EVEN[b]
                    for k in range(KT):
                        mm = pe.matmul(bank(at, width), w["ck"][:, k, a * P:a * P + P], ctxTv[:, n, k, c:c + width],
                                       start=k == 0, stop=k == KT - 1)
                else:
                    for t in range(a, b):
                        rows = slice(0, keys_of(t))
                        for k in range(KT):
                            mm = pe.matmul(bank(at, D, rows, (t - a) * D), ctxTv[:, n, k, t * P:t * P + keys_of(t)], w["cv"][:, k, :],
                                           start=k == 0, stop=k == KT - 1)
                mm.then_inc(s.proj_ps, 1)

            def maxima(n, u, first):
                pair, half = divmod(u, 2)
                if u >= 2:
                    pe.wait_ge(s.mx_red, T["mx"].now() + u - 1)
                for c, width in KEY_CHUNKS_EVEN[2 * half:2 * half + 2]:
                    at = PS[:, 1024 * (u % 2) + c - 1024 * half:1024 * (u % 2) + c - 1024 * half + width]
                    mm = pe.matmul(at, qbdr[:, n, pair // 4, (pair % 4) * P:(pair % 4) * P + P], kTr[:, pair // 4, c:c + width],
                                   start=True, stop=True)
                mm.then_inc(s.mx_ps, 1)

            def weigh(n, t):
                rows = slice(0, keys_of(t))
                pe.wait_ge(s.pr_ready, T["pr"].up())
                for g in range(KT):
                    for j in range(4):
                        mm = pe.matmul(bank(4, P, slice(32 * j, 32 * j + 32), g * P), ctxN[rows, n, t, g * P + 32 * j:g * P + 32 * j + 32],
                                       probs[rows, t % PROBS, (4 * g + j) * P:(4 * g + j) * P + P],
                                       start=t == 0 and g == 0, stop=t == KEY_TILES - 1, skip_group_check=True)
                mm.then_inc(s.pv_done, 1)

            def pe_batch(n, last):
                count[0] = 0
                pe.wait_ge(s.kTr_ready, T["kTr"].up())
                if n == 0:
                    pe.wait_ge(s.qbdr_ready, T["qbdr"].up(4))
                    pe.wait_ge(s.qbd_ready, T["qbd"].up(4))
                if not (last and n == 1):
                    pe.wait_ge((s.ctxB1_in, s.ctxB0_in)[n], T["ctxB"].now() + (16 if n else 0))
                for u in range(MAX_UNITS):
                    maxima(n, u, False)
                    if u >= 4 and not (last and n == 1):
                        project(PIECES[u - 4], 1 - n)
                T["mx"].up(MAX_UNITS)
                if not (last and n == 1):
                    for piece in PIECES[MAX_UNITS - 4:]:
                        project(piece, 1 - n)
                    T["psb"].up(len(PIECES))
                pe.wait_ge(s.m8_ready, T["m8"].up())
                pe.matmul(bank(7, 1, at=511), ones[:, :], ones[:, 0:1], start=True, stop=True)
                pe.transpose(bank(7, P, slice(0, 40)), m8[:, :], ident[:, :]).then_inc(s.m8T_ps, 1)
                pe.wait_ge(s.shift_ready, T["shift"].up(2))
                for t in range(KEY_TILES):
                    rows = slice(0, keys_of(t))
                    for a in range(KT):
                        at = bank(2 * (t % 2) + a, 512, rows)
                        pe.matmul(at, onesb[:, rows], shift[:, a * 512:a * 512 + 512], start=True, stop=False)
                        mm = pe.matmul(at, kTv[:, n, a, t * P:t * P + keys_of(t)], qbd[:, n, a, :], start=False, stop=True)
                    mm.then_inc(s.sc_ps, 1)
                    if t >= 1:
                        weigh(n, t - 1)
                weigh(n, KEY_TILES - 1)
                pe.wait_ge(s.sum_done, T["pr"].now())
                for g in range(KT):
                    for j in range(4):
                        mm = pe.matmul(bank(5, P, slice(32 * j, 32 * j + 32), g * P), ones[:, 0:32],
                                       probs_sum[:, (4 * g + j) * P:(4 * g + j) * P + P], start=g == 0, stop=True, skip_group_check=True)
                mm.then_inc(s.den_ps, 1)
                T["sum"].up()

            def pe_pair(last):
                transpose_xn()
                pe.wait_ge(s.xnT_ready, T["xnT"].up())
                for o in range(KT):
                    for k in range(KT):
                        mm = pe.matmul(bank(7, P, at=o * P), w["cq"][:, k, o * P:o * P + P], xnT[:, k, :], start=k == 0, stop=k == KT - 1)
                mm.then_inc(s.qB_ps, 1)
                for n in range(2):
                    pe_batch(n, last)
                T["ctxB"].up(16)
                pe.wait_ge(s.attn_ready, T["attn"].up(2))
                for k in range(KT):
                    mm = pe.matmul(bank(7, D), attn_ch[:, k, :], w["cp"][:, k, :], start=k == 0, stop=k == KT - 1)
                mm.then_inc(s.po_ps, 1)
                transpose_xn()
                pe.wait_ge(s.xnT_ready, T["xnT"].up())
                for n, m in enumerate(("hq", "hk")):
                    for a in range(KT):
                        pe.matmul(bank(7, P, at=(2 * n + a) * P), w[m][:, a, :], xnT[:, a, :], start=True, stop=True)
                for a in range(KT):
                    mm = pe.matmul(bank(5, P, at=a * P), xnT[:, a, :], w["hv"][:, a, :], start=True, stop=True)
                mm.then_inc(s.sqkv_ps, 1)
                pe.wait_ge(s.sqkv_ready, T["sqkv"].up(3))
                pe.wait_ge(s.skbd_ready, T["skbd"].up(2))
                for q in range(QUARTERS):
                    a = q * HPQ // HPT
                    h = q * HPQ % HPT
                    if q:
                        pe.wait_ge(s.cat_ready, T["cat"].up())
                    pe.matmul(bank(6), sqT[:, a, :], skbd[:, a, h:h + HPQ, :].rearrange("p h t -> p (h t)"), start=True, stop=True).then_inc(s.s4_ps, 1)
                    pe.wait_ge(s.p4_ready, T["p4"].up())
                    for k in range(HPQ):
                        mm = pe.transpose(bank(7, P, at=k * P), s4[:, k, :], ident[:, :])
                    mm.then_inc(s.p4T_ps, 1)
                    pe.wait_ge(s.p4T_ready, T["p4T"].up())
                    for k in range(HPQ):
                        mm = pe.matmul(bank(4, HD, at=k * HD), p4T[:, k, :], v4[:, (q * HPQ + k) * HD:(q * HPQ + k + 1) * HD], start=True, stop=True)
                    mm.then_inc(s.o4_ps, 1)
                    T["s4m"].up()
                pe.wait_ge(s.cat_ready, T["cat"].up())
                pe.matmul(bank(7, 1), ones[:, :], ones[:, 0:1], start=True, stop=True)
                catv = cat[:, :].rearrange("p (i r) -> p r i", r=4)
                for r in range(4):
                    for b in range(2):
                        rows = slice(b * S, b * S + S)
                        mm = pe.matmul(bank(5 + b, D, rows), catv[rows, r, :], wo[rows, r, :], start=r == 0, stop=r == 3)
                mm.then_inc(s.wo_ps, 1)
                T["x_done"].up(3)

            pe.wait_ge(s.x_done, XDONE_F)
            count[0] = 0
            pe.wait_ge(s.ctxB0_in, 16)
            for piece in PIECES:
                project(piece, 0)
            T["psb"].up(len(PIECES))
            T["ctxB"].up(16)
            with pe.Fori(0, TILES - 1) as i:
                enter("B", i)
                pe_pair(False)
            leave("B", TILES - 1)
            pe_pair(True)

            with pe.Fori(0, TILES) as i:
                for t in ("xn", "xnT"):
                    T[t].enter("M", i)
                transpose_xn()
                pe.wait_ge(s.xnT_ready, T["xnT"].up())
                for k in range(KT):
                    mm = pe.matmul(bank(2, EXPERTS), xnT[:, k, :], w["router"][:, k, :], start=k == 0, stop=k == KT - 1)
                mm.then_inc(s.logits_ps, 1)
            pe.wait_ge(s.rsum_ready, 1)
            pe.matmul(bank(3, 2 * EXPERTS), ones[:, :], rsmall[:, 40:40 + 2 * EXPERTS], start=True, stop=True).then_inc(s.rsum_ps, 1)
            pe.wait_ge(s.xT_all, TILES)
            pe.wait_ge(s.gates_ready, 1)
            wide = CHUNKS * HT
            with pe.Fori(0, EXPERTS // 2) as i:
                for n in range(2):
                    pe.wait_ge((s.expert0_in, s.expert1_in)[n], i * 16 + 16)
                    gw, uw, dw = (expert_w[n][:, 2048 * m:2048 * m + 2048] for m in range(3))
                    gw, uw = (m.rearrange("p (k h) -> p k h", k=KT) for m in (gw, uw))
                    dw = dw.rearrange("p (j n) -> p j n", j=HT)
                    for c in range(CHUNKS):
                        for j in range(HT):
                            at = (n * CHUNKS + c) * HT + j
                            if at >= 2:
                                pe.wait_ge(s.hM_ready, i * (2 * wide) + at - 1)
                            for k in range(KT):
                                mm = pe.matmul(bank(j % 2), gw[:, k, j * P:j * P + P], xnTall[:, k, c * CHUNK:c * CHUNK + CHUNK],
                                               start=k == 0, stop=k == KT - 1)
                            mm.then_inc(s.g_ps, 1)
                            for k in range(KT):
                                mm = pe.matmul(bank(2 + j % 2), uw[:, k, j * P:j * P + P], xnTall[:, k, c * CHUNK:c * CHUNK + CHUNK],
                                               start=k == 0, stop=k == KT - 1)
                            mm.then_inc(s.u_ps, 1)
                        pe.wait_ge(s.hM_ready, i * (2 * wide) + (n * CHUNKS + c + 1) * HT)
                        for k in range(TPC):
                            tile = (n * CHUNKS + c) * TPC + k
                            if tile >= 2:
                                pe.wait_ge(s.eo_added, i * (2 * CHUNKS * TPC) + tile - 1)
                            for j in range(HT):
                                mm = pe.matmul(bank(4 + k % 2, D), hM[:, j, k * P:k * P + P], dw[:, j, :], start=j == 0, stop=j == HT - 1)
                            mm.then_inc(s.eo_ps, 1)

        @block.vector
        def _(v):
            names = dict(step=dict(A=7, F=56, B=31, M=1),
                         rstd=dict(A=2, F=TPC, B=2, M=1), scores=dict(A=1), pT=dict(A=4), probsA=dict(A=1), av=dict(A=1), outA=dict(A=1),
                         ss=dict(A=1), sp=dict(A=1), so=dict(A=1), x_done=dict(A=2, F=TPC, B=3),
                         xqT=dict(F=TPC), rows=dict(F=2), h_ps=dict(F=HT), mid=dict(F=HT), silu=dict(F=HT), hmaxT=dict(F=1), o=dict(F=TPC),
                         qB=dict(B=1), mx=dict(B=2 * MAX_UNITS), m8T=dict(B=2), pr=dict(B=2 * KEY_TILES), den=dict(B=2),
                         po=dict(B=1), s4=dict(B=QUARTERS), p4=dict(B=QUARTERS), o4=dict(B=QUARTERS), wo=dict(B=1),
                         logits=dict(M=1))
            T = {k: Tally(**q) for k, q in names.items()}

            def enter(phase, i):
                for t in T.values():
                    t.enter(phase, i)

            def leave(phase, n):
                for t in T.values():
                    t.leave(phase, n)

            def own():
                return T["step"].up()

            def layer_norm(xi):
                v.bn_stats(stat[:, :], xi).then_inc(s.vec_step, 1)
                v.wait_ge(s.vec_step, own())
                v.tensor_copy(carrier_v[:, :], eps[:, :])
                v.bn_aggr(mv[:, :], stat[:, :]).then_inc(s.ln_var, 1)
                v.wait_ge(s.ln_rstd, T["rstd"].up())
                return v.tensor_scalar(xn[:, :], xi, mv[:, 0:1], rstd[:, 1:2], ALU.subtract, ALU.mult)

            def diagonals(at):
                for k in range(TPC):
                    ins = v.tensor_scalar(diag[:, k, :], ident[:, :], small[:, at + k:at + k + 1], None, ALU.mult)
                    if k < TPC - 1:
                        ins.then_inc(s.vec_step, 1)
                T["step"].up(TPC - 1)
                ins.then_inc(s.diag_ready, 1)

            def side_taps(j):
                acc = hacc[j % 2].rearrange("p (b t) -> p b t", b=BPC)
                v.wait_ge(s.conv_mid, T["mid"].up())
                v.scalar_tensor_tensor(acc, hpad[j % 3][:, :, 0:S], convw[:, j, 0:1], acc, ALU.mult, ALU.add).then_inc(s.vec_step, 1)
                v.wait_ge(s.vec_step, own())
                v.scalar_tensor_tensor(acc, hpad[j % 3][:, :, 2:S + 2], convw[:, j, 2:3], acc, ALU.mult, ALU.add).then_inc(s.conv_done, 1)

            v.wait_ge(s.weights_in, WEIGHTS_IN)
            for n, r in enumerate((w1_raw, w2_raw)):
                v.tensor_reduce(small[:, n:n + 1], r, AX, ALU.add, apply_absolute_value=True).then_inc(s.vec_step, 1)
            v.wait_ge(s.vec_step, T["step"].up(2))
            v.wait_ge(s.consts_ready, NCONST + 1)
            v.tensor_reduce(parity[:, 0:1], head_of[:, 0::2], AX, ALU.add).then_inc(s.vec_step, 1)
            v.tensor_reduce(parity[:, 1:2], head_of[:, 1::2], AX, ALU.add).then_inc(s.tern_sum, 1)
            T["step"].up()
            v.wait_ge(s.tern_ps, 1)
            v.tensor_scalar(small[:, 80:82], bank(2, 2), 1.0 / (HID * D), 1e-5, ALU.mult, ALU.max).then_inc(s.vec_step, 1)
            v.wait_ge(s.vec_step, own())
            v.reciprocal(small[:, 82:84], small[:, 80:82]).then_inc(s.vec_step, 1)
            v.tensor_scalar(small[:, 84:86], small[:, 80:82], 1 / 127, None, ALU.mult).then_inc(s.vec_step, 1)
            v.wait_ge(s.vec_step, T["step"].up(2))
            for n, (r, q) in enumerate(((w1_raw, w1q), (w2_raw, w2q))):
                v.tensor_scalar(r, r, small[:, 82 + n:83 + n], MAGIC, ALU.mult, ALU.add).then_inc(s.vec_step, 1)
                v.wait_ge(s.vec_step, own())
                v.tensor_scalar(r, r, MAGIC, 1.0, ALU.subtract, ALU.min).then_inc(s.vec_step, 1)
                v.wait_ge(s.vec_step, own())
                v.tensor_scalar(q[:, :, :].rearrange("p a n -> p (a n)"), r, -1.0, None, ALU.max).then_inc(s.vec_step, 1)
                v.wait_ge(s.vec_step, own())

            with v.Fori(0, TILES) as i:
                enter("A", i)
                xi = x[:, bass.ds(i, 1), :].rearrange("p a n -> p (a n)")
                layer_norm(xi).then_inc(s.xn_ready, 1)
                v.wait_ge(s.scores_ps, T["scores"].up())
                v.tensor_reduce(small[:, 0:1], PS[:, 2048:2048 + NK], AX, ALU.max).then_inc(s.vec_step, 1)
                v.wait_ge(s.vec_step, own())
                v.tensor_scalar(small[:, 1:2], small[:, 0:1], -1 / 16, None, ALU.mult).then_inc(s.nmax_ready, 1)
                for q in range(4):
                    v.wait_ge(s.pT_ps, T["pT"].up())
                    if q < 3:
                        v.tensor_copy(probsAT[:, 4 * q:4 * q + 4, :].rearrange("p t q -> p (t q)"), bank(q)).then_inc(s.pT_ready, 1)
                    else:
                        v.tensor_copy(probsAT[0:LAST_KEYS, 12, :], bank(3, P, slice(0, LAST_KEYS))).then_inc(s.pT_ready, 1)
                v.wait_ge(s.probsA_ready, T["probsA"].up())
                v.reciprocal(small[:, 3:4], small[:, 2:3]).then_inc(s.vec_step, 1)
                v.wait_ge(s.vec_step, own())
                v.wait_ge(s.av_ps, T["av"].up())
                v.tensor_scalar(xn[:, :], bank(4, D), small[:, 3:4], None, ALU.mult).then_inc(s.att_ready, 1)
                v.wait_ge(s.outA_ps, T["outA"].up())
                v.tensor_tensor(xi, bank(1, D), xi, ALU.add).then_inc(s.x_done, 1)
                v.wait_ge(s.x_done, T["x_done"].up())
                v.tensor_copy(carrier_v[:, :], eps[:, :])
                layer_norm(xi).then_inc(s.xn_ready, 1)
                v.wait_ge(s.ss_ps, T["ss"].up())
                v.tensor_tensor(s_s, bank(3, P), causal[:, :], ALU.add).then_inc(s.vec_step, 1)
                v.wait_ge(s.vec_step, own())
                v.tensor_reduce(small[:, 4:5], s_s, AX, ALU.max).then_inc(s.vec_step, 1)
                v.wait_ge(s.vec_step, own())
                v.tensor_scalar(small[:, 5:6], small[:, 4:5], -1 / 8, None, ALU.mult).then_inc(s.snmax_ready, 1)
                v.wait_ge(s.sp_ready, T["sp"].up())
                v.reciprocal(small[:, 7:8], small[:, 6:7]).then_inc(s.vec_step, 1)
                v.wait_ge(s.vec_step, own())
                v.wait_ge(s.so_ps, T["so"].up())
                v.scalar_tensor_tensor(xi, bank(5, D), small[:, 7:8], xi, ALU.mult, ALU.add).then_inc(s.x_done, 1)
                T["x_done"].up()
            leave("A", TILES)

            for n in range(3):
                v.memset(hpad[n], 0.0).then_inc(s.vec_step, 1)
            v.wait_ge(s.vec_step, T["step"].up(3))
            with v.Fori(0, CHUNKS) as c:
                enter("F", c)
                for k in range(TPC):
                    xk = x[:, bass.ds(c * TPC + k, 1), :].rearrange("p a n -> p (a n)")
                    layer_norm(xk).then_inc(s.vec_step, 1)
                    v.wait_ge(s.vec_step, own())
                    v.tensor_reduce(small[:, 0:1], xn[:, :], AX, ALU.max, apply_absolute_value=True).then_inc(s.vec_step, 1)
                    v.wait_ge(s.vec_step, own())
                    v.tensor_scalar(small[:, 8 + k:9 + k], small[:, 0:1], 1e-5, None, ALU.max).then_inc(s.vec_step, 1)
                    v.wait_ge(s.vec_step, own())
                    v.reciprocal(small[:, 1:2], small[:, 8 + k:9 + k]).then_inc(s.vec_step, 1)
                    v.wait_ge(s.vec_step, own())
                    v.tensor_scalar(small[:, 2:3], small[:, 1:2], 127.0, None, ALU.mult).then_inc(s.vec_step, 1)
                    v.wait_ge(s.vec_step, own())
                    v.tensor_scalar(xn[:, :], xn[:, :], small[:, 2:3], MAGIC, ALU.mult, ALU.add).then_inc(s.vec_step, 1)
                    v.wait_ge(s.vec_step, own())
                    if k:
                        v.wait_ge(s.xqT_ps, T["xqT"].up())
                    v.tensor_scalar(xq, xn[:, :], MAGIC, None, ALU.subtract).then_inc(s.xq_ready, 1)
                T["xqT"].up()
                v.tensor_scalar(small[:, 12:16], small[:, 8:12], small[:, 84:85], None, ALU.mult).then_inc(s.vec_step, 1)
                v.wait_ge(s.vec_step, own())
                diagonals(12)
                v.wait_ge(s.rows_ready, T["rows"].up())
                for j in range(HT):
                    v.wait_ge(s.h_ps, T["h_ps"].up())
                    v.tensor_tensor(hpad[j % 3][:, :, 1:S + 1], bank(2 + j % 2).rearrange("p (b t) -> p b t", b=BPC),
                                    rowscale.rearrange("p (b t) -> p b t", b=BPC), ALU.mult).then_inc(s.h_scaled, 1)
                    if j >= 1:
                        side_taps(j - 1)
                side_taps(HT - 1)
                v.wait_ge(s.silu_done, T["silu"].up(HT))
                v.tensor_reduce(hmax, hs.rearrange("p j t -> p t j"), AX, ALU.max, apply_absolute_value=True).then_inc(s.hmax_ready, 1)
                v.wait_ge(s.hmaxT_ps, T["hmaxT"].up())
                v.tensor_reduce(small[:, 16:20], bank(4).rearrange("p (k t) -> p k t", k=TPC), AX, ALU.max).then_inc(s.vec_step, 1)
                v.wait_ge(s.vec_step, own())
                v.tensor_scalar(small[:, 20:24], small[:, 16:20], 1e-5, None, ALU.max).then_inc(s.vec_step, 1)
                v.wait_ge(s.vec_step, own())
                v.reciprocal(small[:, 24:28], small[:, 20:24]).then_inc(s.vec_step, 1)
                v.wait_ge(s.vec_step, own())
                v.tensor_scalar(small[:, 28:32], small[:, 24:28], 127.0, None, ALU.mult).then_inc(s.vec_step, 1)
                v.tensor_scalar(small[:, 32:36], small[:, 20:24], small[:, 85:86], None, ALU.mult).then_inc(s.vec_step, 1)
                v.wait_ge(s.vec_step, T["step"].up(2))
                diagonals(28)
                v.wait_ge(s.rows_ready, T["rows"].up())
                for j in range(HT):
                    v.tensor_tensor(hs[:, j, :], hs[:, j, :], rowscale, ALU.mult).then_inc(s.vec_step, 1)
                    v.wait_ge(s.vec_step, own())
                    v.tensor_scalar(hq[:, j, :], hs[:, j, :], MAGIC, MAGIC, ALU.add, ALU.subtract).then_inc(s.hq_ready, 1)
                for k in range(TPC):
                    xk = x[:, bass.ds(c * TPC + k, 1), :].rearrange("p a n -> p (a n)")
                    v.wait_ge(s.o_ps, T["o"].up())
                    v.scalar_tensor_tensor(xk, bank(6 + k % 2, D), small[:, 32 + k:33 + k], xk, ALU.mult, ALU.add).then_inc(s.x_done, 1)
                T["x_done"].up(TPC)
                v.wait_ge(s.x_done, T["x_done"].now())
            leave("F", CHUNKS)

            def maxima(b):
                for u in range(MAX_UNITS):
                    pair, half = divmod(u, 2)
                    width = 1024 if half == 0 else NK - 1024
                    v.wait_ge(s.mx_ps, T["mx"].up())
                    v.tensor_reduce(mpart[:, pair, half:half + 1], PS[:, 1024 * (u % 2):1024 * (u % 2) + width], AX, ALU.max)\
                     .then_inc(s.mx_red, 1)
                v.wait_ge(s.mx_red, T["mx"].now())
                v.tensor_reduce(m8[:, 0:PAIRS], mpart[:, :, :], AX, ALU.max).then_inc(s.vec_step, 1)
                v.wait_ge(s.vec_step, own())
                v.tensor_copy(m8[:, 32:32 + PAIRS], m8[:, 0:PAIRS]).then_inc(s.m8_ready, 1)
                v.wait_ge(s.m8T_ps, T["m8T"].up())
                v.tensor_scalar(sh8[:, 0, :], bank(7, P, slice(0, 40)), -1.0, None, ALU.mult).then_inc(s.vec_step, 1)
                v.wait_ge(s.vec_step, own())
                v.scalar_tensor_tensor(sh8[:, 1, :], bank(7, P, slice(0, 40)), -1.0, sh8[:, 0, :], ALU.mult, ALU.subtract)\
                 .then_inc(s.vec_step, 1)
                v.wait_ge(s.vec_step, own())
                for part, rows in enumerate((slice(0, PAIRS), slice(32, 32 + PAIRS))):
                    v.tensor_tensor(shift[rows, :].rearrange("p (h q) -> p h q", h=PAIRS),
                                    sh8[rows, part, None, :].broadcast_to([PAIRS, PAIRS, P]),
                                    ident[rows, rows, None].broadcast_to([PAIRS, PAIRS, P]), ALU.mult).then_inc(s.shift_ready, 1)

            def vec_pair(xi, last):
                layer_norm(xi).then_inc(s.xn_ready, 1)
                v.wait_ge(s.qB_ready, T["qB"].up())
                for b in range(2):
                    for a in range(KT):
                        v.tensor_tensor(qbd[:, b, a, :].rearrange("p (h q) -> p h q", h=HPT),
                                        qT[:, a, None, b * S:b * S + S].broadcast_to([P, HPT, S]),
                                        head_of[:, :, None].broadcast_to([P, HPT, S]), ALU.mult).then_inc(s.qbd_ready, 1)
                for b in range(2):
                    maxima(b)
                    for t in range(KEY_TILES):
                        rows = slice(0, keys_of(t))
                        v.wait_ge(s.pr_ready, T["pr"].up())
                        if t == 0:
                            v.tensor_copy(probs_sum[:, :], probs[:, 0, :]).then_inc(s.sum_done, 1)
                        else:
                            v.wait_ge(s.sum_done, T["pr"].now(less=1))
                            v.tensor_tensor(probs_sum[rows, :], probs_sum[rows, :], probs[rows, t % PROBS, :], ALU.add).then_inc(s.sum_done, 1)
                    v.wait_ge(s.den_ps, T["den"].up())
                    weighed = weighed_sb[:, 0:256]
                    v.reciprocal(weighed, bank(5, 256)).then_inc(s.vec_step, 1)
                    v.wait_ge(s.vec_step, own())
                    v.tensor_tensor(weighed, bank(4, 256), weighed, ALU.mult).then_inc(s.vec_step, 1)
                    v.wait_ge(s.vec_step, own())
                    wv = weighed.rearrange("p (g h q) -> p g h q", g=KT, h=2)
                    mine = attn_ch[:, :, b * S:b * S + S]
                    v.tensor_scalar(mine, wv[:, :, 0, :], parity[:, 0:1], None, ALU.mult).then_inc(s.vec_step, 1)
                    v.wait_ge(s.vec_step, own())
                    v.scalar_tensor_tensor(mine, wv[:, :, 1, :], parity[:, 1:2], mine, ALU.mult, ALU.add).then_inc(s.attn_ready, 1)
                v.wait_ge(s.po_ps, T["po"].up())
                v.tensor_tensor(xi, bank(7, D), xi, ALU.add).then_inc(s.vec_step, 1)
                v.wait_ge(s.vec_step, own())
                v.tensor_tensor(xi, xi, bias_p[:, :], ALU.add).then_inc(s.x_done, 1)
                v.wait_ge(s.x_done, T["x_done"].up())
                v.tensor_copy(carrier_v[:, :], eps[:, :])
                layer_norm(xi).then_inc(s.xn_ready, 1)
                for q in range(QUARTERS):
                    v.wait_ge(s.s4_ps, T["s4"].up())
                    v.tensor_tensor(s4, bank(6).rearrange("p (h t) -> p h t", h=HPQ),
                                    causal[:, None, :].broadcast_to([P, HPQ, P]), ALU.add).then_inc(s.vec_step, 1)
                    v.wait_ge(s.vec_step, own())
                    v.tensor_reduce(small[:, 40:40 + HPQ], s4, AX, ALU.max).then_inc(s.vec_step, 1)
                    v.wait_ge(s.vec_step, own())
                    v.tensor_tensor(s4, s4, small[:, 40:40 + HPQ, None].broadcast_to([P, HPQ, P]), ALU.subtract).then_inc(s.s4_masked, 1)
                    v.wait_ge(s.p4_ready, T["p4"].up())
                    v.tensor_reduce(small[:, 44:44 + HPQ], s4, AX, ALU.add).then_inc(s.vec_step, 1)
                    v.wait_ge(s.vec_step, own())
                    v.reciprocal(small[:, 48:48 + HPQ], small[:, 44:44 + HPQ]).then_inc(s.vec_step, 1)
                    v.wait_ge(s.vec_step, own())
                    v.wait_ge(s.o4_ps, T["o4"].up())
                    v.tensor_tensor(cat[:, q * HPQ * HD:(q + 1) * HPQ * HD].rearrange("p (h e) -> p h e", h=HPQ),
                                    bank(4, HPQ * HD).rearrange("p (h e) -> p h e", h=HPQ),
                                    small[:, 48:48 + HPQ, None].broadcast_to([P, HPQ, HD]), ALU.mult).then_inc(s.cat_ready, 1)
                v.wait_ge(s.wo_ps, T["wo"].up())
                for b in range(2):
                    rows = slice(b * S, b * S + S)
                    v.tensor_tensor(xi[rows, :], bank(5 + b, D, rows), xi[rows, :], ALU.add).then_inc(s.x_done, 1)
                T["x_done"].up(2)

            with v.Fori(0, TILES - 1) as i:
                enter("B", i)
                vec_pair(x[:, bass.ds(i, 1), :].rearrange("p a n -> p (a n)"), False)
            leave("B", TILES - 1)
            vec_pair(x[:, TILES - 1, :], True)
            v.wait_ge(s.x_done, XDONE_B)

            for k in ("rstd", "logits", "step"):
                T[k].rate = 0
            with v.Fori(0, TILES) as i:
                enter("M", i)
                layer_norm(x[:, bass.ds(i, 1), :].rearrange("p a n -> p (a n)")).then_inc(s.xn_ready, 1)
                v.wait_ge(s.logits_ps, T["logits"].up())
                v.tensor_copy(logits[:, bass.ds(i, 1), :].rearrange("p a e -> p (a e)"), bank(2, EXPERTS)).then_inc(s.logits_sb, 1)
            leave("M", TILES)
            v.wait_ge(s.logits_sb, TILES)

            def rows16(at):
                return small[:, at:at + TILES]

            def wide(a):
                return a[:, :, None].broadcast_to([P, TILES, EXPERTS])

            ranks = rank[:, None, :].broadcast_to([P, TILES, EXPERTS])
            v.tensor_reduce(rows16(0), logits, AX, ALU.max).then_inc(s.vec_step, 1)
            v.wait_ge(s.vec_step, own())
            v.tensor_tensor(logits, logits, wide(rows16(0)), ALU.subtract).then_inc(s.rexp_in, 1)
            v.wait_ge(s.rexp_out, 1)

            def first_of_largest(p, largest, hot):
                v.tensor_reduce(largest, p, AX, ALU.max).then_inc(s.vec_step, 1)
                v.wait_ge(s.vec_step, own())
                v.tensor_tensor(rc, p, wide(largest), ALU.is_equal).then_inc(s.vec_step, 1)
                v.wait_ge(s.vec_step, own())
                v.tensor_tensor(rc, rc, ranks, ALU.mult).then_inc(s.vec_step, 1)
                v.wait_ge(s.vec_step, own())
                v.tensor_reduce(rows16(32), rc, AX, ALU.max).then_inc(s.vec_step, 1)
                v.wait_ge(s.vec_step, own())
                v.tensor_tensor(hot, rc, wide(rows16(32)), ALU.is_equal).then_inc(s.vec_step, 1)
                v.wait_ge(s.vec_step, own())

            first_of_largest(rp, rows16(0), ro1)
            v.scalar_tensor_tensor(rp, ro1, -4.0, rp, ALU.mult, ALU.add).then_inc(s.vec_step, 1)
            v.wait_ge(s.vec_step, own())
            first_of_largest(rp, rows16(16), ro2)
            v.tensor_tensor(rows16(32), rows16(0), rows16(16), ALU.add).then_inc(s.vec_step, 1)
            v.wait_ge(s.vec_step, own())
            v.reciprocal(rows16(48), rows16(32)).then_inc(s.vec_step, 1)
            v.wait_ge(s.vec_step, own())
            v.tensor_tensor(rc, ro1, wide(rows16(0)), ALU.mult).then_inc(s.vec_step, 1)
            v.tensor_tensor(rp, ro2, wide(rows16(16)), ALU.mult).then_inc(s.vec_step, 1)
            v.tensor_tensor(ro1, ro1, ro2, ALU.add).then_inc(s.vec_step, 1)
            v.wait_ge(s.vec_step, T["step"].up(3))
            v.tensor_tensor(rc, rc, rp, ALU.add).then_inc(s.vec_step, 1)
            v.wait_ge(s.vec_step, own())
            v.tensor_tensor(rc, rc, wide(rows16(48)), ALU.mult).then_inc(s.vec_step, 1)
            v.wait_ge(s.vec_step, own())
            v.tensor_reduce(rsmall[:, 0:EXPERTS], rc.rearrange("p t e -> p e t"), AX, ALU.add).then_inc(s.vec_step, 1)
            v.tensor_reduce(rsmall[:, EXPERTS:2 * EXPERTS], ro1.rearrange("p t e -> p e t"), AX, ALU.add).then_inc(s.vec_step, 1)
            v.wait_ge(s.vec_step, T["step"].up(2))
            v.tensor_copy(rsmall[:, 40:56], rsmall[:, 0:16]).then_inc(s.rsum_ready, 1)
            v.wait_ge(s.rsum_ps, 1)
            v.tensor_scalar(rsmall[:, 16:24], bank(3, EXPERTS, at=EXPERTS), 1.0, None, ALU.max).then_inc(s.vec_step, 1)
            v.wait_ge(s.vec_step, own())
            v.reciprocal(rsmall[:, 24:32], rsmall[:, 16:24]).then_inc(s.vec_step, 1)
            v.wait_ge(s.vec_step, own())
            v.tensor_tensor(rsmall[:, 32:40], bank(3, EXPERTS), rsmall[:, 24:32], ALU.mult).then_inc(s.vec_step, 1)
            v.wait_ge(s.vec_step, own())
            v.tensor_tensor(gates[:, :, :], ro1, rsmall[:, None, 32:40].broadcast_to([P, TILES, EXPERTS]), ALU.mult).then_inc(s.gates_ready, 1)
            v.wait_ge(s.gates_ready, 1)

            wide_n = CHUNKS * HT
            with v.Fori(0, EXPERTS // 2) as i:
                for n in range(2):
                    for c in range(CHUNKS):
                        for j in range(HT):
                            at = (n * CHUNKS + c) * HT + j
                            if j == 0 and at:
                                v.wait_ge(s.eo_ps, i * (2 * CHUNKS * TPC) + (n * CHUNKS + c) * TPC)
                            v.wait_ge(s.silu_g_ready, i * (2 * wide_n) + at + 1)
                            v.wait_ge(s.u_ps, i * (2 * wide_n) + at + 1)
                            v.tensor_tensor(hM[:, j, :], bank(2 + j % 2), silu_g[j % 2], ALU.mult).then_inc(s.hM_ready, 1)
                        for k in range(TPC):
                            tile = (n * CHUNKS + c) * TPC + k
                            v.wait_ge(s.eo_ps, i * (2 * CHUNKS * TPC) + tile + 1)
                            xk = x[:, c * TPC + k, :]
                            v.scalar_tensor_tensor(xk, bank(4 + k % 2, D), gates[:, c * TPC + k, bass.ds(2 * i + n, 1)], xk,
                                                   ALU.mult, ALU.add).then_inc(s.eo_added, 1)


def kernel(**inputs):
    import numpy as np
    import concourse.bacc as bacc
    from concourse import mybir as mb
    from concourse.bass_utils import run_bass_kernel_spmd

    a = {k: np.asarray(v) for k, v in inputs.items()}

    def rows(m):
        return np.ascontiguousarray(m.reshape(-1, P, m.shape[-1]).transpose(1, 0, 2))

    def by_head(m):
        out = np.zeros((P, KT, P), m.dtype)
        for h in range(HEADS):
            r = (h % HPT) * HD
            out[r:r + HD, h // HPT, r:r + HD] = m[h]
        return out

    ctx = a["ctx_1024"]
    ctxT = np.zeros((B, P, KT, NKP), ctx.dtype)
    ctxT[:, :, :, :NK] = ctx.transpose(0, 2, 1).reshape(B, KT, P, NK).transpose(0, 2, 1, 3)
    ctxN = np.zeros((B, KEY_TILES * P, D), ctx.dtype)
    ctxN[:, :NK] = ctx
    ctxN = ctxN.reshape(B, KEY_TILES, P, D).transpose(0, 2, 1, 3)
    wkv = a["L1_xattn_W_kv"]
    ffn = [rows(a["L1_ffn_gate_w"][e].T).reshape(P, -1) for e in range(EXPERTS)], \
          [rows(a["L1_ffn_up_w"][e].T).reshape(P, -1) for e in range(EXPERTS)], \
          [rows(a["L1_ffn_down_w"][e].T).reshape(P, -1) for e in range(EXPERTS)]
    wo = a["L1_attn_W_O"].reshape(4, 64, D).transpose(1, 0, 2)
    arrays = {
        "x": a["x"].reshape(TILES, P, D).transpose(1, 0, 2),
        "ctxT": ctxT.reshape(B, P, KT * NKP),
        "ctxN": ctxN.reshape(B, P, KEY_TILES * D),
        "w_xqT": rows(a["L0_xattn_Wq"].T), "w_xkT": rows(a["L0_xattn_Wk"].T), "w_xv": rows(a["L0_xattn_Wv"]),
        "w_sq": rows(a["L0_attn_Wq"]), "w_sk": rows(a["L0_attn_Wk"]), "w_sv": rows(a["L0_attn_Wv"]),
        "w1T": rows(a["L0_ffn_w1"].T).reshape(P, -1), "w2T": rows(a["L0_ffn_w2"].T).reshape(P, -1),
        "conv_w": rows(a["L0_ffn_conv_w"].reshape(HID, 3)), "conv_b": a["L0_ffn_conv_b"].reshape(HT, P).T,
        "w_ck": rows(wkv[:, :D]), "w_cv": rows(wkv[:, D:]), "w_cq": rows(a["L1_xattn_W_q"]), "w_cp": rows(a["L1_xattn_W_proj"]),
        "b_p": np.broadcast_to(a["L1_xattn_b_proj"], (P, D)),
        "w_hq": by_head(a["L1_attn_Wq"]), "w_hk": by_head(a["L1_attn_Wk"]), "w_hv": by_head(a["L1_attn_Wv"]),
        "w_o": np.concatenate([wo, wo]),
        "w_router": rows(a["L1_ffn_router_w"].T),
        "experts": np.stack([np.concatenate(three, axis=1) for three in zip(*ffn)]),
    }
    nc = bacc.Bacc("TRN2", target_bir_lowering=False, num_devices=1)
    fed, io = {}, {}
    for name, m in arrays.items():
        fed[f"in_{name}"] = np.ascontiguousarray(m)
        io[name] = nc.dram_tensor(f"in_{name}", m.shape, mb.dt.from_np(m.dtype), kind="ExternalInput").ap()
    out = nc.dram_tensor("out", (P, TILES, D), F32, kind="ExternalOutput").ap()
    build(nc, io, out)
    got = run_bass_kernel_spmd(nc, [fed], core_ids=[0]).results[0]["out"]
    return np.ascontiguousarray(got.transpose(1, 0, 2)).reshape(B, S, D)
```

```python
from contextlib import ExitStack

import concourse.bass as bass
from concourse import mybir

ALU = mybir.AluOpType
ACT = mybir.ActivationFunctionType
F32 = mybir.dt.float32
F32R = mybir.dt.float32r
BF16 = mybir.dt.bfloat16
AX = mybir.AxisListType.X

P = 128
B, S, D = 32, 64, 256
NK = 1601
NKP = NK + 1
TILES = B * S // P
KT = D // P
KEY_TILES = -(-NK // P)
LAST_KEYS = NK - (KEY_TILES - 1) * P
HEADS, HD = 16, 16
PAIRS = HEADS // 2
HPT = P // HD
HID = 1024
HT = HID // P
EXPERTS = 8
CHUNK = 512
CHUNKS = B * S // CHUNK
TPC = CHUNK // P
BPC = CHUNK // S
EPS = 1e-5
MASKED = -1e30
MAGIC = 12582912.0
KEY_CHUNKS = [(c, min(512, NK - c)) for c in range(0, NK, 512)]
KEY_CHUNKS_EVEN = [(c, min(512, NKP - c)) for c in range(0, NKP, 512)]
MAX_UNITS = 2 * PAIRS
K_PIECES = [("k", o, c) for o in range(KT) for c in range(len(KEY_CHUNKS_EVEN))]
V_PIECES = [("v", t, min(t + 2, KEY_TILES)) for t in range(0, KEY_TILES, 2)]
PIECES = K_PIECES + V_PIECES
PIECE_AFTER = (0, 2, 4, 6, 8, 10, 12, 14, 15)
PROBS = 3
QUARTERS = 4
HPQ = HEADS // QUARTERS

WEIGHTS = dict(sq=64, sk=64, sv=D, ck=D, cv=D, cq=D, cp=D, hq=P, hk=P, hv=P, router=EXPERTS)


def keys_of(t):
    return P if t < KEY_TILES - 1 else LAST_KEYS


class Tally:

    def __init__(self, **per):
        self.base, self.done, self.trip, self.per = 0, 0, None, per
        self.rate = 0

    def up(self, n=1):
        self.done += n
        return self.now()

    def now(self, less=0):
        fixed = self.base + self.done - less
        return fixed if self.trip is None else self.trip * self.rate + fixed

    def enter(self, phase, trip, first=0):
        self.rate = self.per.get(phase, 0)
        self.base, self.done, self.trip = self.base + self.done - first * self.rate, 0, trip

    def leave(self, phase, trips, first=0):
        assert self.done == self.rate, (phase, self.done, self.rate)
        self.base, self.done, self.trip = self.base + (first + trips) * self.rate, 0, None


def build(nc, io, out):
    ctx = ExitStack()
    with ctx:
        def sb(name, shape, dt=F32):
            return ctx.enter_context(nc.sbuf_tensor(name, shape, dt))

        def sem(name):
            return ctx.enter_context(nc.semaphore(name))

        x = sb("x", [P, TILES, D])
        ctxT = sb("ctxT", [P, 2, KT * NKP])
        ctxN = sb("ctxN", [P, 2, KEY_TILES, D])
        kT = sb("kT", [P, 2, KT * NKP])
        kTr = sb("kTr", [P, KT, NKP], F32R)
        probs = sb("probs", [P, PROBS, HEADS * S])
        probs_sum = sb("probs_sum", [P, HEADS * S])
        qbd = sb("qbd", [P, 2, KT, HPT * S])
        qbdr = sb("qbdr", [P, 2, KT, HPT * S], F32R)
        shift = sb("shift", [P, HEADS * S], BF16)
        ident = sb("ident", [P, P])
        identb = sb("identb", [P, P], BF16)
        ones = sb("ones", [P, P])
        onesb = sb("onesb", [P, P], BF16)
        head_of = sb("head_of", [P, HPT])
        parity = sb("parity", [P, 2])
        causal = sb("causal", [P, P])
        neghalf = sb("neghalf", [P, 1])
        eps = sb("eps", [P, 1])
        carrier_g = sb("carrier_g", [P, HT])
        carrier_v = sb("carrier_v", [P, 1])
        rank = sb("rank", [P, EXPERTS])
        xn = sb("xn", [P, D])
        xnT = sb("xnT", [P, KT, P])
        big = sb("big", [P, 4096])
        w = {n: sb("w_" + n, [P, KT, width]) for n, width in WEIGHTS.items()}
        fold = sb("fold", [P, KT, D])
        vout = sb("vout", [P, KT, D])
        wo = sb("wo", [P, 4, D])
        bias_p = sb("bias_p", [P, D])
        convw = sb("convw", [P, HT, 3])
        convb = sb("convb", [P, HT])
        w1q = sb("w1q", [P, KT, HID], BF16)
        w2q = sb("w2q", [P, HT, D], BF16)
        stat = sb("stat", [P, 6])
        mv = sb("mv", [P, 2])
        rstd = sb("rstd", [P, 2])
        small = sb("small", [P, 96])
        mpart = sb("mpart", [P, PAIRS, 2])
        m8 = sb("m8", [P, 40])
        sh8 = sb("sh8", [40, 2, P], BF16)
        attn_ch = sb("attn_ch", [P, KT, P])
        PS = ctx.enter_context(nc.psum_tensor("PS", [P, 8 * 512], F32))

        def bank(n, width=512, rows=slice(0, P), at=0):
            return PS[rows, 512 * n + at:512 * n + at + width]

        ctxTv = ctxT[:, :, :].rearrange("p b (k n) -> p b k n", k=KT)
        kTv = kT[:, :, :].rearrange("p b (k n) -> p b k n", k=KT)
        ctxNf = ctxN[:, :, :, :].rearrange("p b t n -> p (b t n)")
        probsA = big[:, 0:NK]
        probsAT = big[:, 1664:1664 + KEY_TILES * P].rearrange("p (t q) -> p t q", q=P)
        qkT = big[:, 3328:3584].rearrange("p (k t) -> p k t", k=KT)
        qk_s = kT[0:64, 0, 0:256]
        v_s = kT[:, 0, 256:512]
        s_s = kT[:, 0, 512:640]
        p_s = kT[:, 0, 640:768]
        pT_s = kT[:, 0, 768:896]
        hs = ctxNf[:, 0:HT * CHUNK].rearrange("p (j t) -> p j t", j=HT)
        hq = qbd[:, :, :, :].rearrange("p b k n -> p (b k n)").bitcast(BF16).rearrange("p (j t) -> p j t", j=HT)
        xq = big[:, 0:128].bitcast(BF16)
        xqT = big[:, 128:640].bitcast(BF16).rearrange("p (k t) -> p k t", k=KT)
        diag = big[:, 640:1152].rearrange("p (k t) -> p k t", k=TPC)
        rowscale = big[:, 1152:1664]
        hpad = [kT[:, 0, 600 * n:600 * n + BPC * (S + 2)].rearrange("p (b t) -> p b t", b=BPC) for n in range(3)]
        hacc = [kT[:, 1, 512 * n:512 * n + 512] for n in range(2)]
        hmax = big[:, 1664:2176]
        qT = big[:, 0:256].rearrange("p (k t) -> p k t", k=KT)
        sqT = big[:, 256:512].rearrange("p (k t) -> p k t", k=KT)
        skT = big[:, 512:768].rearrange("p (k t) -> p k t", k=KT)
        s4 = [big[:, 768 + 512 * n:1280 + 512 * n].rearrange("p (h t) -> p h t", h=HPQ) for n in range(2)]
        skbd = [big[:, 1792 + 512 * n:2304 + 512 * n].rearrange("p (h t) -> p h t", h=HPQ) for n in range(2)]
        v4 = big[:, 2816:3072]
        p4T = big[:, 3072:3584].rearrange("p (h t) -> p h t", h=HPQ)
        s4_max = small[:, 40:44]
        s4_nmax = [small[:, 44 + 4 * n:48 + 4 * n] for n in range(2)]
        s4_sum = [small[:, 52 + 4 * n:56 + 4 * n] for n in range(2)]
        s4_inv = [small[:, 60 + 4 * n:64 + 4 * n] for n in range(2)]
        cat = sb("cat", [P, D])
        gates = sb("gates", [P, TILES, EXPERTS])
        weighed_sb = sb("weighed", [P, D])
        xnTall = big[:, :].rearrange("p (k t) -> p k t", k=KT)
        hM = ctxNf[:, 0:HT * CHUNK].rearrange("p (j t) -> p j t", j=HT)
        expert_w = [t[:, :, :].rearrange("p b n -> p (b n)")[:, 0:6144] for t in (ctxT, kT)]
        silu_g = [probs[:, n, 0:512] for n in range(2)]
        rt = probs_sum[:, :]
        logits, rp, ro1, ro2, rc = (rt[:, 128 * n:128 * n + 128].rearrange("p (t e) -> p t e", e=EXPERTS) for n in range(5))
        rsmall = qbd[:, 0, 0, :]

        S_ = {n: sem(n) for n in """
            weights_in consts_ready ctxT_in ctxN_in ctxB0_in ctxB1_in expert0_in expert1_in out_stored
            vec_step pool_step act_step ln_var ln_rstd xn_ready xn_ps xnT_ready
            fold_ps fold_ready tern_sum tern_ps
            qk_ps qk_ready scores_ps nmax_ready probsA_ready pT_ps pT_ready av_ps att_ready attT_ps attT_ready outA_ps x_done
            qkv_ps qkv_ready ss_ps snmax_ready sp_ready spT_ps spT_ready so_ps
            xq_ready xqT_ps xqT_ready diag_ready rows_ps rows_ready h_ps h_scaled conv_mid conv_done silu_done
            hmax_ready hmaxT_ps hq_ready o_ps
            proj_ps proj_sb kTr_ready mx_ps mx_red m8_ready m8T_ps shift_ready
            qB_ps qB_ready qbd_ready qbdr_ready sc_ps pr_ready pv_done sum_done den_ps attn_ready
            po_ps sqkv_ps sqkv_ready skbd_ready s4_ps s4_masked p4_ready p4T_ps p4T_ready o4_ps cat_ready wo_ps
            xT_all logits_ps logits_sb gates_ready rexp_in rexp_out rsum_ready rsum_ps g_ps u_ps silu_g_ready hM_ready eo_ps eo_added
            """.split()}
        s = type("Sems", (), S_)

        block = ctx.enter_context(nc.Block())
        NCONST = 22

        raw = ctxNf
        wqT_raw, wkT_raw, wv_raw = (raw[:, 512 * n:512 * n + 512].rearrange("p (k n) -> p k n", k=KT) for n in range(3))
        w1_raw = kT[:, 0, 0:KT * HID]
        w2_raw = kT[:, 1, 0:HT * D]
        loads = [(w[n][:, :, :], io["w_" + n]) for n in WEIGHTS] + [
            (wqT_raw, io["w_xqT"]), (wkT_raw, io["w_xkT"]), (wv_raw, io["w_xv"]),
            (w1_raw, io["w1T"]), (w2_raw, io["w2T"]), (wo[:, :, :], io["w_o"]),
            (bias_p[:, :], io["b_p"]), (convw[:, :, :], io["conv_w"]), (convb[:, :], io["conv_b"]),
            (x[:, :, :], io["x"])]
        WEIGHTS_IN = 16 * len(loads)
        XDONE_A = 2 * TILES
        XDONE_F = XDONE_A + TILES
        XDONE_B = XDONE_F + 3 * TILES
        XNT_READY_B = 4 * TILES

        @block.sync
        def _(sp):
            for dst, src in loads:
                sp.dma_start(dst, src).then_inc(s.weights_in, 16)

            def pair_of(src, i):
                return src[bass.ds(2 * i, 2), :, :].rearrange("b p n -> p b n")

            sp.dma_start(ctxT[:, :, :], pair_of(io["ctxT"], 0)).then_inc(s.ctxT_in, 16)
            sp.wait_ge(s.fold_ps, 2)
            nkeys = ctxN[:, :, :, :].rearrange("p b t n -> p b (t n)")
            sp.dma_start(nkeys, pair_of(io["ctxN"], 0)).then_inc(s.ctxN_in, 16)
            with sp.Fori(1, TILES) as i:
                sp.wait_ge(s.scores_ps, i)
                sp.dma_start(ctxT[:, :, :], pair_of(io["ctxT"], i)).then_inc(s.ctxT_in, 16)
                sp.wait_ge(s.av_ps, i)
                sp.dma_start(nkeys, pair_of(io["ctxN"], i)).then_inc(s.ctxN_in, 16)
            sp.wait_ge(s.scores_ps, TILES)
            for n in range(2):
                sp.dma_start(ctxT[:, n, :], io["ctxT"][n, :, :]).then_inc((s.ctxB0_in, s.ctxB1_in)[n], 16)
            with sp.Fori(1, TILES) as i:
                for n in range(2):
                    sp.wait_ge(s.proj_ps, i * (2 * len(PIECES)) + (n - 1) * len(PIECES))
                    sp.dma_start(ctxT[:, n, :], io["ctxT"][bass.ds(2 * i + n, 1), :, :].rearrange("b p n -> (b p) n"))\
                      .then_inc((s.ctxB0_in, s.ctxB1_in)[n], 16)
            sp.wait_ge(s.proj_ps, B * len(PIECES))
            sp.dma_start(expert_w[0], io["experts"][0, :, :]).then_inc(s.expert0_in, 16)
            sp.wait_ge(s.x_done, XDONE_B)
            sp.dma_start(expert_w[1], io["experts"][1, :, :]).then_inc(s.expert1_in, 16)
            with sp.Fori(1, EXPERTS // 2) as i:
                for n in range(2):
                    sp.wait_ge(s.eo_ps, i * (2 * CHUNKS * TPC) + (n - 1) * CHUNKS * TPC)
                    sp.dma_start(expert_w[n], io["experts"][bass.ds(2 * i + n, 1), :, :].rearrange("e p n -> (e p) n"))\
                      .then_inc((s.expert0_in, s.expert1_in)[n], 16)
            sp.wait_ge(s.eo_added, EXPERTS * CHUNKS * TPC)
            sp.dma_start(out, x[:, :, :]).then_inc(s.out_stored, 16)
            sp.wait_ge(s.out_stored, 16)

        @block.gpsimd
        def _(g):
            step = Tally(A=2 * 1, F=TPC * 1, B=2, M=1)
            var = Tally(A=2, F=TPC, B=2, M=1)

            g.memset(ident[:, :], 0.0).then_inc(s.consts_ready, 1)
            g.memset(ones[:, :], 1.0).then_inc(s.consts_ready, 1)
            g.memset(onesb[:, :], 1.0).then_inc(s.consts_ready, 1)
            g.memset(head_of[:, :], 1.0).then_inc(s.consts_ready, 1)
            g.memset(causal[:, :], 0.0).then_inc(s.consts_ready, 1)
            g.memset(neghalf[:, :], -0.5).then_inc(s.consts_ready, 1)
            g.memset(eps[:, :], EPS).then_inc(s.consts_ready, 1)
            g.memset(shift[:, :], 0.0).then_inc(s.consts_ready, 1)
            g.memset(m8[:, :], 0.0).then_inc(s.consts_ready, 1)
            for e in range(EXPERTS):
                g.memset(rank[:, e:e + 1], float(EXPERTS - e)).then_inc(s.consts_ready, 1)
            g.wait_ge(s.consts_ready, 17)
            g.affine_select(out=ident[:, :], in_=ident[:, :], compare_op=ALU.not_equal, fill=1.0, base=0,
                            pattern=[[-1, P]], channel_multiplier=1).then_inc(s.consts_ready, 1)
            g.affine_select(out=head_of[:, :], in_=head_of[:, :], compare_op=ALU.is_ge, fill=0.0, base=0,
                            pattern=[[-HD, HPT]], channel_multiplier=1).then_inc(s.consts_ready, 1)
            g.affine_select(out=causal[:, :], in_=causal[:, :], compare_op=ALU.is_ge, fill=MASKED, base=0,
                            pattern=[[-1, P]], channel_multiplier=1).then_inc(s.consts_ready, 1)
            g.wait_ge(s.consts_ready, 20)
            g.affine_select(out=head_of[:, :], in_=head_of[:, :], compare_op=ALU.is_ge, fill=0.0, base=HD - 1,
                            pattern=[[HD, HPT]], channel_multiplier=-1).then_inc(s.consts_ready, 1)
            g.wait_ge(s.consts_ready, 21)
            g.memset(causal[S:P, 0:S], MASKED).then_inc(s.consts_ready, 1)

            def rsqrt():
                g.wait_ge(s.ln_var, var.up())
                g.tensor_tensor(rstd[:, 0:1], mv[:, 1:2], eps[:, :], ALU.add).then_inc(s.pool_step, 1)
                g.wait_ge(s.pool_step, step.up())
                g.tensor_tensor(rstd[:, 1:2], rstd[:, 0:1], neghalf[:, :], ALU.pow).then_inc(s.ln_rstd, 1)

            def enter(phase, i, first=0):
                for t in (step, var):
                    t.enter(phase, i, first)

            def leave(phase, n, first=0):
                for t in (step, var):
                    t.leave(phase, n, first)

            with g.Fori(0, TILES) as i:
                enter("A", i)
                rsqrt()
                rsqrt()
            leave("A", TILES)
            hsc = Tally(F=HT)
            with g.Fori(0, CHUNKS) as c:
                enter("F", c)
                hsc.enter("F", c)
                for k in range(TPC):
                    rsqrt()
                for j in range(HT):
                    if j >= 2:
                        g.wait_ge(s.silu_done, c * HT + j - 1)
                    g.wait_ge(s.h_scaled, hsc.up())
                    g.tensor_tensor(carrier_g[:, j:j + 1], eps[:, :], eps[:, :], ALU.add)
                    g.tensor_scalar(hacc[j % 2].rearrange("p (b t) -> p b t", b=BPC), hpad[j % 3][:, :, 1:S + 1],
                                    convw[:, j, 1:2], convb[:, j:j + 1], ALU.mult, ALU.add).then_inc(s.conv_mid, 1)
            leave("F", CHUNKS)
            psb = Tally(B=2 * len(PIECES))
            mxp = Tally(B=2 * MAX_UNITS)
            qb = Tally(B=1)
            sqk = Tally(B=3)
            s4p = Tally(B=QUARTERS)
            scp = Tally(B=2 * KEY_TILES)
            bt = (psb, mxp, qb, sqk, s4p, scp)

            def round_keys(n):
                g.wait_ge(s.proj_sb, psb.up(len(PIECES)))
                g.tensor_tensor(carrier_g[:, 0:1], eps[:, :], eps[:, :], ALU.add)
                g.tensor_copy(kTr[:, :, :], kTv[:, n, :, :]).then_inc(s.kTr_ready, 1)

            def spread_queries(b):
                for to, done in ((qbdr, s.qbdr_ready), (qbd, s.qbd_ready)):
                    g.tensor_tensor(to[:, b, :, :].rearrange("p a (h q) -> p a h q", h=HPT),
                                    qT[:, :, None, b * S:b * S + S].broadcast_to([P, KT, HPT, S]),
                                    head_of[:, None, :, None].broadcast_to([P, KT, HPT, S]), ALU.mult).then_inc(done, 1)

            def finish():
                rsqrt()
                g.wait_ge(s.sqkv_ready, sqk.up(3))
                for q in range(QUARTERS):
                    a, h = divmod(q * HPQ, HPT)
                    if q >= 2:
                        g.wait_ge(s.s4_ps, s4p.up())
                    g.tensor_tensor(skbd[q % 2], skT[:, a, None, :].broadcast_to([P, HPQ, P]),
                                    head_of[:, h:h + HPQ, None].broadcast_to([P, HPQ, P]), ALU.mult).then_inc(s.skbd_ready, 1)
                s4p.up(2)

            def pool_pair(first, last):
                if not first:
                    g.wait_ge(s.sc_ps, scp.now())
                spread_queries(1)
                if not first:
                    finish()
                g.wait_ge(s.mx_ps, mxp.up(MAX_UNITS))
                round_keys(1)
                if not last:
                    g.wait_ge(s.mx_ps, mxp.up(MAX_UNITS))
                    round_keys(0)
                    rsqrt()
                    g.wait_ge(s.qB_ready, qb.up())
                    g.wait_ge(s.sc_ps, scp.now() + KEY_TILES)
                    spread_queries(0)
                scp.up(2 * KEY_TILES)

            rsqrt()
            g.wait_ge(s.qB_ready, qb.up())
            spread_queries(0)
            round_keys(0)
            pool_pair(True, False)
            with g.Fori(1, TILES - 1) as i:
                enter("B", i, 1)
                for t in bt:
                    t.enter("B", i, 1)
                pool_pair(False, False)
            leave("B", TILES - 2, 1)
            for t in bt:
                t.leave("B", TILES - 2, 1)
            pool_pair(False, True)
            finish()
            xt = Tally(M=1)
            with g.Fori(0, TILES) as i:
                enter("M", i)
                xt.enter("M", i)
                rsqrt()
                g.wait_ge(s.xnT_ready, XNT_READY_B + xt.up())
                g.tensor_copy(xnTall[:, :, bass.ds(i * P, P)], xnT[:, :, :]).then_inc(s.xT_all, 1)

        @block.scalar
        def _(act):
            names = dict(xn_ps=dict(A=2, B=2, M=1), qk_ps=dict(A=1), nmax=dict(A=1), attT=dict(A=1), qkv=dict(A=1),
                         snmax=dict(A=1), spT=dict(A=1),
                         xqT=dict(F=TPC), rows=dict(F=2), conv=dict(F=HT),
                         proj=dict(B=2 * len(PIECES)), sc=dict(B=2 * KEY_TILES), pv=dict(B=2 * KEY_TILES),
                         qB=dict(B=1), sqkv=dict(B=1), s4=dict(B=QUARTERS), p4T=dict(B=QUARTERS), qbd=dict(B=2))
            T = {k: Tally(**v) for k, v in names.items()}

            def enter(phase, i, first=0):
                for t in T.values():
                    t.enter(phase, i, first)

            def leave(phase, n, first=0):
                for t in T.values():
                    t.leave(phase, n, first)

            def copy_xnT(at=0):
                act.wait_ge(s.xn_ps, T["xn_ps"].up())
                act.copy(xnT[:, :, :].rearrange("p k t -> p (k t)"), bank(at, 256)).then_inc(s.xnT_ready, 1)

            act.wait_ge(s.consts_ready, NCONST)
            act.copy(identb[:, :], ident[:, :]).then_inc(s.consts_ready, 1)
            act.wait_ge(s.fold_ps, 1)
            act.copy(fold[:, :, :].rearrange("p k n -> p (k n)"), bank(0)).then_inc(s.fold_ready, 1)
            act.wait_ge(s.fold_ps, 2)
            act.copy(vout[:, :, :].rearrange("p k n -> p (k n)"), bank(1)).then_inc(s.fold_ready, 1)

            with act.Fori(0, TILES) as i:
                enter("A", i)
                copy_xnT()
                act.wait_ge(s.qk_ps, T["qk_ps"].up())
                act.copy(qkT.rearrange("p k t -> p (k t)"), bank(1, 256)).then_inc(s.qk_ready, 1)
                act.wait_ge(s.nmax_ready, T["nmax"].up())
                act.activation(probsA, PS[:, 2048:2048 + NK], ACT.Exp, bias=small[:, 1:2], scale=1 / 16,
                               accum_out=small[:, 2:3]).then_inc(s.probsA_ready, 1)
                act.wait_ge(s.attT_ps, T["attT"].up())
                act.copy(xnT[:, :, :].rearrange("p k t -> p (k t)"), bank(0, 256)).then_inc(s.attT_ready, 1)
                copy_xnT()
                act.wait_ge(s.qkv_ps, T["qkv"].up())
                act.copy(qk_s, bank(1, 256, slice(0, 64))).then_inc(s.qkv_ready, 1)
                act.copy(v_s, bank(2, 256)).then_inc(s.qkv_ready, 1)
                act.wait_ge(s.snmax_ready, T["snmax"].up())
                act.activation(p_s, s_s, ACT.Exp, bias=small[:, 5:6], scale=1 / 8,
                               accum_out=small[:, 6:7]).then_inc(s.sp_ready, 1)
                act.wait_ge(s.spT_ps, T["spT"].up())
                act.copy(pT_s, bank(4, P)).then_inc(s.spT_ready, 1)
            leave("A", TILES)

            with act.Fori(0, CHUNKS) as c:
                enter("F", c)
                for k in range(TPC):
                    act.wait_ge(s.xqT_ps, T["xqT"].up())
                    act.copy(xqT[:, :, k * P:k * P + P], bank(0, P).bitcast(BF16).rearrange("p (k t) -> p k t", k=KT))\
                       .then_inc(s.xqT_ready, 1)
                act.wait_ge(s.rows_ps, T["rows"].up())
                act.copy(rowscale, bank(1)).then_inc(s.rows_ready, 1)
                for j in range(HT):
                    act.wait_ge(s.conv_done, T["conv"].up())
                    act.activation(hs[:, j, :], hacc[j % 2], ACT.Silu).then_inc(s.silu_done, 1)
                act.wait_ge(s.rows_ps, T["rows"].up())
                act.copy(rowscale, bank(5)).then_inc(s.rows_ready, 1)
            leave("F", CHUNKS)

            def evac(piece, n):
                act.wait_ge(s.proj_ps, T["proj"].up())
                at = 6 - pieces_evac[0] % 2
                pieces_evac[0] += 1
                kind, a, b = piece
                if kind == "k":
                    c, width = KEY_CHUNKS_EVEN[b]
                    act.copy(kTv[:, n, a, c:c + width], bank(at, width)).then_inc(s.proj_sb, 1)
                elif b - a == 2:
                    act.copy(ctxN[:, n, a:b, :].rearrange("p t n -> p (t n)"), bank(at)).then_inc(s.proj_sb, 1)
                else:
                    act.copy(ctxN[0:LAST_KEYS, n, a, :], bank(at, D, slice(0, LAST_KEYS))).then_inc(s.proj_sb, 1)

            pieces_evac = [0]

            def finish(g):
                if g == 2:
                    copy_xnT(7)
                if g == 3:
                    act.wait_ge(s.sqkv_ps, T["sqkv"].up())
                    act.copy(sqT.rearrange("p k t -> p (k t)"), bank(7, 256)).then_inc(s.sqkv_ready, 1)
                    act.copy(skT.rearrange("p k t -> p (k t)"), bank(7, 256, at=256)).then_inc(s.sqkv_ready, 1)
                    act.copy(v4, bank(6, 256)).then_inc(s.sqkv_ready, 1)
                if g in (5, 7, 9, 11):
                    n = (g - 5) // 2 % 2
                    act.wait_ge(s.s4_masked, T["s4"].up())
                    for k in range(HPQ):
                        act.activation(s4[n][:, k, :], s4[n][:, k, :], ACT.Exp, bias=s4_nmax[n][:, k:k + 1], scale=HD ** -0.5,
                                       accum_out=s4_sum[n][:, k:k + 1]).then_inc(s.p4_ready, 1)
                if g in (6, 8, 10, 12):
                    act.wait_ge(s.p4T_ps, T["p4T"].up())
                    act.copy(p4T.rearrange("p h t -> p (h t)"), bank(7)).then_inc(s.p4T_ready, 1)

            def prepare(g):
                if g == 19:
                    copy_xnT(7)
                if g == 20:
                    act.wait_ge(s.qB_ps, T["qB"].up())
                    act.mul(qT.rearrange("p k t -> p (k t)"), bank(7, 256), HD ** -0.5).then_inc(s.qB_ready, 1)

            def act_pair(first, last):
                for b in range(2):
                    if not (last and b == 1):
                        pieces_evac[0] = 0
                        for piece in PIECES:
                            evac(piece, (b + 1) % 2)
                    for t in range(KEY_TILES):
                        g = b * KEY_TILES + t
                        rows = slice(0, keys_of(t))
                        act.wait_ge(s.sc_ps, T["sc"].up())
                        if t >= PROBS:
                            act.wait_ge(s.sum_done, T["pv"].now() + t - PROBS + 1)
                        act.activation(probs[rows, t % PROBS, :], PS[rows, 1024 * (t % 2):1024 * (t % 2) + 1024],
                                       ACT.Exp).then_inc(s.pr_ready, 1)
                        if not first:
                            finish(g)
                        if not last:
                            if g == 20:
                                act.wait_ge(s.qbd_ready, T["qbd"].up())
                                T["qbd"].up()
                            prepare(g)
                    T["pv"].up(KEY_TILES)

            T["qbd"].up()
            prepare(19)
            prepare(20)
            pieces_evac[0] = 0
            for piece in PIECES:
                evac(piece, 0)
            act_pair(True, False)
            with act.Fori(1, TILES - 1) as i:
                enter("B", i, 1)
                act_pair(False, False)
            leave("B", TILES - 2, 1)
            act_pair(False, True)
            for g in range(16):
                finish(g)

            with act.Fori(0, TILES) as i:
                enter("M", i)
                copy_xnT()
            leave("M", TILES)
            act.wait_ge(s.rexp_in, 1)
            act.activation(rp, logits, ACT.Exp).then_inc(s.rexp_out, 1)
            with act.Fori(0, EXPERTS // 2) as i:
                for n in range(2 * CHUNKS * HT):
                    act.wait_ge(s.g_ps, i * (2 * CHUNKS * HT) + n + 1)
                    if n >= 2:
                        act.wait_ge(s.hM_ready, i * (2 * CHUNKS * HT) + n - 1)
                    act.activation(silu_g[n % 2], bank(n % 2), ACT.Silu).then_inc(s.silu_g_ready, 1)

        @block.tensor
        def _(pe):
            names = dict(xn=dict(A=2, B=2, M=1), xnT=dict(A=2, B=2, M=1), qk=dict(A=1), probsA=dict(A=1), pT=dict(A=4),
                         att=dict(A=1), attT=dict(A=1), qkv=dict(A=2), sp=dict(A=1), spT=dict(A=1),
                         xq=dict(F=TPC), xqT=dict(F=TPC), diag=dict(F=2), h_scaled=dict(F=HT), hmax=dict(F=1), hq=dict(F=HT),
                         psb=dict(B=2 * len(PIECES)), mx=dict(B=2 * MAX_UNITS), m8=dict(B=2), shift=dict(B=4),
                         kTr=dict(B=2), qbd=dict(B=2), qbdr=dict(B=2), pr=dict(B=2 * KEY_TILES),
                         attn=dict(B=2), sqkv=dict(B=3), skbd=dict(B=QUARTERS), s4m=dict(B=QUARTERS), p4=dict(B=QUARTERS * HPQ), p4T=dict(B=QUARTERS),
                         cat=dict(B=QUARTERS), x_done=dict(A=2, F=TPC, B=3),
                         ctx=dict(A=16), ctxB=dict(B=16))
            T = {k: Tally(**v) for k, v in names.items()}

            def enter(phase, i, first=0):
                for t in T.values():
                    t.enter(phase, i, first)

            def leave(phase, n, first=0):
                for t in T.values():
                    t.leave(phase, n, first)

            pe.wait_ge(s.weights_in, WEIGHTS_IN)
            pe.wait_ge(s.consts_ready, NCONST + 1)
            for o in range(KT):
                for k in range(KT):
                    mm = pe.matmul(bank(0, D, at=o * D), wqT_raw[:, k, o * P:o * P + P], wkT_raw[:, k, :], start=k == 0, stop=k == KT - 1)
            mm.then_inc(s.fold_ps, 1)
            for o in range(KT):
                for k in range(KT):
                    mm = pe.matmul(bank(1, D, at=o * D), wkT_raw[:, k, o * P:o * P + P], wv_raw[:, k, :], start=k == 0, stop=k == KT - 1)
            mm.then_inc(s.fold_ps, 1)
            pe.wait_ge(s.tern_sum, 1)
            pe.matmul(bank(2, 2), ones[:, :], small[:, 0:2], start=True, stop=True).then_inc(s.tern_ps, 1)
            pe.wait_ge(s.fold_ready, 2)

            def transpose_xn(to=0):
                pe.wait_ge(s.xn_ready, T["xn"].up())
                for k in range(KT):
                    mm = pe.transpose(bank(to, P, at=k * P), xn[:, k * P:k * P + P], ident[:, :])
                mm.then_inc(s.xn_ps, 1)

            with pe.Fori(0, TILES) as i:
                enter("A", i)
                transpose_xn()
                pe.wait_ge(s.xnT_ready, T["xnT"].up())
                for o in range(KT):
                    for k in range(KT):
                        mm = pe.matmul(bank(1, P, at=o * P), fold[:, k, o * P:o * P + P], xnT[:, k, :], start=k == 0, stop=k == KT - 1)
                mm.then_inc(s.qk_ps, 1)
                pe.wait_ge(s.qk_ready, T["qk"].up())
                pe.wait_ge(s.ctxT_in, T["ctx"].up(16))
                for n, (c, width) in enumerate(KEY_CHUNKS):
                    for k in range(KT):
                        for b in range(2):
                            mm = pe.matmul(bank(4 + n, width, slice(b * S, b * S + S)), qkT[:, k, b * S:b * S + S],
                                           ctxTv[:, b, k, c:c + width], start=k == 0, stop=k == KT - 1)
                mm.then_inc(s.scores_ps, 1)
                pe.wait_ge(s.probsA_ready, T["probsA"].up())
                for t in range(KEY_TILES):
                    mm = pe.transpose(bank(t // 4, P, slice(0, keys_of(t)), (t % 4) * P), probsA[:, t * P:t * P + keys_of(t)], ident[:, :])
                    if t % 4 == 3 or t == KEY_TILES - 1:
                        mm.then_inc(s.pT_ps, 1)
                pe.wait_ge(s.ctxN_in, T["ctx"].now())
                for t in range(KEY_TILES):
                    if t % 4 == 0:
                        pe.wait_ge(s.pT_ready, T["pT"].up())
                    rows = slice(0, keys_of(t))
                    for b in range(2):
                        mm = pe.matmul(bank(4, D, slice(b * S, b * S + S)), probsAT[rows, t, b * S:b * S + S], ctxN[rows, b, t, :],
                                       start=t == 0, stop=t == KEY_TILES - 1)
                mm.then_inc(s.av_ps, 1)
                pe.wait_ge(s.att_ready, T["att"].up())
                for k in range(KT):
                    mm = pe.transpose(bank(0, P, at=k * P), xn[:, k * P:k * P + P], ident[:, :])
                mm.then_inc(s.attT_ps, 1)
                pe.wait_ge(s.attT_ready, T["attT"].up())
                for k in range(KT):
                    mm = pe.matmul(bank(1, D), xnT[:, k, :], vout[:, k, :], start=k == 0, stop=k == KT - 1)
                mm.then_inc(s.outA_ps, 1)
                transpose_xn()
                pe.wait_ge(s.xnT_ready, T["xnT"].up())
                for n, m in enumerate(("sq", "sk")):
                    for k in range(KT):
                        pe.matmul(bank(1, P, slice(0, 64), n * P), w[m][:, k, :], xnT[:, k, :], start=k == 0, stop=k == KT - 1)
                for k in range(KT):
                    mm = pe.matmul(bank(2, D), xnT[:, k, :], w["sv"][:, k, :], start=k == 0, stop=k == KT - 1)
                mm.then_inc(s.qkv_ps, 1)
                pe.wait_ge(s.qkv_ready, T["qkv"].up(2))
                pe.matmul(bank(3, P), qk_s[:, 0:P], qk_s[:, P:2 * P], start=True, stop=True).then_inc(s.ss_ps, 1)
                pe.wait_ge(s.sp_ready, T["sp"].up())
                pe.transpose(bank(4, P), p_s, ident[:, :]).then_inc(s.spT_ps, 1)
                pe.wait_ge(s.spT_ready, T["spT"].up())
                pe.matmul(bank(5, D), pT_s, v_s, start=True, stop=True).then_inc(s.so_ps, 1)
                T["x_done"].up(2)
            leave("A", TILES)

            with pe.Fori(0, CHUNKS) as c:
                enter("F", c)
                for k in range(TPC):
                    pe.wait_ge(s.xq_ready, T["xq"].up())
                    if k:
                        pe.wait_ge(s.xqT_ready, T["xqT"].up())
                    for a in range(KT):
                        mm = pe.transpose(bank(0, P).bitcast(BF16)[:, a * P:a * P + P], xq[:, a * P:a * P + P], identb[:, :])
                    mm.then_inc(s.xqT_ps, 1)
                pe.wait_ge(s.diag_ready, T["diag"].up())
                for k in range(TPC):
                    mm = pe.matmul(bank(1, P, at=k * P), ones[:, :], diag[:, k, :], start=True, stop=True)
                mm.then_inc(s.rows_ps, 1)
                pe.wait_ge(s.xqT_ready, T["xqT"].up())
                for j in range(HT):
                    if j >= 2:
                        pe.wait_ge(s.h_scaled, T["h_scaled"].up())
                    for a in range(KT):
                        mm = pe.matmul(bank(2 + j % 2), w1q[:, a, j * P:j * P + P], xqT[:, a, :], start=a == 0, stop=a == KT - 1)
                    mm.then_inc(s.h_ps, 1)
                T["h_scaled"].up(2)
                pe.wait_ge(s.hmax_ready, T["hmax"].up())
                for k in range(TPC):
                    mm = pe.transpose(bank(4, P, at=k * P), hmax[:, k * P:k * P + P], ident[:, :])
                mm.then_inc(s.hmaxT_ps, 1)
                pe.wait_ge(s.diag_ready, T["diag"].up())
                for k in range(TPC):
                    mm = pe.matmul(bank(5, P, at=k * P), ones[:, :], diag[:, k, :], start=True, stop=True)
                mm.then_inc(s.rows_ps, 1)
                pe.wait_ge(s.hq_ready, T["hq"].up(HT))
                for k in range(TPC):
                    if k >= 2:
                        pe.wait_ge(s.x_done, T["x_done"].up())
                    for j in range(HT):
                        mm = pe.matmul(bank(6 + k % 2, D), hq[:, j, k * P:k * P + P], w2q[:, j, :], start=j == 0, stop=j == HT - 1)
                    mm.then_inc(s.o_ps, 1)
                T["x_done"].up(2)
            leave("F", CHUNKS)

            count = [0]

            def project(piece, n):
                kind, a, b = piece
                at = 6 - count[0] % 2
                count[0] += 1
                if count[0] > 2:
                    pe.wait_ge(s.proj_sb, T["psb"].now() + count[0] - 2)
                if kind == "k":
                    c, width = KEY_CHUNKS_EVEN[b]
                    for k in range(KT):
                        mm = pe.matmul(bank(at, width), w["ck"][:, k, a * P:a * P + P], ctxTv[:, n, k, c:c + width],
                                       start=k == 0, stop=k == KT - 1)
                else:
                    for t in range(a, b):
                        rows = slice(0, keys_of(t))
                        for k in range(KT):
                            mm = pe.matmul(bank(at, D, rows, (t - a) * D), ctxTv[:, n, k, t * P:t * P + keys_of(t)], w["cv"][:, k, :],
                                           start=k == 0, stop=k == KT - 1)
                mm.then_inc(s.proj_ps, 1)

            def maxima(n, u):
                pair, half = divmod(u, 2)
                if u >= 2:
                    pe.wait_ge(s.mx_red, T["mx"].now() + u - 1)
                for c, width in KEY_CHUNKS_EVEN[2 * half:2 * half + 2]:
                    at = 1024 * ((u + 1) % 2) + c - 1024 * half
                    at = PS[:, at:at + width]
                    mm = pe.matmul(at, qbdr[:, n, pair // 4, (pair % 4) * P:(pair % 4) * P + P], kTr[:, pair // 4, c:c + width],
                                   start=True, stop=True)
                mm.then_inc(s.mx_ps, 1)

            def weigh(n, t):
                rows = slice(0, keys_of(t))
                pe.wait_ge(s.pr_ready, T["pr"].up())
                for g in range(KT):
                    for j in range(4):
                        mm = pe.matmul(bank(4, P, slice(32 * j, 32 * j + 32), g * P), ctxN[rows, n, t, g * P + 32 * j:g * P + 32 * j + 32],
                                       probs[rows, t % PROBS, (4 * g + j) * P:(4 * g + j) * P + P],
                                       start=t == 0 and g == 0, stop=t == KEY_TILES - 1, skip_group_check=True)
                mm.then_inc(s.pv_done, 1)

            def end_batch(n, fin):
                pe.wait_ge(s.sum_done, T["pr"].now())
                if n == 0 and fin:
                    pe.wait_ge(s.p4T_ready, T["p4T"].now() + 1)
                for g in range(KT):
                    for j in range(4):
                        mm = pe.matmul(bank(7, P, slice(32 * j, 32 * j + 32), g * P), ones[:, 0:32],
                                       probs_sum[:, (4 * g + j) * P:(4 * g + j) * P + P], start=g == 0, stop=True, skip_group_check=True)
                mm.then_inc(s.den_ps, 1)

            def finish(g):
                if g == 0:
                    pe.wait_ge(s.attn_ready, T["attn"].up(2))
                    for k in range(KT):
                        mm = pe.matmul(bank(7, D), attn_ch[:, k, :], w["cp"][:, k, :], start=k == 0, stop=k == KT - 1)
                    mm.then_inc(s.po_ps, 1)
                if g == 2:
                    transpose_xn(7)
                if g == 3:
                    pe.wait_ge(s.proj_sb, T["psb"].now())
                    pe.wait_ge(s.xnT_ready, T["xnT"].up())
                    for n, m in enumerate(("hq", "hk")):
                        for a in range(KT):
                            pe.matmul(bank(7, P, at=(2 * n + a) * P), w[m][:, a, :], xnT[:, a, :], start=True, stop=True)
                    for a in range(KT):
                        mm = pe.matmul(bank(6, P, at=a * P), xnT[:, a, :], w["hv"][:, a, :], start=True, stop=True)
                    mm.then_inc(s.sqkv_ps, 1)
                if g in (4, 6, 8, 10):
                    q = (g - 4) // 2
                    if q == 0:
                        pe.wait_ge(s.sqkv_ready, T["sqkv"].up(3))
                    else:
                        pe.wait_ge(s.s4_masked, T["s4m"].up())
                    pe.wait_ge(s.skbd_ready, T["skbd"].up())
                    pe.matmul(bank(6), sqT[:, q // 2, :], skbd[q % 2].rearrange("p h t -> p (h t)"), start=True, stop=True)\
                      .then_inc(s.s4_ps, 1)
                if g in (6, 8, 10, 12):
                    q = (g - 6) // 2
                    pe.wait_ge(s.p4_ready, T["p4"].up(HPQ))
                    for k in range(HPQ):
                        mm = pe.transpose(bank(7, P, at=k * P), s4[q % 2][:, k, :], ident[:, :])
                    mm.then_inc(s.p4T_ps, 1)
                if g in (7, 9, 11, 13):
                    q = (g - 7) // 2
                    if q:
                        pe.wait_ge(s.cat_ready, T["cat"].up())
                    else:
                        pe.wait_ge(s.proj_sb, T["psb"].now())
                    if q == 3:
                        pe.wait_ge(s.proj_sb, T["psb"].now())
                    pe.wait_ge(s.p4T_ready, T["p4T"].up())
                    for k in range(HPQ):
                        mm = pe.matmul(bank(5, HD, at=k * HD), p4T[:, k, :], v4[:, (q * HPQ + k) * HD:(q * HPQ + k + 1) * HD], start=True, stop=True)
                    mm.then_inc(s.o4_ps, 1)
                if g == 15:
                    T["s4m"].up()
                    pe.wait_ge(s.cat_ready, T["cat"].up())
                    pe.matmul(bank(7, 1), ones[:, :], ones[:, 0:1], start=True, stop=True)
                    catv = cat[:, :].rearrange("p (i r) -> p r i", r=4)
                    for r in range(4):
                        for b in range(2):
                            rows = slice(b * S, b * S + S)
                            mm = pe.matmul(bank(5 + b, D, rows), catv[rows, r, :], wo[rows, r, :], start=r == 0, stop=r == 3)
                    mm.then_inc(s.wo_ps, 1)
                    T["x_done"].up(3)

            def prepare(g):
                if g == 19:
                    transpose_xn(7)
                if g == 20:
                    pe.wait_ge(s.xnT_ready, T["xnT"].up())
                    for o in range(KT):
                        for k in range(KT):
                            mm = pe.matmul(bank(7, P, at=o * P), w["cq"][:, k, o * P:o * P + P], xnT[:, k, :], start=k == 0, stop=k == KT - 1)
                    mm.then_inc(s.qB_ps, 1)

            def pe_batch(n, first, last):
                ahead = not (last and n == 1)
                pieces = list(PIECES) if ahead else []
                count[0] = 0
                pe.wait_ge(s.kTr_ready, T["kTr"].up())
                pe.wait_ge(s.qbdr_ready, T["qbdr"].up())
                pe.wait_ge(s.qbd_ready, T["qbd"].up())
                if ahead:
                    pe.wait_ge((s.ctxB1_in, s.ctxB0_in)[n], T["ctxB"].now() + (16 if n else 0))
                for u in range(MAX_UNITS):
                    maxima(n, u)
                    if not (first and n == 0):
                        if u == 0:
                            weigh(1 - n, KEY_TILES - 1)
                        if u == 2:
                            end_batch(1 - n, not first)
                    if ahead and u in PIECE_AFTER:
                        project(pieces.pop(0), 1 - n)
                T["mx"].up(MAX_UNITS)
                if ahead:
                    project(pieces.pop(0), 1 - n)
                pe.wait_ge(s.m8_ready, T["m8"].up())
                pe.matmul(bank(2, 1, at=511), ones[:, :], ones[:, 0:1], start=True, stop=True)
                pe.transpose(bank(2, P, slice(0, 40)), m8[:, :], ident[:, :]).then_inc(s.m8T_ps, 1)
                for piece in pieces:
                    project(piece, 1 - n)
                if ahead:
                    T["psb"].up(len(PIECES))
                pe.wait_ge(s.shift_ready, T["shift"].up(2))
                for t in range(KEY_TILES):
                    rows = slice(0, keys_of(t))
                    for a in range(KT):
                        at = bank(2 * (t % 2) + a, 512, rows)
                        pe.matmul(at, onesb[:, rows], shift[:, a * 512:a * 512 + 512], start=True, stop=False)
                        mm = pe.matmul(at, kTv[:, n, a, t * P:t * P + keys_of(t)], qbd[:, n, a, :], start=False, stop=True)
                    mm.then_inc(s.sc_ps, 1)
                    if t >= 1:
                        weigh(n, t - 1)
                    if not first:
                        finish(n * KEY_TILES + t)
                    if not last:
                        prepare(n * KEY_TILES + t)

            def pe_pair(first, last):
                for n in range(2):
                    pe_batch(n, first, last)
                T["ctxB"].up(16)

            pe.wait_ge(s.x_done, XDONE_F)
            prepare(19)
            prepare(20)
            count[0] = 0
            pe.wait_ge(s.ctxB0_in, 16)
            for piece in PIECES:
                project(piece, 0)
            T["psb"].up(len(PIECES))
            T["ctxB"].up(16)
            pe_pair(True, False)
            with pe.Fori(1, TILES - 1) as i:
                enter("B", i, 1)
                pe_pair(False, False)
            leave("B", TILES - 2, 1)
            pe_pair(False, True)
            weigh(1, KEY_TILES - 1)
            end_batch(1, True)
            for g in range(16):
                finish(g)

            with pe.Fori(0, TILES) as i:
                for t in ("xn", "xnT"):
                    T[t].enter("M", i)
                transpose_xn()
                pe.wait_ge(s.xnT_ready, T["xnT"].up())
                for k in range(KT):
                    mm = pe.matmul(bank(2, EXPERTS), xnT[:, k, :], w["router"][:, k, :], start=k == 0, stop=k == KT - 1)
                mm.then_inc(s.logits_ps, 1)
            pe.wait_ge(s.rsum_ready, 1)
            pe.matmul(bank(3, 2 * EXPERTS), ones[:, :], rsmall[:, 40:40 + 2 * EXPERTS], start=True, stop=True).then_inc(s.rsum_ps, 1)
            pe.wait_ge(s.xT_all, TILES)
            pe.wait_ge(s.gates_ready, 1)
            wide = CHUNKS * HT
            with pe.Fori(0, EXPERTS // 2) as i:
                for n in range(2):
                    pe.wait_ge((s.expert0_in, s.expert1_in)[n], i * 16 + 16)
                    gw, uw, dw = (expert_w[n][:, 2048 * m:2048 * m + 2048] for m in range(3))
                    gw, uw = (m.rearrange("p (k h) -> p k h", k=KT) for m in (gw, uw))
                    dw = dw.rearrange("p (j n) -> p j n", j=HT)
                    for c in range(CHUNKS):
                        for j in range(HT):
                            at = (n * CHUNKS + c) * HT + j
                            if at >= 2:
                                pe.wait_ge(s.hM_ready, i * (2 * wide) + at - 1)
                            for k in range(KT):
                                mm = pe.matmul(bank(j % 2), gw[:, k, j * P:j * P + P], xnTall[:, k, c * CHUNK:c * CHUNK + CHUNK],
                                               start=k == 0, stop=k == KT - 1)
                            mm.then_inc(s.g_ps, 1)
                            for k in range(KT):
                                mm = pe.matmul(bank(2 + j % 2), uw[:, k, j * P:j * P + P], xnTall[:, k, c * CHUNK:c * CHUNK + CHUNK],
                                               start=k == 0, stop=k == KT - 1)
                            mm.then_inc(s.u_ps, 1)
                        pe.wait_ge(s.hM_ready, i * (2 * wide) + (n * CHUNKS + c + 1) * HT)
                        for k in range(TPC):
                            tile = (n * CHUNKS + c) * TPC + k
                            if tile >= 2:
                                pe.wait_ge(s.eo_added, i * (2 * CHUNKS * TPC) + tile - 1)
                            for j in range(HT):
                                mm = pe.matmul(bank(4 + k % 2, D), hM[:, j, k * P:k * P + P], dw[:, j, :], start=j == 0, stop=j == HT - 1)
                            mm.then_inc(s.eo_ps, 1)

        @block.vector
        def _(v):
            names = dict(step=dict(A=7, F=56, B=27, M=1),
                         rstd=dict(A=2, F=TPC, B=2, M=1), scores=dict(A=1), pT=dict(A=4), probsA=dict(A=1), av=dict(A=1), outA=dict(A=1),
                         ss=dict(A=1), sp=dict(A=1), so=dict(A=1), x_done=dict(A=2, F=TPC, B=3),
                         xqT=dict(F=TPC), rows=dict(F=2), h_ps=dict(F=HT), mid=dict(F=HT), silu=dict(F=HT), hmaxT=dict(F=1), o=dict(F=TPC),
                         mx=dict(B=2 * MAX_UNITS), m8T=dict(B=2), pr=dict(B=2 * KEY_TILES), den=dict(B=2),
                         po=dict(B=1), s4=dict(B=QUARTERS), p4=dict(B=QUARTERS * HPQ), p4T=dict(B=QUARTERS), o4=dict(B=QUARTERS), wo=dict(B=1),
                         logits=dict(M=1))
            T = {k: Tally(**q) for k, q in names.items()}

            def enter(phase, i, first=0):
                for t in T.values():
                    t.enter(phase, i, first)

            def leave(phase, n, first=0):
                for t in T.values():
                    t.leave(phase, n, first)

            def own():
                return T["step"].up()

            def layer_norm(xi):
                moments(xi)
                return normalize(xi)

            def moments(xi):
                v.bn_stats(stat[:, :], xi).then_inc(s.vec_step, 1)
                v.wait_ge(s.vec_step, own())
                v.tensor_copy(carrier_v[:, :], eps[:, :])
                v.bn_aggr(mv[:, :], stat[:, :]).then_inc(s.ln_var, 1)

            def normalize(xi):
                v.wait_ge(s.ln_rstd, T["rstd"].up())
                return v.tensor_scalar(xn[:, :], xi, mv[:, 0:1], rstd[:, 1:2], ALU.subtract, ALU.mult)

            def diagonals(at):
                for k in range(TPC):
                    ins = v.tensor_scalar(diag[:, k, :], ident[:, :], small[:, at + k:at + k + 1], None, ALU.mult)
                    if k < TPC - 1:
                        ins.then_inc(s.vec_step, 1)
                T["step"].up(TPC - 1)
                ins.then_inc(s.diag_ready, 1)

            def side_taps(j):
                acc = hacc[j % 2].rearrange("p (b t) -> p b t", b=BPC)
                v.wait_ge(s.conv_mid, T["mid"].up())
                v.scalar_tensor_tensor(acc, hpad[j % 3][:, :, 0:S], convw[:, j, 0:1], acc, ALU.mult, ALU.add).then_inc(s.vec_step, 1)
                v.wait_ge(s.vec_step, own())
                v.scalar_tensor_tensor(acc, hpad[j % 3][:, :, 2:S + 2], convw[:, j, 2:3], acc, ALU.mult, ALU.add).then_inc(s.conv_done, 1)

            v.wait_ge(s.weights_in, WEIGHTS_IN)
            for n, r in enumerate((w1_raw, w2_raw)):
                v.tensor_reduce(small[:, n:n + 1], r, AX, ALU.add, apply_absolute_value=True).then_inc(s.vec_step, 1)
            v.wait_ge(s.vec_step, T["step"].up(2))
            v.wait_ge(s.consts_ready, NCONST + 1)
            v.tensor_reduce(parity[:, 0:1], head_of[:, 0::2], AX, ALU.add).then_inc(s.vec_step, 1)
            v.tensor_reduce(parity[:, 1:2], head_of[:, 1::2], AX, ALU.add).then_inc(s.tern_sum, 1)
            T["step"].up()
            v.wait_ge(s.tern_ps, 1)
            v.tensor_scalar(small[:, 80:82], bank(2, 2), 1.0 / (HID * D), 1e-5, ALU.mult, ALU.max).then_inc(s.vec_step, 1)
            v.wait_ge(s.vec_step, own())
            v.reciprocal(small[:, 82:84], small[:, 80:82]).then_inc(s.vec_step, 1)
            v.tensor_scalar(small[:, 84:86], small[:, 80:82], 1 / 127, None, ALU.mult).then_inc(s.vec_step, 1)
            v.wait_ge(s.vec_step, T["step"].up(2))
            for n, (r, q) in enumerate(((w1_raw, w1q), (w2_raw, w2q))):
                v.tensor_scalar(r, r, small[:, 82 + n:83 + n], MAGIC, ALU.mult, ALU.add).then_inc(s.vec_step, 1)
                v.wait_ge(s.vec_step, own())
                v.tensor_scalar(r, r, MAGIC, 1.0, ALU.subtract, ALU.min).then_inc(s.vec_step, 1)
                v.wait_ge(s.vec_step, own())
                v.tensor_scalar(q[:, :, :].rearrange("p a n -> p (a n)"), r, -1.0, None, ALU.max).then_inc(s.vec_step, 1)
                v.wait_ge(s.vec_step, own())

            with v.Fori(0, TILES) as i:
                enter("A", i)
                xi = x[:, bass.ds(i, 1), :].rearrange("p a n -> p (a n)")
                layer_norm(xi).then_inc(s.xn_ready, 1)
                v.wait_ge(s.scores_ps, T["scores"].up())
                v.tensor_reduce(small[:, 0:1], PS[:, 2048:2048 + NK], AX, ALU.max).then_inc(s.vec_step, 1)
                v.wait_ge(s.vec_step, own())
                v.tensor_scalar(small[:, 1:2], small[:, 0:1], -1 / 16, None, ALU.mult).then_inc(s.nmax_ready, 1)
                for q in range(4):
                    v.wait_ge(s.pT_ps, T["pT"].up())
                    if q < 3:
                        v.tensor_copy(probsAT[:, 4 * q:4 * q + 4, :].rearrange("p t q -> p (t q)"), bank(q)).then_inc(s.pT_ready, 1)
                    else:
                        v.tensor_copy(probsAT[0:LAST_KEYS, 12, :], bank(3, P, slice(0, LAST_KEYS))).then_inc(s.pT_ready, 1)
                v.wait_ge(s.probsA_ready, T["probsA"].up())
                v.reciprocal(small[:, 3:4], small[:, 2:3]).then_inc(s.vec_step, 1)
                v.wait_ge(s.vec_step, own())
                v.wait_ge(s.av_ps, T["av"].up())
                v.tensor_scalar(xn[:, :], bank(4, D), small[:, 3:4], None, ALU.mult).then_inc(s.att_ready, 1)
                v.wait_ge(s.outA_ps, T["outA"].up())
                v.tensor_tensor(xi, bank(1, D), xi, ALU.add).then_inc(s.x_done, 1)
                v.wait_ge(s.x_done, T["x_done"].up())
                v.tensor_copy(carrier_v[:, :], eps[:, :])
                layer_norm(xi).then_inc(s.xn_ready, 1)
                v.wait_ge(s.ss_ps, T["ss"].up())
                v.tensor_tensor(s_s, bank(3, P), causal[:, :], ALU.add).then_inc(s.vec_step, 1)
                v.wait_ge(s.vec_step, own())
                v.tensor_reduce(small[:, 4:5], s_s, AX, ALU.max).then_inc(s.vec_step, 1)
                v.wait_ge(s.vec_step, own())
                v.tensor_scalar(small[:, 5:6], small[:, 4:5], -1 / 8, None, ALU.mult).then_inc(s.snmax_ready, 1)
                v.wait_ge(s.sp_ready, T["sp"].up())
                v.reciprocal(small[:, 7:8], small[:, 6:7]).then_inc(s.vec_step, 1)
                v.wait_ge(s.vec_step, own())
                v.wait_ge(s.so_ps, T["so"].up())
                v.scalar_tensor_tensor(xi, bank(5, D), small[:, 7:8], xi, ALU.mult, ALU.add).then_inc(s.x_done, 1)
                T["x_done"].up()
            leave("A", TILES)

            for n in range(3):
                v.memset(hpad[n], 0.0).then_inc(s.vec_step, 1)
            v.wait_ge(s.vec_step, T["step"].up(3))
            with v.Fori(0, CHUNKS) as c:
                enter("F", c)
                for k in range(TPC):
                    xk = x[:, bass.ds(c * TPC + k, 1), :].rearrange("p a n -> p (a n)")
                    layer_norm(xk).then_inc(s.vec_step, 1)
                    v.wait_ge(s.vec_step, own())
                    v.tensor_reduce(small[:, 0:1], xn[:, :], AX, ALU.max, apply_absolute_value=True).then_inc(s.vec_step, 1)
                    v.wait_ge(s.vec_step, own())
                    v.tensor_scalar(small[:, 8 + k:9 + k], small[:, 0:1], 1e-5, None, ALU.max).then_inc(s.vec_step, 1)
                    v.wait_ge(s.vec_step, own())
                    v.reciprocal(small[:, 1:2], small[:, 8 + k:9 + k]).then_inc(s.vec_step, 1)
                    v.wait_ge(s.vec_step, own())
                    v.tensor_scalar(small[:, 2:3], small[:, 1:2], 127.0, None, ALU.mult).then_inc(s.vec_step, 1)
                    v.wait_ge(s.vec_step, own())
                    v.tensor_scalar(xn[:, :], xn[:, :], small[:, 2:3], MAGIC, ALU.mult, ALU.add).then_inc(s.vec_step, 1)
                    v.wait_ge(s.vec_step, own())
                    if k:
                        v.wait_ge(s.xqT_ps, T["xqT"].up())
                    v.tensor_scalar(xq, xn[:, :], MAGIC, None, ALU.subtract).then_inc(s.xq_ready, 1)
                T["xqT"].up()
                v.tensor_scalar(small[:, 12:16], small[:, 8:12], small[:, 84:85], None, ALU.mult).then_inc(s.vec_step, 1)
                v.wait_ge(s.vec_step, own())
                diagonals(12)
                v.wait_ge(s.rows_ready, T["rows"].up())
                for j in range(HT):
                    v.wait_ge(s.h_ps, T["h_ps"].up())
                    v.tensor_tensor(hpad[j % 3][:, :, 1:S + 1], bank(2 + j % 2).rearrange("p (b t) -> p b t", b=BPC),
                                    rowscale.rearrange("p (b t) -> p b t", b=BPC), ALU.mult).then_inc(s.h_scaled, 1)
                    if j >= 1:
                        side_taps(j - 1)
                side_taps(HT - 1)
                v.wait_ge(s.silu_done, T["silu"].up(HT))
                v.tensor_reduce(hmax, hs.rearrange("p j t -> p t j"), AX, ALU.max, apply_absolute_value=True).then_inc(s.hmax_ready, 1)
                v.wait_ge(s.hmaxT_ps, T["hmaxT"].up())
                v.tensor_reduce(small[:, 16:20], bank(4).rearrange("p (k t) -> p k t", k=TPC), AX, ALU.max).then_inc(s.vec_step, 1)
                v.wait_ge(s.vec_step, own())
                v.tensor_scalar(small[:, 20:24], small[:, 16:20], 1e-5, None, ALU.max).then_inc(s.vec_step, 1)
                v.wait_ge(s.vec_step, own())
                v.reciprocal(small[:, 24:28], small[:, 20:24]).then_inc(s.vec_step, 1)
                v.wait_ge(s.vec_step, own())
                v.tensor_scalar(small[:, 28:32], small[:, 24:28], 127.0, None, ALU.mult).then_inc(s.vec_step, 1)
                v.tensor_scalar(small[:, 32:36], small[:, 20:24], small[:, 85:86], None, ALU.mult).then_inc(s.vec_step, 1)
                v.wait_ge(s.vec_step, T["step"].up(2))
                diagonals(28)
                v.wait_ge(s.rows_ready, T["rows"].up())
                for j in range(HT):
                    v.tensor_tensor(hs[:, j, :], hs[:, j, :], rowscale, ALU.mult).then_inc(s.vec_step, 1)
                    v.wait_ge(s.vec_step, own())
                    v.tensor_scalar(hq[:, j, :], hs[:, j, :], MAGIC, MAGIC, ALU.add, ALU.subtract).then_inc(s.hq_ready, 1)
                for k in range(TPC):
                    xk = x[:, bass.ds(c * TPC + k, 1), :].rearrange("p a n -> p (a n)")
                    v.wait_ge(s.o_ps, T["o"].up())
                    v.scalar_tensor_tensor(xk, bank(6 + k % 2, D), small[:, 32 + k:33 + k], xk, ALU.mult, ALU.add).then_inc(s.x_done, 1)
                T["x_done"].up(TPC)
                v.wait_ge(s.x_done, T["x_done"].now())
            leave("F", CHUNKS)

            def end_batch(b):
                v.wait_ge(s.den_ps, T["den"].up())
                v.reciprocal(weighed_sb[:, :], bank(7, 256)).then_inc(s.vec_step, 1)
                v.wait_ge(s.vec_step, own())
                v.tensor_tensor(weighed_sb[:, :], bank(4, 256), weighed_sb[:, :], ALU.mult).then_inc(s.vec_step, 1)
                v.wait_ge(s.vec_step, own())
                wv = weighed_sb[:, :].rearrange("p (g h q) -> p g h q", g=KT, h=2)
                mine = attn_ch[:, :, b * S:b * S + S]
                v.tensor_scalar(mine, wv[:, :, 0, :], parity[:, 0:1], None, ALU.mult).then_inc(s.vec_step, 1)
                v.wait_ge(s.vec_step, own())
                v.scalar_tensor_tensor(mine, wv[:, :, 1, :], parity[:, 1:2], mine, ALU.mult, ALU.add).then_inc(s.attn_ready, 1)

            def maxima(b, first):
                for u in range(MAX_UNITS):
                    pair, half = divmod(u, 2)
                    width = 1024 if half == 0 else NK - 1024
                    at = 1024 * ((u + 1) % 2)
                    v.wait_ge(s.mx_ps, T["mx"].up())
                    v.tensor_reduce(mpart[:, pair, half:half + 1], PS[:, at:at + width], AX, ALU.max).then_inc(s.mx_red, 1)
                    if u == 2 and not (first and b == 0):
                        end_batch(1 - b)
                v.wait_ge(s.mx_red, T["mx"].now())
                v.tensor_reduce(m8[:, 0:PAIRS], mpart[:, :, :], AX, ALU.max).then_inc(s.vec_step, 1)
                v.wait_ge(s.vec_step, own())
                v.tensor_copy(m8[:, 32:32 + PAIRS], m8[:, 0:PAIRS]).then_inc(s.m8_ready, 1)
                v.wait_ge(s.m8T_ps, T["m8T"].up())
                v.tensor_scalar(sh8[:, 0, :], bank(2, P, slice(0, 40)), -1.0, None, ALU.mult).then_inc(s.vec_step, 1)
                v.wait_ge(s.vec_step, own())
                v.scalar_tensor_tensor(sh8[:, 1, :], bank(2, P, slice(0, 40)), -1.0, sh8[:, 0, :], ALU.mult, ALU.subtract)\
                 .then_inc(s.vec_step, 1)
                v.wait_ge(s.vec_step, own())
                for part, rows in enumerate((slice(0, PAIRS), slice(32, 32 + PAIRS))):
                    v.tensor_tensor(shift[rows, :].rearrange("p (h q) -> p h q", h=PAIRS),
                                    sh8[rows, part, None, :].broadcast_to([PAIRS, PAIRS, P]),
                                    ident[rows, rows, None].broadcast_to([PAIRS, PAIRS, P]), ALU.mult).then_inc(s.shift_ready, 1)

            def finish(g, xi):
                if g == 0:
                    v.wait_ge(s.po_ps, T["po"].up())
                    v.tensor_tensor(xi, bank(7, D), xi, ALU.add).then_inc(s.vec_step, 1)
                    v.wait_ge(s.vec_step, own())
                    v.tensor_tensor(xi, xi, bias_p[:, :], ALU.add).then_inc(s.x_done, 1)
                    v.wait_ge(s.x_done, T["x_done"].up())
                    v.tensor_copy(carrier_v[:, :], eps[:, :])
                    moments(xi)
                if g == 1:
                    normalize(xi).then_inc(s.xn_ready, 1)
                if g in (4, 6, 8, 10):
                    q = (g - 4) // 2
                    if q >= 2:
                        v.wait_ge(s.p4T_ps, T["p4T"].up())
                    v.wait_ge(s.s4_ps, T["s4"].up())
                    v.tensor_tensor(s4[q % 2], bank(6).rearrange("p (h t) -> p h t", h=HPQ),
                                    causal[:, None, :].broadcast_to([P, HPQ, P]), ALU.add).then_inc(s.vec_step, 1)
                    v.wait_ge(s.vec_step, own())
                    v.tensor_reduce(s4_max, s4[q % 2], AX, ALU.max).then_inc(s.vec_step, 1)
                    v.wait_ge(s.vec_step, own())
                    v.tensor_scalar(s4_nmax[q % 2], s4_max, -(HD ** -0.5), None, ALU.mult).then_inc(s.s4_masked, 1)
                if g in (7, 9, 11, 13):
                    q = (g - 7) // 2
                    v.wait_ge(s.p4_ready, T["p4"].up(HPQ))
                    v.reciprocal(s4_inv[q % 2], s4_sum[q % 2]).then_inc(s.vec_step, 1)
                    v.wait_ge(s.vec_step, own())
                    v.wait_ge(s.o4_ps, T["o4"].up())
                    v.tensor_tensor(cat[:, q * HPQ * HD:(q + 1) * HPQ * HD].rearrange("p (h e) -> p h e", h=HPQ),
                                    bank(5, HPQ * HD).rearrange("p (h e) -> p h e", h=HPQ),
                                    s4_inv[q % 2][:, :, None].broadcast_to([P, HPQ, HD]), ALU.mult).then_inc(s.cat_ready, 1)
                if g == 15:
                    T["p4T"].up(2)
                    v.wait_ge(s.wo_ps, T["wo"].up())
                    for b in range(2):
                        rows = slice(b * S, b * S + S)
                        v.tensor_tensor(xi[rows, :], bank(5 + b, D, rows), xi[rows, :], ALU.add).then_inc(s.x_done, 1)
                    T["x_done"].up(2)

            def prepare(g, xi):
                if g == 17:
                    moments(xi)
                if g == 18:
                    normalize(xi).then_inc(s.xn_ready, 1)

            def vec_pair(before, after):
                for b in range(2):
                    maxima(b, before is None)
                    for t in range(KEY_TILES):
                        rows = slice(0, keys_of(t))
                        v.wait_ge(s.pr_ready, T["pr"].up())
                        if t == 0:
                            v.tensor_copy(probs_sum[:, :], probs[:, 0, :]).then_inc(s.sum_done, 1)
                        else:
                            v.wait_ge(s.sum_done, T["pr"].now(less=1))
                            v.tensor_tensor(probs_sum[rows, :], probs_sum[rows, :], probs[rows, t % PROBS, :], ALU.add).then_inc(s.sum_done, 1)
                        if before is not None:
                            finish(b * KEY_TILES + t, before)
                        if after is not None:
                            prepare(b * KEY_TILES + t, after)

            def tile_of_x(i):
                return x[:, bass.ds(i, 1), :].rearrange("p a n -> p (a n)")

            prepare(17, x[:, 0, :])
            prepare(18, x[:, 0, :])
            vec_pair(None, x[:, 1, :])
            with v.Fori(1, TILES - 1) as i:
                enter("B", i, 1)
                vec_pair(tile_of_x(i - 1), tile_of_x(i + 1))
            leave("B", TILES - 2, 1)
            vec_pair(x[:, TILES - 2, :], None)
            end_batch(1)
            for g in range(16):
                finish(g, x[:, TILES - 1, :])
            v.wait_ge(s.x_done, XDONE_B)

            for k in ("rstd", "logits", "step"):
                T[k].rate = 0
            with v.Fori(0, TILES) as i:
                enter("M", i)
                layer_norm(x[:, bass.ds(i, 1), :].rearrange("p a n -> p (a n)")).then_inc(s.xn_ready, 1)
                v.wait_ge(s.logits_ps, T["logits"].up())
                v.tensor_copy(logits[:, bass.ds(i, 1), :].rearrange("p a e -> p (a e)"), bank(2, EXPERTS)).then_inc(s.logits_sb, 1)
            leave("M", TILES)
            v.wait_ge(s.logits_sb, TILES)

            def rows16(at):
                return small[:, at:at + TILES]

            def wide(a):
                return a[:, :, None].broadcast_to([P, TILES, EXPERTS])

            ranks = rank[:, None, :].broadcast_to([P, TILES, EXPERTS])
            v.tensor_reduce(rows16(0), logits, AX, ALU.max).then_inc(s.vec_step, 1)
            v.wait_ge(s.vec_step, own())
            v.tensor_tensor(logits, logits, wide(rows16(0)), ALU.subtract).then_inc(s.rexp_in, 1)
            v.wait_ge(s.rexp_out, 1)

            def first_of_largest(p, largest, hot):
                v.tensor_reduce(largest, p, AX, ALU.max).then_inc(s.vec_step, 1)
                v.wait_ge(s.vec_step, own())
                v.tensor_tensor(rc, p, wide(largest), ALU.is_equal).then_inc(s.vec_step, 1)
                v.wait_ge(s.vec_step, own())
                v.tensor_tensor(rc, rc, ranks, ALU.mult).then_inc(s.vec_step, 1)
                v.wait_ge(s.vec_step, own())
                v.tensor_reduce(rows16(32), rc, AX, ALU.max).then_inc(s.vec_step, 1)
                v.wait_ge(s.vec_step, own())
                v.tensor_tensor(hot, rc, wide(rows16(32)), ALU.is_equal).then_inc(s.vec_step, 1)
                v.wait_ge(s.vec_step, own())

            first_of_largest(rp, rows16(0), ro1)
            v.scalar_tensor_tensor(rp, ro1, -4.0, rp, ALU.mult, ALU.add).then_inc(s.vec_step, 1)
            v.wait_ge(s.vec_step, own())
            first_of_largest(rp, rows16(16), ro2)
            v.tensor_tensor(rows16(32), rows16(0), rows16(16), ALU.add).then_inc(s.vec_step, 1)
            v.wait_ge(s.vec_step, own())
            v.reciprocal(rows16(48), rows16(32)).then_inc(s.vec_step, 1)
            v.wait_ge(s.vec_step, own())
            v.tensor_tensor(rc, ro1, wide(rows16(0)), ALU.mult).then_inc(s.vec_step, 1)
            v.tensor_tensor(rp, ro2, wide(rows16(16)), ALU.mult).then_inc(s.vec_step, 1)
            v.tensor_tensor(ro1, ro1, ro2, ALU.add).then_inc(s.vec_step, 1)
            v.wait_ge(s.vec_step, T["step"].up(3))
            v.tensor_tensor(rc, rc, rp, ALU.add).then_inc(s.vec_step, 1)
            v.wait_ge(s.vec_step, own())
            v.tensor_tensor(rc, rc, wide(rows16(48)), ALU.mult).then_inc(s.vec_step, 1)
            v.wait_ge(s.vec_step, own())
            v.tensor_reduce(rsmall[:, 0:EXPERTS], rc.rearrange("p t e -> p e t"), AX, ALU.add).then_inc(s.vec_step, 1)
            v.tensor_reduce(rsmall[:, EXPERTS:2 * EXPERTS], ro1.rearrange("p t e -> p e t"), AX, ALU.add).then_inc(s.vec_step, 1)
            v.wait_ge(s.vec_step, T["step"].up(2))
            v.tensor_copy(rsmall[:, 40:56], rsmall[:, 0:16]).then_inc(s.rsum_ready, 1)
            v.wait_ge(s.rsum_ps, 1)
            v.tensor_scalar(rsmall[:, 16:24], bank(3, EXPERTS, at=EXPERTS), 1.0, None, ALU.max).then_inc(s.vec_step, 1)
            v.wait_ge(s.vec_step, own())
            v.reciprocal(rsmall[:, 24:32], rsmall[:, 16:24]).then_inc(s.vec_step, 1)
            v.wait_ge(s.vec_step, own())
            v.tensor_tensor(rsmall[:, 32:40], bank(3, EXPERTS), rsmall[:, 24:32], ALU.mult).then_inc(s.vec_step, 1)
            v.wait_ge(s.vec_step, own())
            v.tensor_tensor(gates[:, :, :], ro1, rsmall[:, None, 32:40].broadcast_to([P, TILES, EXPERTS]), ALU.mult).then_inc(s.gates_ready, 1)
            v.wait_ge(s.gates_ready, 1)

            wide_n = CHUNKS * HT
            with v.Fori(0, EXPERTS // 2) as i:
                for n in range(2):
                    for c in range(CHUNKS):
                        for j in range(HT):
                            at = (n * CHUNKS + c) * HT + j
                            if j == 0 and at:
                                v.wait_ge(s.eo_ps, i * (2 * CHUNKS * TPC) + (n * CHUNKS + c) * TPC)
                            v.wait_ge(s.silu_g_ready, i * (2 * wide_n) + at + 1)
                            v.wait_ge(s.u_ps, i * (2 * wide_n) + at + 1)
                            v.tensor_tensor(hM[:, j, :], bank(2 + j % 2), silu_g[j % 2], ALU.mult).then_inc(s.hM_ready, 1)
                        for k in range(TPC):
                            tile = (n * CHUNKS + c) * TPC + k
                            v.wait_ge(s.eo_ps, i * (2 * CHUNKS * TPC) + tile + 1)
                            xk = x[:, c * TPC + k, :]
                            v.scalar_tensor_tensor(xk, bank(4 + k % 2, D), gates[:, c * TPC + k, bass.ds(2 * i + n, 1)], xk,
                                                   ALU.mult, ALU.add).then_inc(s.eo_added, 1)


def kernel(**inputs):
    import numpy as np
    import concourse.bacc as bacc
    from concourse import mybir as mb
    from concourse.bass_utils import run_bass_kernel_spmd

    a = {k: np.asarray(v) for k, v in inputs.items()}

    def rows(m):
        return np.ascontiguousarray(m.reshape(-1, P, m.shape[-1]).transpose(1, 0, 2))

    def by_head(m):
        out = np.zeros((P, KT, P), m.dtype)
        for h in range(HEADS):
            r = (h % HPT) * HD
            out[r:r + HD, h // HPT, r:r + HD] = m[h]
        return out

    ctx = a["ctx_1024"]
    ctxT = np.zeros((B, P, KT, NKP), ctx.dtype)
    ctxT[:, :, :, :NK] = ctx.transpose(0, 2, 1).reshape(B, KT, P, NK).transpose(0, 2, 1, 3)
    ctxN = np.zeros((B, KEY_TILES * P, D), ctx.dtype)
    ctxN[:, :NK] = ctx
    ctxN = ctxN.reshape(B, KEY_TILES, P, D).transpose(0, 2, 1, 3)
    wkv = a["L1_xattn_W_kv"]
    ffn = [rows(a["L1_ffn_gate_w"][e].T).reshape(P, -1) for e in range(EXPERTS)], \
          [rows(a["L1_ffn_up_w"][e].T).reshape(P, -1) for e in range(EXPERTS)], \
          [rows(a["L1_ffn_down_w"][e].T).reshape(P, -1) for e in range(EXPERTS)]
    wo = a["L1_attn_W_O"].reshape(4, 64, D).transpose(1, 0, 2)
    arrays = {
        "x": a["x"].reshape(TILES, P, D).transpose(1, 0, 2),
        "ctxT": ctxT.reshape(B, P, KT * NKP),
        "ctxN": ctxN.reshape(B, P, KEY_TILES * D),
        "w_xqT": rows(a["L0_xattn_Wq"].T), "w_xkT": rows(a["L0_xattn_Wk"].T), "w_xv": rows(a["L0_xattn_Wv"]),
        "w_sq": rows(a["L0_attn_Wq"]), "w_sk": rows(a["L0_attn_Wk"]), "w_sv": rows(a["L0_attn_Wv"]),
        "w1T": rows(a["L0_ffn_w1"].T).reshape(P, -1), "w2T": rows(a["L0_ffn_w2"].T).reshape(P, -1),
        "conv_w": rows(a["L0_ffn_conv_w"].reshape(HID, 3)), "conv_b": a["L0_ffn_conv_b"].reshape(HT, P).T,
        "w_ck": rows(wkv[:, :D]), "w_cv": rows(wkv[:, D:]), "w_cq": rows(a["L1_xattn_W_q"]), "w_cp": rows(a["L1_xattn_W_proj"]),
        "b_p": np.broadcast_to(a["L1_xattn_b_proj"], (P, D)),
        "w_hq": by_head(a["L1_attn_Wq"]), "w_hk": by_head(a["L1_attn_Wk"]), "w_hv": by_head(a["L1_attn_Wv"]),
        "w_o": np.concatenate([wo, wo]),
        "w_router": rows(a["L1_ffn_router_w"].T),
        "experts": np.stack([np.concatenate(three, axis=1) for three in zip(*ffn)]),
    }
    nc = bacc.Bacc("TRN2", target_bir_lowering=False, num_devices=1)
    fed, io = {}, {}
    for name, m in arrays.items():
        fed[f"in_{name}"] = np.ascontiguousarray(m)
        io[name] = nc.dram_tensor(f"in_{name}", m.shape, mb.dt.from_np(m.dtype), kind="ExternalInput").ap()
    out = nc.dram_tensor("out", (P, TILES, D), F32, kind="ExternalOutput").ap()
    build(nc, io, out)
    got = run_bass_kernel_spmd(nc, [fed], core_ids=[0]).results[0]["out"]
    return np.ascontiguousarray(got.transpose(1, 0, 2)).reshape(B, S, D)
```

```python
from contextlib import ExitStack

import concourse.bass as bass
from concourse import mybir

ALU = mybir.AluOpType
ACT = mybir.ActivationFunctionType
F32 = mybir.dt.float32
F32R = mybir.dt.float32r
BF16 = mybir.dt.bfloat16
AX = mybir.AxisListType.X

P = 128
B, S, D = 32, 64, 256
NK = 1601
NKP = NK + 1
TILES = B * S // P
KT = D // P
KEY_TILES = -(-NK // P)
LAST_KEYS = NK - (KEY_TILES - 1) * P
HEADS, HD = 16, 16
PAIRS = HEADS // 2
HPT = P // HD
HID = 1024
HT = HID // P
EXPERTS = 8
CHUNK = 512
CHUNKS = B * S // CHUNK
TPC = CHUNK // P
BPC = CHUNK // S
UJ = HT // 2
UW = 2 * KT * UJ * P + UJ * D
STEPS = 2 * CHUNKS
EPS = 1e-5
MASKED = -1e30
MAGIC = 12582912.0
KEY_CHUNKS = [(c, min(512, NK - c)) for c in range(0, NK, 512)]
HALF = NKP // 2 + NKP // 2 % 2
MAX_CHUNKS = [(0, 512), (512, HALF - 512), (HALF, 512), (HALF + 512, NKP - HALF - 512)]
PROJ_CHUNKS = [(0, HALF - 400), (HALF - 400, 400), (HALF, 400), (HALF + 400, NKP - HALF - 400)]
CTX_PARTS = 2
MAX_UNITS = 2 * PAIRS
K_PIECES = [("k", o, c) for o in range(KT) for c in range(len(PROJ_CHUNKS))]
V_PIECES = [("v", t, min(t + 2, KEY_TILES)) for t in range(0, KEY_TILES, 2)]
PIECES = K_PIECES + V_PIECES
PIECE_AFTER = (0, 2, 3, 4, 5, 7, 9, 10, 12, 13, 15)
CTX_STEPS = (1, 2, 6, 7)
PROBS = 3
QUARTERS = 4
HPQ = HEADS // QUARTERS

WEIGHTS = dict(sq=64, sk=64, sv=D, cq=D, cp=D, hq=P, hk=P, hv=P, router=EXPERTS)

A_WEIGHTS = ("sq", "sk", "sv")


def keys_of(t):
    return P if t < KEY_TILES - 1 else LAST_KEYS


class Tally:

    def __init__(self, **per):
        self.base, self.done, self.trip, self.per = 0, 0, None, per
        self.rate = 0

    def up(self, n=1):
        self.done += n
        return self.now()

    def now(self, less=0):
        fixed = self.base + self.done - less
        return fixed if self.trip is None else self.trip * self.rate + fixed

    def enter(self, phase, trip, first=0):
        self.rate = self.per.get(phase, 0)
        self.base, self.done, self.trip = self.base + self.done - first * self.rate, 0, trip

    def leave(self, phase, trips, first=0):
        assert self.done == self.rate, (phase, self.done, self.rate)
        self.base, self.done, self.trip = self.base + (first + trips) * self.rate, 0, None


def build(nc, io, out):
    ctx = ExitStack()
    with ctx:
        def sb(name, shape, dt=F32):
            return ctx.enter_context(nc.sbuf_tensor(name, shape, dt))

        def sem(name):
            return ctx.enter_context(nc.semaphore(name))

        x = sb("x", [P, TILES, D])
        ident = sb("ident", [P, P])
        ones = sb("ones", [P, P])
        neghalf = sb("neghalf", [P, 1])
        eps = sb("eps", [P, 1])
        carrier_g = sb("carrier_g", [P, HT])
        carrier_v = sb("carrier_v", [P, 1])
        rank = sb("rank", [P, EXPERTS])
        gates = sb("gates", [P, TILES, EXPERTS])
        xn = sb("xn", [P, D])
        xnT = sb("xnT", [P, KT, P])
        w = {n: sb("w_" + n, [P, KT, width]) for n, width in WEIGHTS.items() if n not in A_WEIGHTS}
        stat = sb("stat", [P, 6])
        mv = sb("mv", [P, 2])
        rstd = sb("rstd", [P, 2])
        small = sb("small", [P, 96])
        onesb = sb("onesb", [P, P], BF16)
        head_of = sb("head_of", [P, HPT])
        parity = sb("parity", [P, 2])
        causal = sb("causal", [P, P])
        cat = sb("cat", [P, D])
        attn_ch = sb("attn_ch", [P, KT, P])
        shift = sb("shift", [P, HEADS * S], BF16)
        m8 = sb("m8", [P, 40])
        wo = sb("wo", [P, 4, D])
        bias_p = sb("bias_p", [P, D])

        def scope():
            held = ExitStack()
            return held, lambda name, shape, dt=F32: held.enter_context(nc.sbuf_tensor(name, shape, dt))

        phase_m, sb_m = scope()
        unit_raw = [sb_m(f"unit_raw{n}", [P, UW]) for n in range(2)]
        unit_hi = [sb_m(f"unit_hi{n}", [P, UW], F32R) for n in range(2)]
        unit_lo = [sb_m(f"unit_lo{n}", [P, UW], F32R) for n in range(2)]
        xT_hi = sb_m("xT_hi", [P, KT, B * S], F32R)
        xT_lo = sb_m("xT_lo", [P, KT, B * S], F32R)
        h_hi = [sb_m(f"h_hi{n}", [P, UJ, CHUNK], F32R) for n in range(2)]
        h_lo = [sb_m(f"h_lo{n}", [P, UJ, CHUNK], F32R) for n in range(2)]
        hidden = [sb_m(f"hidden{n}", [P, CHUNK]) for n in range(2)]
        silu_g = [sb_m(f"silu_g{n}", [P, CHUNK]) for n in range(2)]
        rt = sb_m("rt", [P, 5 * TILES * EXPERTS])
        rsmall = sb_m("rsmall", [P, 56])
        moments_m = sb_m("moments_m", [P, TILES, 6])
        mv_m = sb_m("mv_m", [P, TILES, 2])
        rstd_m = sb_m("rstd_m", [P, 2, TILES])
        xn_m = [sb_m(f"xn_m{n}", [P, D]) for n in range(TPC)]
        xnT_m = [sb_m(f"xnT_m{n}", [P, KT, P]) for n in range(TPC)]
        phase_m.close()
        phase_b, sb_b = scope()
        ctx_raw = sb_b("ctx_raw", [P, NKP])
        ctx_hi = sb_b("ctx_hi", [P, KT, NKP], F32R)
        ctx_lo = sb_b("ctx_lo", [P, KT, NKP], F32R)
        vals = sb_b("vals", [P, 2, KEY_TILES, D])
        k_hi = sb_b("k_hi", [P, 2, KT, NKP], F32R)
        k_lo = sb_b("k_lo", [P, 2, KT, NKP], F32R)
        probs = sb_b("probs", [P, PROBS, HEADS * S])
        probs_sum = sb_b("probs_sum", [P, HEADS * S])
        qbd_hi = sb_b("qbd_hi", [P, 2, KT, HPT * S], F32R)
        qbd_lo = sb_b("qbd_lo", [P, 2, KT, HPT * S], F32R)
        q_hi = sb_b("q_hi", [P, KT, P], F32R)
        q_lo = sb_b("q_lo", [P, KT, P])
        wkv_hi = sb_b("wkv_hi", [P, KT, 2 * D], F32R)
        wkv_lo = sb_b("wkv_lo", [P, KT, 2 * D], F32R)
        sideB = sb_b("sideB", [P, 3584])
        mpart = sb_b("mpart", [P, PAIRS, 2])
        sh8 = sb_b("sh8", [40, 2, P], BF16)
        weighed_sb = sb_b("weighed", [P, D])
        phase_b.close()
        ctxT = sb("ctxT", [P, 2, KT * NKP])
        ctxN = sb("ctxN", [P, 2, KEY_TILES, D])
        work = sb("work", [P, 2, KT * NKP])
        hq_buf = sb("hq_buf", [P, 2048])
        identb = sb("identb", [P, P], BF16)
        big = sb("big", [P, 4096])
        w_a = {n: sb("w_" + n, [P, KT, width]) for n, width in WEIGHTS.items() if n in A_WEIGHTS}
        w.update(w_a)
        fold = sb("fold", [P, KT, D])
        vout = sb("vout", [P, KT, D])
        convw = sb("convw", [P, HT, 3])
        convb = sb("convb", [P, HT])
        w1q = sb("w1q", [P, KT, HID], BF16)
        w2q = sb("w2q", [P, HT, D], BF16)
        stat_s = sb("stat_s", [P, 6])
        mv_s = sb("mv_s", [P, 2])
        rstd_s = sb("rstd_s", [P, 2])
        moments_f = sb("moments_f", [P, TPC, 6])
        mv_f = sb("mv_f", [P, TPC, 2])
        rstd_f = sb("rstd_f", [P, 2, TPC])
        PS = ctx.enter_context(nc.psum_tensor("PS", [P, 8 * 512], F32))

        def bank(n, width=512, rows=slice(0, P), at=0):
            return PS[rows, 512 * n + at:512 * n + at + width]

        ctxTv = ctxT[:, :, :].rearrange("p b (k n) -> p b k n", k=KT)
        ctxNf = ctxN[:, :, :, :].rearrange("p b t n -> p (b t n)")
        probsA = big[:, 0:NK]
        probsAT = big[:, 1664:1664 + KEY_TILES * P].rearrange("p (t q) -> p t q", q=P)
        qkT = big[:, 3328:3584].rearrange("p (k t) -> p k t", k=KT)
        att = cat[:, :]
        attT = attn_ch
        xs = big[:, 3584:3840]
        xsT = big[:, 3840:4096].rearrange("p (k t) -> p k t", k=KT)
        qk_s = work[0:64, 0, 0:256]
        v_s = work[:, 0, 256:512]
        s_s = work[:, 0, 512:640]
        p_s = work[:, 0, 640:768]
        pT_s = work[:, 0, 768:896]
        hs = ctxNf[:, 0:HT * CHUNK].rearrange("p (j t) -> p j t", j=HT)
        hq = hq_buf[:, :].bitcast(BF16).rearrange("p (j t) -> p j t", j=HT)
        xq = [big[:, 2176 + 128 * n:2304 + 128 * n].bitcast(BF16) for n in range(TPC)]
        xn_f = [big[:, 2688 + 256 * n:2944 + 256 * n] for n in range(TPC)]
        xqT = big[:, 128:640].bitcast(BF16).rearrange("p (k t) -> p k t", k=KT)
        diag = big[:, 640:1152].rearrange("p (k t) -> p k t", k=TPC)
        rowscale = big[:, 1152:1664]
        hpad = [work[:, 0, 600 * n:600 * n + BPC * (S + 2)].rearrange("p (b t) -> p b t", b=BPC) for n in range(3)]
        hacc = [work[:, 1, 512 * n:512 * n + 512] for n in range(2)]
        hmax = big[:, 1664:2176]
        qT = sideB[:, 0:256].rearrange("p (k t) -> p k t", k=KT)
        sqT = sideB[:, 256:512].rearrange("p (k t) -> p k t", k=KT)
        skT = sideB[:, 512:768].rearrange("p (k t) -> p k t", k=KT)
        s4 = [sideB[:, 768 + 512 * n:1280 + 512 * n].rearrange("p (h t) -> p h t", h=HPQ) for n in range(2)]
        skbd = [sideB[:, 1792 + 512 * n:2304 + 512 * n].rearrange("p (h t) -> p h t", h=HPQ) for n in range(2)]
        v4 = sideB[:, 2816:3072]
        p4T = sideB[:, 3072:3584].rearrange("p (h t) -> p h t", h=HPQ)
        k_raw = [sideB[:, 768 + 512 * n:1280 + 512 * n] for n in range(2)]
        wkv_raw = probs[:, 0, :]
        s4_max = small[:, 40:44]
        s4_nmax = [small[:, 44 + 4 * n:48 + 4 * n] for n in range(2)]
        s4_sum = [small[:, 52 + 4 * n:56 + 4 * n] for n in range(2)]
        s4_inv = [small[:, 60 + 4 * n:64 + 4 * n] for n in range(2)]
        logits, rp, ro1, ro2, rc = (rt[:, P * n:P * n + P].rearrange("p (t e) -> p t e", e=EXPERTS) for n in range(5))

        def unit_parts(m):
            gate, up = (m[:, KT * UJ * P * n:KT * UJ * P * (n + 1)].rearrange("p (k h) -> p k h", k=KT) for n in range(2))
            return gate, up, m[:, 2 * KT * UJ * P:UW].rearrange("p (j n) -> p j n", j=UJ)

        S_ = {n: sem(n) for n in """
            first_in weights_in consts_ready ctxT_in ctxN_in ctxB_in wkv_in unit0_in unit1_in out_stored
            vec_step pool_step ln_var ln_rstd xn_ready xn_ps xnT_ready xs_ready xs_ps xsT_ready
            fold_ps fold_ready tern_sum tern_ps
            qk_ps qk_ready scores_ps nmax_ready probsA_ready pT_ps pT_ready av_ps att_ready attT_ps attT_ready outA_ps x_done
            qkv_ps qkv_ready ss_ps snmax_ready sp_ready spT_ps spT_ready so_ps
            xq_ready xqT_ps xqT_ready diag_ready rows_ps rows_ready h_ps h_scaled conv_mid conv_done silu_done odd_scaled
            hmax_ready hmaxT_ps hq_ready o_ps
            wkv_hi_ready wkv_lo_ready ctx_hi_ready ctx_lo_ready proj_ps k_raw_ready k_hi_ready k_lo_ready v_ready mx_ps mx_red m8_ready m8T_ps shift_ready
            qB_ps qB_ready q_hi_ready q_lo_ready qbd_hi_ready qbd_lo_ready sc_ps pr_ready pv_done sum_done den_ps attn_ready
            po_ps sqkv_ps sqkv_ready skbd_ready s4_ps s4_masked p4_ready p4T_ps p4T_ready o4_ps cat_ready wo_ps
            xT_all xT_lo_all logits_ps logits_sb gates_ready rexp_in rexp_out rsum_ready rsum_ps
            unit_hi_ready unit_lo_ready g_ps u_ps silu_g_ready hidden_ready h_hi_ready h_lo_ready eo_ps eo_added
            """.split()}
        s = type("Sems", (), S_)

        block = ctx.enter_context(nc.Block())
        NCONST = 22

        raw = ctxNf
        wqT_raw, wkT_raw, wv_raw = (raw[:, 512 * n:512 * n + 512].rearrange("p (k n) -> p k n", k=KT) for n in range(3))
        w1_raw = work[:, 0, 0:KT * HID]
        w2_raw = work[:, 1, 0:HT * D]
        first_loads = [
            (wqT_raw, io["w_xqT"]), (wkT_raw, io["w_xkT"]), (wv_raw, io["w_xv"]),
            (x[:, :, :], io["x"]), (w1_raw, io["w1T"]), (w2_raw, io["w2T"])]
        loads = [(w[n][:, :, :], io["w_" + n]) for n in WEIGHTS] + [
            (wo[:, :, :], io["w_o"]), (bias_p[:, :], io["b_p"]), (convw[:, :, :], io["conv_w"]), (convb[:, :], io["conv_b"])]
        FIRST_IN = 16 * len(first_loads)
        WEIGHTS_IN = 16 * len(loads)
        XDONE_A = 2 * TILES
        XDONE_F = XDONE_A + TILES
        XDONE_B = XDONE_F + 3 * TILES
        XNT_READY_B = 3 * TILES

        @block.sync
        def _(sp):
            for dst, src in first_loads:
                sp.dma_start(dst, src).then_inc(s.first_in, 16)

            def pair_of(src, i):
                return src[bass.ds(2 * i, 2), :, :].rearrange("b p n -> p b n")

            sp.dma_start(ctxT[:, :, :], pair_of(io["ctxT"], 0)).then_inc(s.ctxT_in, 16)
            for dst, src in loads:
                sp.dma_start(dst, src).then_inc(s.weights_in, 16)
            sp.wait_ge(s.fold_ps, 2)
            nkeys = ctxN[:, :, :, :].rearrange("p b t n -> p b (t n)")
            sp.dma_start(nkeys, pair_of(io["ctxN"], 0)).then_inc(s.ctxN_in, 16)
            with sp.Fori(1, TILES) as i:
                sp.wait_ge(s.scores_ps, i)
                sp.dma_start(ctxT[:, :, :], pair_of(io["ctxT"], i)).then_inc(s.ctxT_in, 16)
                sp.wait_ge(s.av_ps, i)
                sp.dma_start(nkeys, pair_of(io["ctxN"], i)).then_inc(s.ctxN_in, 16)
            sp.wait_ge(s.scores_ps, TILES)
            for a in range(KT):
                if a:
                    sp.wait_ge(s.ctx_lo_ready, a * CTX_PARTS)
                sp.dma_start(ctx_raw[:, :], io["ctxT"][0, :, a * NKP:(a + 1) * NKP]).then_inc(s.ctxB_in, 16)
                if not a:
                    sp.wait_ge(s.x_done, XDONE_F)
                    sp.dma_start(wkv_raw, io["w_kv"]).then_inc(s.wkv_in, 16)
            with sp.Fori(1, B) as n:
                for a in range(KT):
                    sp.wait_ge(s.ctx_lo_ready, n * (KT * CTX_PARTS) + a * CTX_PARTS)
                    sp.dma_start(ctx_raw[:, :], io["ctxT"][bass.ds(n, 1), :, a * NKP:(a + 1) * NKP].rearrange("b p n -> (b p) n"))\
                      .then_inc(s.ctxB_in, 16)
            sp.wait_ge(s.proj_ps, B * len(PIECES))
            sp.dma_start(unit_raw[0][:, :], io["experts"][0, :, :]).then_inc(s.unit0_in, 16)
            sp.dma_start(unit_raw[1][:, :], io["experts"][1, :, :]).then_inc(s.unit1_in, 16)
            with sp.Fori(1, EXPERTS) as e:
                for n in range(2):
                    sp.wait_ge(s.unit_lo_ready, 2 * e + (n - 1))
                    sp.dma_start(unit_raw[n][:, :], io["experts"][bass.ds(2 * e + n, 1), :, :].rearrange("e p n -> (e p) n"))\
                      .then_inc((s.unit0_in, s.unit1_in)[n], 16)
            sp.wait_ge(s.eo_added, EXPERTS * STEPS * TPC)
            sp.dma_start(out, x[:, :, :]).then_inc(s.out_stored, 16)
            sp.wait_ge(s.out_stored, 16)

        @block.gpsimd
        def _(g):
            step = Tally(A=2, F=1, B=2)
            var = Tally(A=2, F=TPC, B=2)

            g.memset(ident[:, :], 0.0).then_inc(s.consts_ready, 1)
            g.memset(ones[:, :], 1.0).then_inc(s.consts_ready, 1)
            g.memset(onesb[:, :], 1.0).then_inc(s.consts_ready, 1)
            g.memset(head_of[:, :], 1.0).then_inc(s.consts_ready, 1)
            g.memset(causal[:, :], 0.0).then_inc(s.consts_ready, 1)
            g.memset(neghalf[:, :], -0.5).then_inc(s.consts_ready, 1)
            g.memset(eps[:, :], EPS).then_inc(s.consts_ready, 1)
            g.memset(shift[:, :], 0.0).then_inc(s.consts_ready, 1)
            g.memset(m8[:, :], 0.0).then_inc(s.consts_ready, 1)
            for e in range(EXPERTS):
                g.memset(rank[:, e:e + 1], float(EXPERTS - e)).then_inc(s.consts_ready, 1)
            g.wait_ge(s.consts_ready, 17)
            g.affine_select(out=ident[:, :], in_=ident[:, :], compare_op=ALU.not_equal, fill=1.0, base=0,
                            pattern=[[-1, P]], channel_multiplier=1).then_inc(s.consts_ready, 1)
            g.affine_select(out=head_of[:, :], in_=head_of[:, :], compare_op=ALU.is_ge, fill=0.0, base=0,
                            pattern=[[-HD, HPT]], channel_multiplier=1).then_inc(s.consts_ready, 1)
            g.affine_select(out=causal[:, :], in_=causal[:, :], compare_op=ALU.is_ge, fill=MASKED, base=0,
                            pattern=[[-1, P]], channel_multiplier=1).then_inc(s.consts_ready, 1)
            g.wait_ge(s.consts_ready, 20)
            g.affine_select(out=head_of[:, :], in_=head_of[:, :], compare_op=ALU.is_ge, fill=0.0, base=HD - 1,
                            pattern=[[HD, HPT]], channel_multiplier=-1).then_inc(s.consts_ready, 1)
            g.wait_ge(s.consts_ready, 21)
            g.memset(causal[S:P, 0:S], MASKED).then_inc(s.consts_ready, 1)

            def rsqrt(mv=mv, rstd=rstd):
                g.wait_ge(s.ln_var, var.up())
                g.tensor_tensor(rstd[:, 0:1], mv[:, 1:2], eps[:, :], ALU.add).then_inc(s.pool_step, 1)
                g.wait_ge(s.pool_step, step.up())
                g.tensor_tensor(rstd[:, 1:2], rstd[:, 0:1], neghalf[:, :], ALU.pow).then_inc(s.ln_rstd, 1)

            def rsqrt_tiles(mv, rstd, tiles):
                g.wait_ge(s.ln_var, var.up(tiles))
                g.tensor_tensor(rstd[:, 0, :], mv[:, :, 1], eps[:, 0:1].broadcast_to([P, tiles]), ALU.add).then_inc(s.pool_step, 1)
                g.wait_ge(s.pool_step, step.up())
                g.tensor_tensor(rstd[:, 1, :], rstd[:, 0, :], neghalf[:, 0:1].broadcast_to([P, tiles]), ALU.pow).then_inc(s.ln_rstd, 1)

            def enter(phase, i, first=0):
                for t in (step, var):
                    t.enter(phase, i, first)

            def leave(phase, n, first=0):
                for t in (step, var):
                    t.leave(phase, n, first)

            rsqrt()
            rsqrt()
            with g.Fori(1, TILES - 1) as i:
                enter("A", i, 1)
                rsqrt(mv_s, rstd_s)
                rsqrt()
            leave("A", TILES - 2, 1)
            rsqrt(mv_s, rstd_s)
            rsqrt(mv_s, rstd_s)
            hsc = Tally(F=HT)
            rows = Tally(F=2)
            with g.Fori(0, CHUNKS) as c:
                enter("F", c)
                hsc.enter("F", c)
                rows.enter("F", c)
                rsqrt_tiles(mv_f, rstd_f, TPC)
                for j in range(HT):
                    if j >= 2:
                        g.wait_ge(s.silu_done, c * HT + j - 1)
                    g.wait_ge(s.h_scaled, hsc.up())
                    g.tensor_tensor(carrier_g[:, j:j + 1], eps[:, :], eps[:, :], ALU.add)
                    g.tensor_scalar(hacc[j % 2].rearrange("p (b t) -> p b t", b=BPC), hpad[j % 3][:, :, 1:S + 1],
                                    convw[:, j, 1:2], convb[:, j:j + 1], ALU.mult, ALU.add).then_inc(s.conv_mid, 1)
                g.wait_ge(s.rows_ready, rows.up(2))
                for j in range(1, HT, 2):
                    g.tensor_tensor(hs[:, j, :], hs[:, j, :], rowscale, ALU.mult).then_inc(s.odd_scaled, 1)
            leave("F", CHUNKS)
            qb = Tally(B=1)
            sqk = Tally(B=3)
            s4p = Tally(B=QUARTERS)
            scp = Tally(B=2 * KEY_TILES)
            ctp = Tally(B=2 * KT * CTX_PARTS)
            kp = Tally(B=2 * len(K_PIECES))
            bt = (qb, sqk, s4p, scp, ctp, kp)

            def split_keys(n):
                for p, (_, a, chunk) in enumerate(K_PIECES):
                    c, width = PROJ_CHUNKS[chunk]
                    g.wait_ge(s.k_hi_ready, kp.up())
                    g.tensor_tensor(k_lo[:, n, a, c:c + width], k_raw[p % 2][:, 0:width], k_hi[:, n, a, c:c + width].bitcast(F32),
                                    ALU.subtract).then_inc(s.k_lo_ready, 1)

            def split_ctx(part):
                a, half = divmod(part, CTX_PARTS)
                cols = slice(half * (NKP // CTX_PARTS), (half + 1) * (NKP // CTX_PARTS))
                g.wait_ge(s.ctx_hi_ready, ctp.up())
                g.tensor_tensor(ctx_lo[:, a, cols], ctx_raw[:, cols], ctx_hi[:, a, cols].bitcast(F32), ALU.subtract).then_inc(s.ctx_lo_ready, 1)

            def spread_queries(b):
                for to, part, done in ((qbd_hi, q_hi[:, :, :].bitcast(F32), s.qbd_hi_ready), (qbd_lo, q_lo[:, :, :], s.qbd_lo_ready)):
                    g.tensor_tensor(to[:, b, :, :].rearrange("p a (h q) -> p a h q", h=HPT),
                                    part[:, :, None, b * S:b * S + S].broadcast_to([P, KT, HPT, S]),
                                    head_of[:, None, :, None].broadcast_to([P, KT, HPT, S]), ALU.mult).then_inc(done, 1)

            def split_queries():
                g.wait_ge(s.q_hi_ready, qb.up())
                g.tensor_tensor(q_lo[:, :, :].rearrange("p k t -> p (k t)"), qT.rearrange("p k t -> p (k t)"),
                                q_hi[:, :, :].bitcast(F32).rearrange("p k t -> p (k t)"), ALU.subtract).then_inc(s.q_lo_ready, 1)
                g.wait_ge(s.q_lo_ready, qb.now())

            def spread_keys(q):
                a, h = divmod(q * HPQ, HPT)
                if q >= 2:
                    g.wait_ge(s.s4_ps, s4p.up())
                g.tensor_tensor(skbd[q % 2], skT[:, a, None, :].broadcast_to([P, HPQ, P]),
                                head_of[:, h:h + HPQ, None].broadcast_to([P, HPQ, P]), ALU.mult).then_inc(s.skbd_ready, 1)

            def pool_pair(first, last):
                if not first:
                    g.wait_ge(s.sc_ps, scp.now())
                spread_queries(1)
                split_keys(1)
                if not first:
                    rsqrt()
                if not last:
                    split_ctx(0)
                    split_ctx(1)
                if not first:
                    g.wait_ge(s.sqkv_ready, sqk.up(3))
                    for q in range(3):
                        spread_keys(q)
                if not last:
                    split_ctx(2)
                    split_ctx(3)
                if not first:
                    spread_keys(3)
                    s4p.up(2)
                if not last:
                    split_keys(0)
                    split_ctx(0)
                    split_ctx(1)
                    rsqrt()
                    split_ctx(2)
                    split_ctx(3)
                    split_queries()
                    g.wait_ge(s.sc_ps, scp.now() + KEY_TILES)
                    spread_queries(0)
                scp.up(2 * KEY_TILES)

            rsqrt()
            split_queries()
            spread_queries(0)
            for part in range(KT * CTX_PARTS):
                split_ctx(part)
            split_keys(0)
            for part in range(KT * CTX_PARTS):
                split_ctx(part)
            pool_pair(True, False)
            with g.Fori(1, TILES - 1) as i:
                enter("B", i, 1)
                for t in bt:
                    t.enter("B", i, 1)
                pool_pair(False, False)
            leave("B", TILES - 2, 1)
            for t in bt:
                t.leave("B", TILES - 2, 1)
            pool_pair(False, True)
            rsqrt()
            g.wait_ge(s.sqkv_ready, sqk.up(3))
            for q in range(QUARTERS):
                spread_keys(q)
            rsqrt_tiles(mv_m, rstd_m, TILES)
            xt = Tally(M=TPC)
            with g.Fori(0, CHUNKS) as c:
                xt.enter("M", c)
                for n in range(TPC):
                    g.wait_ge(s.xnT_ready, XNT_READY_B + xt.up())
                    g.tensor_copy(xT_hi[:, :, bass.ds((c * TPC + n) * P, P)], xnT_m[n][:, :, :]).then_inc(s.xT_all, 1)

            def split_unit(unit, n):
                g.wait_ge(s.unit_hi_ready, unit + 1)
                g.tensor_tensor(unit_lo[n][:, :], unit_raw[n][:, :], unit_hi[n][:, :].bitcast(F32), ALU.subtract).then_inc(s.unit_lo_ready, 1)

            def pool_expert(e, last):
                for n in range(2):
                    for c in range(CHUNKS):
                        step_of = n * CHUNKS + c
                        for j in range(UJ):
                            m = step_of * UJ + j
                            g.wait_ge(s.h_hi_ready, e * (STEPS * UJ) + m + 1)
                            g.tensor_tensor(h_lo[c % 2][:, j, :], hidden[m % 2][:, :], h_hi[c % 2][:, j, :].bitcast(F32), ALU.subtract)\
                             .then_inc(s.h_lo_ready, 1)
                        if c == 1 and not (last and n == 1):
                            split_unit(2 * e + n + 1, 1 - n)

            split_unit(0, 0)
            pool_expert(0, False)
            with g.Fori(1, EXPERTS - 1) as e:
                pool_expert(e, False)
            pool_expert(EXPERTS - 1, True)

        @block.scalar
        def _(act):
            names = dict(xn_ps=dict(A=1, B=2, M=TPC), xs_ps=dict(A=1), qk_ps=dict(A=1), nmax=dict(A=1), attT=dict(A=1), qkv=dict(A=1),
                         snmax=dict(A=1), spT=dict(A=1),
                         xqT=dict(F=TPC), rows=dict(F=2), conv=dict(F=HT),
                         proj=dict(B=2 * len(PIECES)), sc=dict(B=2 * KEY_TILES), pv=dict(B=2 * KEY_TILES),
                         qB=dict(B=1), sqkv=dict(B=1), s4=dict(B=QUARTERS), p4T=dict(B=QUARTERS), qbd=dict(B=2),
                         ctx=dict(B=2 * KT * 16), qmul=dict(B=1), k_lo=dict(B=2 * len(K_PIECES)))
            T = {k: Tally(**v) for k, v in names.items()}

            def enter(phase, i, first=0):
                for t in T.values():
                    t.enter(phase, i, first)

            def leave(phase, n, first=0):
                for t in T.values():
                    t.leave(phase, n, first)

            def copy_xnT(at=0):
                act.wait_ge(s.xn_ps, T["xn_ps"].up())
                act.copy(xnT[:, :, :].rearrange("p k t -> p (k t)"), bank(at, 256)).then_inc(s.xnT_ready, 1)

            act.wait_ge(s.consts_ready, NCONST)
            act.copy(identb[:, :], ident[:, :]).then_inc(s.consts_ready, 1)
            act.wait_ge(s.fold_ps, 1)
            act.copy(fold[:, :, :].rearrange("p k n -> p (k n)"), bank(0)).then_inc(s.fold_ready, 1)
            act.wait_ge(s.fold_ps, 2)
            act.copy(vout[:, :, :].rearrange("p k n -> p (k n)"), bank(1)).then_inc(s.fold_ready, 1)

            def copy_qkT():
                act.wait_ge(s.qk_ps, T["qk_ps"].up())
                act.copy(qkT.rearrange("p k t -> p (k t)"), bank(0, 256, at=256)).then_inc(s.qk_ready, 1)

            def copy_xsT():
                act.wait_ge(s.xs_ps, T["xs_ps"].up())
                act.copy(xsT.rearrange("p k t -> p (k t)"), bank(1, 256)).then_inc(s.xsT_ready, 1)

            def copy_qkv():
                act.wait_ge(s.qkv_ps, T["qkv"].up())
                act.copy(qk_s, bank(1, 256, slice(0, 64), 256)).then_inc(s.qkv_ready, 1)
                act.copy(v_s, bank(2, 256)).then_inc(s.qkv_ready, 1)

            def exp_s():
                act.wait_ge(s.snmax_ready, T["snmax"].up())
                act.activation(p_s, s_s, ACT.Exp, bias=small[:, 5:6], scale=1 / 8,
                               accum_out=small[:, 6:7]).then_inc(s.sp_ready, 1)

            def copy_pT_s():
                act.wait_ge(s.spT_ps, T["spT"].up())
                act.copy(pT_s, bank(1, P)).then_inc(s.spT_ready, 1)

            def act_pair_a(first, last):
                if not first:
                    copy_xsT()
                act.wait_ge(s.nmax_ready, T["nmax"].up())
                act.activation(probsA, PS[:, 2048:2048 + NK], ACT.Exp, bias=small[:, 1:2], scale=1 / 16,
                               accum_out=small[:, 2:3]).then_inc(s.probsA_ready, 1)
                if not first:
                    copy_qkv()
                    exp_s()
                if not last:
                    copy_xnT()
                if not first:
                    copy_pT_s()
                if not last:
                    copy_qkT()
                act.wait_ge(s.attT_ps, T["attT"].up())
                act.copy(attT[:, :, :].rearrange("p k t -> p (k t)"), bank(5, 256)).then_inc(s.attT_ready, 1)

            copy_xnT()
            copy_qkT()
            act_pair_a(True, False)
            with act.Fori(1, TILES - 1) as i:
                enter("A", i, 1)
                act_pair_a(False, False)
            leave("A", TILES - 2, 1)
            act_pair_a(False, True)
            copy_xsT()
            copy_qkv()
            exp_s()
            copy_pT_s()

            with act.Fori(0, CHUNKS) as c:
                enter("F", c)
                for k in range(TPC):
                    act.wait_ge(s.xqT_ps, T["xqT"].up())
                    act.copy(xqT[:, :, k * P:k * P + P], bank((0, 4)[k % 2], P).bitcast(BF16).rearrange("p (k t) -> p k t", k=KT))\
                       .then_inc(s.xqT_ready, 1)
                act.wait_ge(s.rows_ps, T["rows"].up())
                act.copy(rowscale, bank(1)).then_inc(s.rows_ready, 1)
                for j in range(HT):
                    act.wait_ge(s.conv_done, T["conv"].up())
                    act.activation(hs[:, j, :], hacc[j % 2], ACT.Silu).then_inc(s.silu_done, 1)
                act.wait_ge(s.rows_ps, T["rows"].up())
                act.copy(rowscale, bank(5)).then_inc(s.rows_ready, 1)
            leave("F", CHUNKS)

            def evac(piece, n):
                act.wait_ge(s.proj_ps, T["proj"].up())
                at = 6 - pieces_evac[0] % 2
                pieces_evac[0] += 1
                kind, a, b = piece
                if kind == "k":
                    c, width = PROJ_CHUNKS[b]
                    p = pieces_evac[0] - 1
                    if p >= 2:
                        act.wait_ge(s.k_lo_ready, T["k_lo"].now() + p - 1)
                    act.copy(k_raw[p % 2][:, 0:width], bank(at, width)).then_inc(s.k_raw_ready, 1)
                    act.copy(k_hi[:, n, a, c:c + width], bank(at, width)).then_inc(s.k_hi_ready, 1)
                elif b - a == 2:
                    act.copy(vals[:, n, a:b, :].rearrange("p t n -> p (t n)"), bank(at)).then_inc(s.v_ready, 1)
                else:
                    act.copy(vals[0:LAST_KEYS, n, a, :], bank(at, D, slice(0, LAST_KEYS))).then_inc(s.v_ready, 1)

            def round_ctx(part):
                a, half = divmod(part, CTX_PARTS)
                cols = slice(half * (NKP // CTX_PARTS), (half + 1) * (NKP // CTX_PARTS))
                if half == 0:
                    act.wait_ge(s.ctxB_in, T["ctx"].up(16))
                act.copy(ctx_hi[:, a, cols], ctx_raw[:, cols]).then_inc(s.ctx_hi_ready, 1)

            pieces_evac = [0]

            def finish(g):
                if g == 2:
                    copy_xnT(7)
                if g == 3:
                    act.wait_ge(s.sqkv_ps, T["sqkv"].up())
                    act.copy(sqT.rearrange("p k t -> p (k t)"), bank(7, 256)).then_inc(s.sqkv_ready, 1)
                    act.copy(skT.rearrange("p k t -> p (k t)"), bank(7, 256, at=256)).then_inc(s.sqkv_ready, 1)
                    act.copy(v4, bank(6, 256)).then_inc(s.sqkv_ready, 1)
                if g in (5, 7, 9, 11):
                    n = (g - 5) // 2 % 2
                    act.wait_ge(s.s4_masked, T["s4"].up())
                    for k in range(HPQ):
                        act.activation(s4[n][:, k, :], s4[n][:, k, :], ACT.Exp, bias=s4_nmax[n][:, k:k + 1], scale=HD ** -0.5,
                                       accum_out=s4_sum[n][:, k:k + 1]).then_inc(s.p4_ready, 1)
                if g in (6, 8, 10, 12):
                    act.wait_ge(s.p4T_ps, T["p4T"].up())
                    act.copy(p4T.rearrange("p h t -> p (h t)"), bank(7)).then_inc(s.p4T_ready, 1)

            def prepare(g):
                if g == 19:
                    copy_xnT(7)
                if g == 20:
                    act.wait_ge(s.qB_ps, T["qB"].up())
                    act.mul(qT.rearrange("p k t -> p (k t)"), bank(7, 256), HD ** -0.5).then_inc(s.qB_ready, 1)
                    act.wait_ge(s.qB_ready, T["qmul"].up())
                    act.copy(q_hi[:, :, :].rearrange("p k t -> p (k t)"), qT.rearrange("p k t -> p (k t)")).then_inc(s.q_hi_ready, 1)

            def act_pair(first, last):
                for b in range(2):
                    if not (last and b == 1):
                        pieces_evac[0] = 0
                        for piece in PIECES:
                            evac(piece, (b + 1) % 2)
                        T["k_lo"].up(len(K_PIECES))
                    for t in range(KEY_TILES):
                        g = b * KEY_TILES + t
                        rows = slice(0, keys_of(t))
                        act.wait_ge(s.sc_ps, T["sc"].up())
                        if t >= PROBS:
                            act.wait_ge(s.sum_done, T["pv"].now() + t - PROBS + 1)
                        act.activation(probs[rows, t % PROBS, :], PS[rows, 1024 * (t % 2):1024 * (t % 2) + 1024],
                                       ACT.Exp).then_inc(s.pr_ready, 1)
                        if not first:
                            finish(g)
                        if not last:
                            if g == 20:
                                act.wait_ge(s.qbd_lo_ready, T["qbd"].up())
                                T["qbd"].up()
                            prepare(g)
                            if t in CTX_STEPS:
                                round_ctx(CTX_STEPS.index(t))
                    T["pv"].up(KEY_TILES)

            T["qbd"].up()
            act.wait_ge(s.wkv_in, 16)
            act.copy(wkv_hi[:, :, :].rearrange("p k n -> p (k n)"), wkv_raw).then_inc(s.wkv_hi_ready, 1)
            prepare(19)
            prepare(20)
            for part in range(KT * CTX_PARTS):
                round_ctx(part)
            pieces_evac[0] = 0
            for piece in PIECES:
                evac(piece, 0)
            T["k_lo"].up(len(K_PIECES))
            for part in range(KT * CTX_PARTS):
                round_ctx(part)
            act_pair(True, False)
            with act.Fori(1, TILES - 1) as i:
                enter("B", i, 1)
                act_pair(False, False)
            leave("B", TILES - 2, 1)
            act_pair(False, True)
            for g in range(16):
                finish(g)

            with act.Fori(0, CHUNKS) as c:
                enter("M", c)
                for n in range(TPC):
                    act.wait_ge(s.xn_ps, T["xn_ps"].up())
                    act.copy(xnT_m[n][:, :, :].rearrange("p k t -> p (k t)"), bank(n, D)).then_inc(s.xnT_ready, 1)
            leave("M", CHUNKS)
            act.wait_ge(s.rexp_in, 1)
            act.activation(rp, logits, ACT.Exp).then_inc(s.rexp_out, 1)

            def round_unit(unit, n):
                act.wait_ge((s.unit0_in, s.unit1_in)[n], (unit - n) * 8 + 16)
                act.copy(unit_hi[n][:, :], unit_raw[n][:, :]).then_inc(s.unit_hi_ready, 1)

            def round_hidden(e, m):
                act.wait_ge(s.hidden_ready, e * (STEPS * UJ) + m + 1)
                act.copy(h_hi[m // UJ % 2][:, m % UJ, :], hidden[m % 2][:, :]).then_inc(s.h_hi_ready, 1)

            def act_expert(e, first, last):
                for n in range(2):
                    for c in range(CHUNKS):
                        for j in range(UJ):
                            m = (n * CHUNKS + c) * UJ + j
                            act.wait_ge(s.g_ps, e * (STEPS * UJ) + m + 1)
                            if m >= 2 or not first:
                                act.wait_ge(s.hidden_ready, e * (STEPS * UJ) + m - 1)
                            act.activation(silu_g[m % 2][:, :], bank(m % 2), ACT.Silu).then_inc(s.silu_g_ready, 1)
                            if m:
                                round_hidden(e, m - 1)
                            elif not first:
                                round_hidden(e - 1, STEPS * UJ - 1)
                        if c == 1 and not (last and n == 1):
                            if not (first and n == 0):
                                act.wait_ge(s.eo_ps, e * (STEPS * TPC) + n * (CHUNKS * TPC))
                            round_unit(2 * e + n + 1, 1 - n)

            round_unit(0, 0)
            act_expert(0, True, False)
            with act.Fori(1, EXPERTS - 1) as e:
                act_expert(e, False, False)
            act_expert(EXPERTS - 1, False, True)
            round_hidden(EXPERTS - 1, STEPS * UJ - 1)

        @block.tensor
        def _(pe):
            names = dict(xn=dict(A=1, B=2, M=TPC), xnT=dict(A=1, B=2, M=TPC), xs=dict(A=1), xsT=dict(A=1), qk=dict(A=1), probsA=dict(A=1), pT=dict(A=4),
                         att=dict(A=1), attT=dict(A=1), qkv=dict(A=2), sp=dict(A=1), spT=dict(A=1),
                         xq=dict(F=TPC), xqT=dict(F=TPC), diag=dict(F=2), h_scaled=dict(F=HT), hmax=dict(F=1), hq=dict(F=HT),
                         k_sb=dict(B=2 * len(K_PIECES)), v_sb=dict(B=2 * len(V_PIECES)), mx=dict(B=2 * MAX_UNITS), m8=dict(B=2), shift=dict(B=4),
                         qbd=dict(B=2), pr=dict(B=2 * KEY_TILES),
                         attn=dict(B=2), sqkv=dict(B=3), skbd=dict(B=QUARTERS), s4_masked=dict(B=QUARTERS), p4=dict(B=QUARTERS * HPQ), p4T=dict(B=QUARTERS),
                         cat=dict(B=QUARTERS), x_done=dict(A=2, F=TPC, B=3),
                         ctx=dict(A=16), ctxB=dict(B=2 * KT * CTX_PARTS))
            T = {k: Tally(**v) for k, v in names.items()}

            def enter(phase, i, first=0):
                for t in T.values():
                    t.enter(phase, i, first)

            def leave(phase, n, first=0):
                for t in T.values():
                    t.leave(phase, n, first)

            pe.wait_ge(s.first_in, FIRST_IN)
            pe.wait_ge(s.consts_ready, NCONST + 1)
            for o in range(KT):
                for k in range(KT):
                    mm = pe.matmul(bank(0, D, at=o * D), wqT_raw[:, k, o * P:o * P + P], wkT_raw[:, k, :], start=k == 0, stop=k == KT - 1)
            mm.then_inc(s.fold_ps, 1)
            for o in range(KT):
                for k in range(KT):
                    mm = pe.matmul(bank(1, D, at=o * D), wkT_raw[:, k, o * P:o * P + P], wv_raw[:, k, :], start=k == 0, stop=k == KT - 1)
            mm.then_inc(s.fold_ps, 1)
            pe.wait_ge(s.fold_ready, 2)

            def transpose_xn(to=0):
                pe.wait_ge(s.xn_ready, T["xn"].up())
                for k in range(KT):
                    mm = pe.transpose(bank(to, P, at=k * P), xn[:, k * P:k * P + P], ident[:, :])
                mm.then_inc(s.xn_ps, 1)

            def queries_a():
                pe.wait_ge(s.xnT_ready, T["xnT"].up())
                for o in range(KT):
                    for k in range(KT):
                        mm = pe.matmul(bank(0, P, at=256 + o * P), fold[:, k, o * P:o * P + P], xnT[:, k, :], start=k == 0, stop=k == KT - 1)
                mm.then_inc(s.qk_ps, 1)

            def transpose_xs():
                pe.wait_ge(s.xs_ready, T["xs"].up())
                for k in range(KT):
                    mm = pe.transpose(bank(1, P, at=k * P), xs[:, k * P:k * P + P], ident[:, :])
                mm.then_inc(s.xs_ps, 1)

            def project_s():
                pe.wait_ge(s.xsT_ready, T["xsT"].up())
                for n, m in enumerate(("sq", "sk")):
                    for k in range(KT):
                        pe.matmul(bank(1, P, slice(0, 64), 256 + n * P), w[m][:, k, :], xsT[:, k, :], start=k == 0, stop=k == KT - 1)
                for k in range(KT):
                    mm = pe.matmul(bank(2, D), xsT[:, k, :], w["sv"][:, k, :], start=k == 0, stop=k == KT - 1)
                mm.then_inc(s.qkv_ps, 1)

            def scores_s():
                pe.wait_ge(s.qkv_ready, T["qkv"].up(2))
                pe.matmul(bank(3, P), qk_s[:, 0:P], qk_s[:, P:2 * P], start=True, stop=True).then_inc(s.ss_ps, 1)

            def transpose_p_s():
                pe.wait_ge(s.sp_ready, T["sp"].up())
                pe.transpose(bank(1, P), p_s, ident[:, :]).then_inc(s.spT_ps, 1)

            def weigh_s():
                pe.wait_ge(s.spT_ready, T["spT"].up())
                pe.matmul(bank(2, D, at=256), pT_s, v_s, start=True, stop=True).then_inc(s.so_ps, 1)
                T["x_done"].up()

            def pe_pair_a(first, last):
                pe.wait_ge(s.qk_ready, T["qk"].up())
                pe.wait_ge(s.ctxT_in, T["ctx"].up(16))
                for n, (c, width) in enumerate(KEY_CHUNKS):
                    for k in range(KT):
                        for b in range(2):
                            mm = pe.matmul(bank(4 + n, width, slice(b * S, b * S + S)), qkT[:, k, b * S:b * S + S],
                                           ctxTv[:, b, k, c:c + width], start=k == 0, stop=k == KT - 1)
                mm.then_inc(s.scores_ps, 1)
                if not first:
                    transpose_xs()
                    project_s()
                pe.wait_ge(s.probsA_ready, T["probsA"].up())
                for t in range(KEY_TILES):
                    to = (5, 6, 7, 0)[t // 4]
                    mm = pe.transpose(bank(to, P, slice(0, keys_of(t)), (t % 4) * P), probsA[:, t * P:t * P + keys_of(t)], ident[:, :])
                    if t % 4 == 3 or t == KEY_TILES - 1:
                        mm.then_inc(s.pT_ps, 1)
                if not first:
                    scores_s()
                pe.wait_ge(s.ctxN_in, T["ctx"].now())
                for t in range(KEY_TILES):
                    if t % 4 == 0:
                        pe.wait_ge(s.pT_ready, T["pT"].up())
                    rows = slice(0, keys_of(t))
                    for b in range(2):
                        mm = pe.matmul(bank(4, D, slice(b * S, b * S + S)), probsAT[rows, t, b * S:b * S + S], ctxN[rows, b, t, :],
                                       start=t == 0, stop=t == KEY_TILES - 1)
                mm.then_inc(s.av_ps, 1)
                if not last:
                    transpose_xn()
                if not first:
                    transpose_p_s()
                if not last:
                    queries_a()
                pe.wait_ge(s.att_ready, T["att"].up())
                for k in range(KT):
                    mm = pe.transpose(bank(5, P, at=k * P), att[:, k * P:k * P + P], ident[:, :])
                mm.then_inc(s.attT_ps, 1)
                if not first:
                    weigh_s()
                pe.wait_ge(s.attT_ready, T["attT"].up())
                for k in range(KT):
                    mm = pe.matmul(bank(3, D, at=256), attT[:, k, :], vout[:, k, :], start=k == 0, stop=k == KT - 1)
                mm.then_inc(s.outA_ps, 1)
                T["x_done"].up()

            transpose_xn()
            queries_a()
            pe.wait_ge(s.tern_sum, 1)
            pe.matmul(bank(2, 2), ones[:, :], small[:, 86:88], start=True, stop=True).then_inc(s.tern_ps, 1)
            pe_pair_a(True, False)
            pe.wait_ge(s.weights_in, WEIGHTS_IN)
            with pe.Fori(1, TILES - 1) as i:
                enter("A", i, 1)
                pe_pair_a(False, False)
            leave("A", TILES - 2, 1)
            pe_pair_a(False, True)
            transpose_xs()
            project_s()
            scores_s()
            transpose_p_s()
            weigh_s()

            with pe.Fori(0, CHUNKS) as c:
                enter("F", c)
                for k in range(TPC):
                    pe.wait_ge(s.xq_ready, T["xq"].up())
                    if k >= 2:
                        pe.wait_ge(s.xqT_ready, T["xqT"].up())
                    for a in range(KT):
                        mm = pe.transpose(bank((0, 4)[k % 2], P).bitcast(BF16)[:, a * P:a * P + P], xq[k][:, a * P:a * P + P], identb[:, :])
                    mm.then_inc(s.xqT_ps, 1)
                pe.wait_ge(s.diag_ready, T["diag"].up())
                for k in range(TPC):
                    mm = pe.matmul(bank(1, P, at=k * P), ones[:, :], diag[:, k, :], start=True, stop=True)
                mm.then_inc(s.rows_ps, 1)
                pe.wait_ge(s.xqT_ready, T["xqT"].up(2))
                for j in range(HT):
                    if j >= 2:
                        pe.wait_ge(s.h_scaled, T["h_scaled"].up())
                    for a in range(KT):
                        mm = pe.matmul(bank(2 + j % 2), w1q[:, a, j * P:j * P + P], xqT[:, a, :], start=a == 0, stop=a == KT - 1)
                    mm.then_inc(s.h_ps, 1)
                T["h_scaled"].up(2)
                pe.wait_ge(s.hmax_ready, T["hmax"].up())
                for k in range(TPC):
                    mm = pe.transpose(bank(4, P, at=k * P), hmax[:, k * P:k * P + P], ident[:, :])
                mm.then_inc(s.hmaxT_ps, 1)
                pe.wait_ge(s.diag_ready, T["diag"].up())
                for k in range(TPC):
                    mm = pe.matmul(bank(5, P, at=k * P), ones[:, :], diag[:, k, :], start=True, stop=True)
                mm.then_inc(s.rows_ps, 1)
                pe.wait_ge(s.hq_ready, T["hq"].up(HT))
                for k in range(TPC):
                    if k >= 2:
                        pe.wait_ge(s.x_done, T["x_done"].up())
                    for j in range(HT):
                        mm = pe.matmul(bank(6 + k % 2, D), hq[:, j, k * P:k * P + P], w2q[:, j, :], start=j == 0, stop=j == HT - 1)
                    mm.then_inc(s.o_ps, 1)
                T["x_done"].up(2)
            leave("F", CHUNKS)

            count = [0]

            def project(piece, n):
                kind, a, b = piece
                at = 6 - count[0] % 2
                count[0] += 1
                p = count[0] - 1
                if p >= 2 and p - 2 < len(K_PIECES):
                    pe.wait_ge(s.k_hi_ready, T["k_sb"].now() + p - 1)
                elif p >= 2:
                    pe.wait_ge(s.v_ready, T["v_sb"].now() + p - 1 - len(K_PIECES))
                if kind == "k":
                    c, width = PROJ_CHUNKS[b]
                    cols = slice(a * P, a * P + P)
                    for k in range(KT):
                        pe.matmul(bank(at, width), wkv_hi[:, k, cols], ctx_hi[:, k, c:c + width], start=k == 0, stop=False)
                        pe.matmul(bank(at, width), wkv_hi[:, k, cols], ctx_lo[:, k, c:c + width], start=False, stop=False)
                        mm = pe.matmul(bank(at, width), wkv_lo[:, k, cols], ctx_hi[:, k, c:c + width], start=False, stop=k == KT - 1)
                else:
                    for t in range(a, b):
                        rows = slice(0, keys_of(t))
                        keys = slice(t * P, t * P + keys_of(t))
                        to = bank(at, D, rows, (t - a) * D)
                        for k in range(KT):
                            pe.matmul(to, ctx_hi[:, k, keys], wkv_hi[:, k, D:2 * D], start=k == 0, stop=False)
                            pe.matmul(to, ctx_hi[:, k, keys], wkv_lo[:, k, D:2 * D], start=False, stop=False)
                            mm = pe.matmul(to, ctx_lo[:, k, keys], wkv_hi[:, k, D:2 * D], start=False, stop=k == KT - 1)
                mm.then_inc(s.proj_ps, 1)

            def maxima(n, u):
                pair, half = divmod(u, 2)
                if u >= 2:
                    pe.wait_ge(s.mx_red, T["mx"].now() + u - 1)
                for c, width in MAX_CHUNKS[2 * half:2 * half + 2]:
                    at = 1024 * ((u + 1) % 2) + c - HALF * half
                    at = PS[:, at:at + width]
                    mm = pe.matmul(at, qbd_hi[:, n, pair // 4, (pair % 4) * P:(pair % 4) * P + P], k_hi[:, n, pair // 4, c:c + width],
                                   start=True, stop=True)
                mm.then_inc(s.mx_ps, 1)

            def weigh(n, t):
                rows = slice(0, keys_of(t))
                pe.wait_ge(s.pr_ready, T["pr"].up())
                for g in range(KT):
                    for j in range(4):
                        mm = pe.matmul(bank(4, P, slice(32 * j, 32 * j + 32), g * P), vals[rows, n, t, g * P + 32 * j:g * P + 32 * j + 32],
                                       probs[rows, t % PROBS, (4 * g + j) * P:(4 * g + j) * P + P],
                                       start=t == 0 and g == 0, stop=t == KEY_TILES - 1, skip_group_check=True)
                mm.then_inc(s.pv_done, 1)

            def end_batch(n, fin):
                pe.wait_ge(s.sum_done, T["pr"].now())
                if n == 0 and fin:
                    pe.wait_ge(s.p4T_ready, T["p4T"].now() + 1)
                for g in range(KT):
                    for j in range(4):
                        mm = pe.matmul(bank(7, P, slice(32 * j, 32 * j + 32), g * P), ones[:, 0:32],
                                       probs_sum[:, (4 * g + j) * P:(4 * g + j) * P + P], start=g == 0, stop=True, skip_group_check=True)
                mm.then_inc(s.den_ps, 1)

            def finish(g):
                if g == 0:
                    pe.wait_ge(s.attn_ready, T["attn"].up(2))
                    for k in range(KT):
                        mm = pe.matmul(bank(7, D), attn_ch[:, k, :], w["cp"][:, k, :], start=k == 0, stop=k == KT - 1)
                    mm.then_inc(s.po_ps, 1)
                if g == 2:
                    transpose_xn(7)
                if g == 3:
                    pe.wait_ge(s.v_ready, T["v_sb"].now())
                    pe.wait_ge(s.xnT_ready, T["xnT"].up())
                    for n, m in enumerate(("hq", "hk")):
                        for a in range(KT):
                            pe.matmul(bank(7, P, at=(2 * n + a) * P), w[m][:, a, :], xnT[:, a, :], start=True, stop=True)
                    for a in range(KT):
                        mm = pe.matmul(bank(6, P, at=a * P), xnT[:, a, :], w["hv"][:, a, :], start=True, stop=True)
                    mm.then_inc(s.sqkv_ps, 1)
                if g in (4, 6, 8, 10):
                    q = (g - 4) // 2
                    if q == 0:
                        pe.wait_ge(s.k_lo_ready, T["k_sb"].now())
                        pe.wait_ge(s.sqkv_ready, T["sqkv"].up(3))
                    else:
                        pe.wait_ge(s.s4_masked, T["s4_masked"].up())
                    pe.wait_ge(s.skbd_ready, T["skbd"].up())
                    pe.matmul(bank(6), sqT[:, q // 2, :], skbd[q % 2].rearrange("p h t -> p (h t)"), start=True, stop=True)\
                      .then_inc(s.s4_ps, 1)
                if g in (6, 8, 10, 12):
                    q = (g - 6) // 2
                    pe.wait_ge(s.p4_ready, T["p4"].up(HPQ))
                    for k in range(HPQ):
                        mm = pe.transpose(bank(7, P, at=k * P), s4[q % 2][:, k, :], ident[:, :])
                    mm.then_inc(s.p4T_ps, 1)
                if g in (7, 9, 11, 13):
                    q = (g - 7) // 2
                    if q:
                        pe.wait_ge(s.cat_ready, T["cat"].up())
                    if q in (0, 3):
                        pe.wait_ge(s.v_ready, T["v_sb"].now())
                    pe.wait_ge(s.p4T_ready, T["p4T"].up())
                    for k in range(HPQ):
                        mm = pe.matmul(bank(5, HD, at=k * HD), p4T[:, k, :], v4[:, (q * HPQ + k) * HD:(q * HPQ + k + 1) * HD], start=True, stop=True)
                    mm.then_inc(s.o4_ps, 1)
                if g == 15:
                    T["s4_masked"].up()
                    pe.wait_ge(s.cat_ready, T["cat"].up())
                    pe.matmul(bank(7, 1), ones[:, :], ones[:, 0:1], start=True, stop=True)
                    catv = cat[:, :].rearrange("p (i r) -> p r i", r=4)
                    for r in range(4):
                        for b in range(2):
                            rows = slice(b * S, b * S + S)
                            mm = pe.matmul(bank(5 + b, D, rows), catv[rows, r, :], wo[rows, r, :], start=r == 0, stop=r == 3)
                    mm.then_inc(s.wo_ps, 1)
                    T["x_done"].up(3)

            def prepare(g):
                if g == 19:
                    transpose_xn(7)
                if g == 20:
                    pe.wait_ge(s.xnT_ready, T["xnT"].up())
                    for o in range(KT):
                        for k in range(KT):
                            mm = pe.matmul(bank(7, P, at=o * P), w["cq"][:, k, o * P:o * P + P], xnT[:, k, :], start=k == 0, stop=k == KT - 1)
                    mm.then_inc(s.qB_ps, 1)

            def pe_batch(n, first, last):
                ahead = not (last and n == 1)
                pieces = list(PIECES) if ahead else []
                count[0] = 0
                pe.wait_ge(s.k_lo_ready, T["k_sb"].now())
                pe.wait_ge(s.qbd_hi_ready, T["qbd"].up())
                pe.wait_ge(s.qbd_lo_ready, T["qbd"].now())
                if ahead:
                    pe.wait_ge(s.ctx_lo_ready, T["ctxB"].up(KT * CTX_PARTS))
                for u in range(MAX_UNITS):
                    maxima(n, u)
                    if not (first and n == 0):
                        if u == 0:
                            weigh(1 - n, KEY_TILES - 1)
                        if u == 2:
                            end_batch(1 - n, not first)
                    if ahead and u in PIECE_AFTER:
                        project(pieces.pop(0), 1 - n)
                T["mx"].up(MAX_UNITS)
                if ahead:
                    project(pieces.pop(0), 1 - n)
                pe.wait_ge(s.m8_ready, T["m8"].up())
                pe.matmul(bank(2, 1, at=511), ones[:, :], ones[:, 0:1], start=True, stop=True)
                pe.transpose(bank(2, P, slice(0, 40)), m8[:, :], ident[:, :]).then_inc(s.m8T_ps, 1)
                for piece in pieces:
                    project(piece, 1 - n)
                if ahead:
                    T["k_sb"].up(len(K_PIECES))
                    T["v_sb"].up(len(V_PIECES))
                pe.wait_ge(s.shift_ready, T["shift"].up(2))
                for t in range(KEY_TILES):
                    rows = slice(0, keys_of(t))
                    for a in range(KT):
                        at = bank(2 * (t % 2) + a, 512, rows)
                        pe.matmul(at, onesb[:, rows], shift[:, a * 512:a * 512 + 512], start=True, stop=False)
                        keys = slice(t * P, t * P + keys_of(t))
                        pe.matmul(at, k_hi[:, n, a, keys], qbd_hi[:, n, a, :], start=False, stop=False)
                        pe.matmul(at, k_hi[:, n, a, keys], qbd_lo[:, n, a, :], start=False, stop=False)
                        mm = pe.matmul(at, k_lo[:, n, a, keys], qbd_hi[:, n, a, :], start=False, stop=True)
                    mm.then_inc(s.sc_ps, 1)
                    if t >= 1:
                        weigh(n, t - 1)
                    if not first:
                        finish(n * KEY_TILES + t)
                    if not last:
                        prepare(n * KEY_TILES + t)

            def pe_pair(first, last):
                for n in range(2):
                    pe_batch(n, first, last)

            pe.wait_ge(s.x_done, XDONE_F)
            prepare(19)
            prepare(20)
            count[0] = 0
            pe.wait_ge(s.wkv_lo_ready, 1)
            pe.wait_ge(s.ctx_lo_ready, T["ctxB"].up(KT * CTX_PARTS))
            for piece in PIECES:
                project(piece, 0)
            T["k_sb"].up(len(K_PIECES))
            T["v_sb"].up(len(V_PIECES))
            pe_pair(True, False)
            with pe.Fori(1, TILES - 1) as i:
                enter("B", i, 1)
                pe_pair(False, False)
            leave("B", TILES - 2, 1)
            pe_pair(False, True)
            weigh(1, KEY_TILES - 1)
            end_batch(1, True)
            for g in range(16):
                finish(g)

            with pe.Fori(0, CHUNKS) as c:
                for t in ("xn", "xnT"):
                    T[t].enter("M", c)
                for n in range(TPC):
                    pe.wait_ge(s.xn_ready, T["xn"].up())
                    for k in range(KT):
                        mm = pe.transpose(bank(n, P, at=k * P), xn_m[n][:, k * P:k * P + P], ident[:, :])
                    mm.then_inc(s.xn_ps, 1)
                for n in range(TPC):
                    pe.wait_ge(s.xnT_ready, T["xnT"].up())
                    for k in range(KT):
                        mm = pe.matmul(bank(4 + n, EXPERTS), xnT_m[n][:, k, :], w["router"][:, k, :], start=k == 0, stop=k == KT - 1)
                    mm.then_inc(s.logits_ps, 1)
            pe.wait_ge(s.rsum_ready, 1)
            pe.matmul(bank(3, 2 * EXPERTS), ones[:, :], rsmall[:, 40:40 + 2 * EXPERTS], start=True, stop=True).then_inc(s.rsum_ps, 1)
            pe.wait_ge(s.xT_all, TILES)
            pe.wait_ge(s.gates_ready, 1)

            def up_and_gate(e, n, c, first):
                gate_hi, up_hi, _ = unit_parts(unit_hi[n])
                gate_lo, up_lo, _ = unit_parts(unit_lo[n])
                tokens = slice(c * CHUNK, c * CHUNK + CHUNK)
                if c == 0:
                    pe.wait_ge(s.unit_lo_ready, 2 * e + n + 1)
                for j in range(UJ):
                    m = (n * CHUNKS + c) * UJ + j
                    if m >= 2 or not first:
                        pe.wait_ge(s.hidden_ready, e * (STEPS * UJ) + m - 1)
                    for at, hi, lo, done in ((m % 2, gate_hi, gate_lo, s.g_ps), (2 + m % 2, up_hi, up_lo, s.u_ps)):
                        for k in range(KT):
                            cols = slice(j * P, j * P + P)
                            pe.matmul(bank(at), hi[:, k, cols], xT_hi[:, k, tokens], start=k == 0, stop=False)
                            pe.matmul(bank(at), hi[:, k, cols], xT_lo[:, k, tokens], start=False, stop=False)
                            mm = pe.matmul(bank(at), lo[:, k, cols], xT_hi[:, k, tokens], start=False, stop=k == KT - 1)
                        mm.then_inc(done, 1)

            def down(e, n, c, first):
                _, _, down_hi = unit_parts(unit_hi[n])
                _, _, down_lo = unit_parts(unit_lo[n])
                step = n * CHUNKS + c
                pe.wait_ge(s.h_lo_ready, e * (STEPS * UJ) + (step + 1) * UJ)
                for k in range(TPC):
                    if step or not first:
                        pe.wait_ge(s.eo_added, e * (STEPS * TPC) + (step - 1) * TPC + k + 1)
                    cols = slice(k * P, k * P + P)
                    for j in range(UJ):
                        pe.matmul(bank(4 + k, D), h_hi[c % 2][:, j, cols], down_hi[:, j, :], start=j == 0, stop=False)
                        pe.matmul(bank(4 + k, D), h_hi[c % 2][:, j, cols], down_lo[:, j, :], start=False, stop=False)
                        mm = pe.matmul(bank(4 + k, D), h_lo[c % 2][:, j, cols], down_hi[:, j, :], start=False, stop=j == UJ - 1)
                    mm.then_inc(s.eo_ps, 1)

            def pe_expert(e, first):
                for n in range(2):
                    for c in range(CHUNKS):
                        up_and_gate(e, n, c, first)
                        if n or c:
                            before = n * CHUNKS + c - 1
                            down(e, before // CHUNKS, before % CHUNKS, first)
                        elif not first:
                            down(e - 1, 1, CHUNKS - 1, False)

            pe.wait_ge(s.xT_lo_all, TILES)
            pe_expert(0, True)
            with pe.Fori(1, EXPERTS) as e:
                pe_expert(e, False)
            down(EXPERTS - 1, 1, CHUNKS - 1, False)

        @block.vector
        def _(v):
            names = dict(step=dict(A=7, F=43, B=27),
                         rstd=dict(A=2, F=1, B=2), scores=dict(A=1), pT=dict(A=4), probsA=dict(A=1), av=dict(A=1), outA=dict(A=1),
                         ss=dict(A=1), sp=dict(A=1), so=dict(A=1), x_done=dict(A=2, F=TPC, B=3),
                         rows=dict(F=2), h_ps=dict(F=HT), mid=dict(F=HT), silu=dict(F=HT), hmaxT=dict(F=1), o=dict(F=TPC), odd=dict(F=HT // 2),
                         mx=dict(B=2 * MAX_UNITS), m8T=dict(B=2), pr=dict(B=2 * KEY_TILES), den=dict(B=2),
                         po=dict(B=1), s4=dict(B=QUARTERS), p4=dict(B=QUARTERS * HPQ), p4T=dict(B=QUARTERS), o4=dict(B=QUARTERS), wo=dict(B=1),
                         logits=dict(M=TPC), xT=dict(M=TPC))
            T = {k: Tally(**q) for k, q in names.items()}

            def enter(phase, i, first=0):
                for t in T.values():
                    t.enter(phase, i, first)

            def leave(phase, n, first=0):
                for t in T.values():
                    t.leave(phase, n, first)

            def own():
                return T["step"].up()

            def layer_norm(xi):
                moments(xi)
                return normalize(xi)

            def moments(xi, stat=stat, mv=mv):
                v.bn_stats(stat[:, :], xi).then_inc(s.vec_step, 1)
                v.wait_ge(s.vec_step, own())
                v.tensor_copy(carrier_v[:, :], eps[:, :])
                v.bn_aggr(mv[:, :], stat[:, :]).then_inc(s.ln_var, 1)

            def normalize(xi, xn=xn, mv=mv, rstd=rstd):
                v.wait_ge(s.ln_rstd, T["rstd"].up())
                return v.tensor_scalar(xn[:, :], xi, mv[:, 0:1], rstd[:, 1:2], ALU.subtract, ALU.mult)

            def moments_of(tiles, to, mv):
                for k, xk in enumerate(tiles):
                    v.bn_stats(to[:, k, :], xk).then_inc(s.vec_step, 1)
                v.wait_ge(s.vec_step, T["step"].up(len(tiles)))
                v.tensor_copy(carrier_v[:, :], eps[:, :])
                for k in range(len(tiles)):
                    v.bn_aggr(mv[:, k, :], to[:, k, :]).then_inc(s.ln_var, 1)

            def diagonals(at):
                for k in range(TPC):
                    ins = v.tensor_scalar(diag[:, k, :], ident[:, :], small[:, at + k:at + k + 1], None, ALU.mult)
                    if k < TPC - 1:
                        ins.then_inc(s.vec_step, 1)
                T["step"].up(TPC - 1)
                ins.then_inc(s.diag_ready, 1)

            def side_taps(j):
                acc = hacc[j % 2].rearrange("p (b t) -> p b t", b=BPC)
                v.wait_ge(s.conv_mid, T["mid"].up())
                v.scalar_tensor_tensor(acc, hpad[j % 3][:, :, 0:S], convw[:, j, 0:1], acc, ALU.mult, ALU.add).then_inc(s.vec_step, 1)
                v.wait_ge(s.vec_step, own())
                v.scalar_tensor_tensor(acc, hpad[j % 3][:, :, 2:S + 2], convw[:, j, 2:3], acc, ALU.mult, ALU.add).then_inc(s.conv_done, 1)

            v.wait_ge(s.first_in, FIRST_IN)
            v.wait_ge(s.consts_ready, NCONST + 1)
            layer_norm(x[:, 0, :]).then_inc(s.xn_ready, 1)
            for n, r in enumerate((w1_raw, w2_raw)):
                v.tensor_reduce(small[:, 86 + n:87 + n], r, AX, ALU.add, apply_absolute_value=True).then_inc(s.vec_step, 1)
            v.wait_ge(s.vec_step, T["step"].up(2))
            v.tensor_reduce(parity[:, 0:1], head_of[:, 0::2], AX, ALU.add).then_inc(s.vec_step, 1)
            v.tensor_reduce(parity[:, 1:2], head_of[:, 1::2], AX, ALU.add).then_inc(s.tern_sum, 1)
            T["step"].up()
            v.wait_ge(s.tern_ps, 1)
            v.tensor_scalar(small[:, 80:82], bank(2, 2), 1.0 / (HID * D), 1e-5, ALU.mult, ALU.max).then_inc(s.vec_step, 1)
            v.wait_ge(s.vec_step, own())
            v.reciprocal(small[:, 82:84], small[:, 80:82]).then_inc(s.vec_step, 1)
            v.tensor_scalar(small[:, 84:86], small[:, 80:82], 1 / 127, None, ALU.mult).then_inc(s.vec_step, 1)
            v.wait_ge(s.vec_step, T["step"].up(2))
            for n, (r, q) in enumerate(((w1_raw, w1q), (w2_raw, w2q))):
                v.tensor_scalar(r, r, small[:, 82 + n:83 + n], MAGIC, ALU.mult, ALU.add).then_inc(s.vec_step, 1)
                v.wait_ge(s.vec_step, own())
                v.tensor_scalar(r, r, MAGIC, 1.0, ALU.subtract, ALU.min).then_inc(s.vec_step, 1)
                v.wait_ge(s.vec_step, own())
                v.tensor_scalar(q[:, :, :].rearrange("p a n -> p (a n)"), r, -1.0, None, ALU.max).then_inc(s.vec_step, 1)
                v.wait_ge(s.vec_step, own())

            def tile_of_x(i):
                return x[:, bass.ds(i, 1), :].rearrange("p a n -> p (a n)")

            def norm_s(xi):
                v.wait_ge(s.x_done, T["x_done"].now())
                v.tensor_copy(carrier_v[:, :], eps[:, :])
                moments(xi, stat_s, mv_s)
                normalize(xi, xs, mv_s, rstd_s).then_inc(s.xs_ready, 1)

            def mask_s():
                v.wait_ge(s.ss_ps, T["ss"].up())
                v.tensor_tensor(s_s, bank(3, P), causal[:, :], ALU.add).then_inc(s.vec_step, 1)
                v.wait_ge(s.vec_step, own())
                v.tensor_reduce(small[:, 4:5], s_s, AX, ALU.max).then_inc(s.vec_step, 1)
                v.wait_ge(s.vec_step, own())
                v.tensor_scalar(small[:, 5:6], small[:, 4:5], -1 / 8, None, ALU.mult).then_inc(s.snmax_ready, 1)

            def add_s(xi):
                v.wait_ge(s.sp_ready, T["sp"].up())
                v.reciprocal(small[:, 7:8], small[:, 6:7]).then_inc(s.vec_step, 1)
                v.wait_ge(s.vec_step, own())
                v.wait_ge(s.so_ps, T["so"].up())
                v.scalar_tensor_tensor(xi, bank(2, D, at=256), small[:, 7:8], xi, ALU.mult, ALU.add).then_inc(s.x_done, 1)
                T["x_done"].up()

            def vec_pair_a(before, xi, after):
                if before is not None:
                    norm_s(before)
                v.wait_ge(s.scores_ps, T["scores"].up())
                v.tensor_reduce(small[:, 0:1], PS[:, 2048:2048 + NK], AX, ALU.max).then_inc(s.vec_step, 1)
                v.wait_ge(s.vec_step, own())
                v.tensor_scalar(small[:, 1:2], small[:, 0:1], -1 / 16, None, ALU.mult).then_inc(s.nmax_ready, 1)
                if after is not None:
                    layer_norm(after).then_inc(s.xn_ready, 1)
                for q in range(4):
                    v.wait_ge(s.pT_ps, T["pT"].up())
                    if q < 3:
                        v.tensor_copy(probsAT[:, 4 * q:4 * q + 4, :].rearrange("p t q -> p (t q)"), bank(5 + q)).then_inc(s.pT_ready, 1)
                    else:
                        v.tensor_copy(probsAT[0:LAST_KEYS, 12, :], bank(0, P, slice(0, LAST_KEYS))).then_inc(s.pT_ready, 1)
                if before is not None:
                    mask_s()
                v.wait_ge(s.probsA_ready, T["probsA"].up())
                v.reciprocal(small[:, 3:4], small[:, 2:3]).then_inc(s.vec_step, 1)
                v.wait_ge(s.vec_step, own())
                v.wait_ge(s.av_ps, T["av"].up())
                v.tensor_scalar(att, bank(4, D), small[:, 3:4], None, ALU.mult).then_inc(s.att_ready, 1)
                if before is not None:
                    add_s(before)
                v.wait_ge(s.outA_ps, T["outA"].up())
                v.tensor_tensor(xi, bank(3, D, at=256), xi, ALU.add).then_inc(s.x_done, 1)
                T["x_done"].up()

            vec_pair_a(None, x[:, 0, :], x[:, 1, :])
            v.wait_ge(s.weights_in, WEIGHTS_IN)
            with v.Fori(1, TILES - 1) as i:
                enter("A", i, 1)
                vec_pair_a(tile_of_x(i - 1), tile_of_x(i), tile_of_x(i + 1))
            leave("A", TILES - 2, 1)
            vec_pair_a(x[:, TILES - 2, :], x[:, TILES - 1, :], None)
            norm_s(x[:, TILES - 1, :])
            mask_s()
            add_s(x[:, TILES - 1, :])
            v.wait_ge(s.x_done, XDONE_A)

            for n in range(3):
                v.memset(hpad[n], 0.0).then_inc(s.vec_step, 1)
            v.wait_ge(s.vec_step, T["step"].up(3))
            with v.Fori(0, CHUNKS) as c:
                enter("F", c)
                moments_of([x[:, bass.ds(c * TPC + k, 1), :].rearrange("p a n -> p (a n)") for k in range(TPC)], moments_f, mv_f)
                v.wait_ge(s.ln_rstd, T["rstd"].up())
                for k in range(TPC):
                    xk = x[:, bass.ds(c * TPC + k, 1), :].rearrange("p a n -> p (a n)")
                    v.tensor_scalar(xn_f[k], xk, mv_f[:, k, 0:1], rstd_f[:, 1, k:k + 1], ALU.subtract, ALU.mult).then_inc(s.vec_step, 1)
                for k in range(TPC):
                    v.wait_ge(s.vec_step, own())
                    v.tensor_reduce(small[:, k:k + 1], xn_f[k], AX, ALU.max, apply_absolute_value=True).then_inc(s.vec_step, 1)
                v.wait_ge(s.vec_step, T["step"].up(TPC))
                v.tensor_scalar(small[:, 8:12], small[:, 0:4], 1e-5, None, ALU.max).then_inc(s.vec_step, 1)
                v.wait_ge(s.vec_step, own())
                v.reciprocal(small[:, 4:8], small[:, 8:12]).then_inc(s.vec_step, 1)
                v.wait_ge(s.vec_step, own())
                v.tensor_scalar(small[:, 64:68], small[:, 4:8], 127.0, None, ALU.mult).then_inc(s.vec_step, 1)
                v.wait_ge(s.vec_step, own())
                for k in range(TPC):
                    v.tensor_scalar(xn_f[k], xn_f[k], small[:, 64 + k:65 + k], MAGIC, ALU.mult, ALU.add).then_inc(s.vec_step, 1)
                for k in range(TPC):
                    v.wait_ge(s.vec_step, own())
                    v.tensor_scalar(xq[k], xn_f[k], MAGIC, None, ALU.subtract).then_inc(s.xq_ready, 1)
                v.tensor_scalar(small[:, 12:16], small[:, 8:12], small[:, 84:85], None, ALU.mult).then_inc(s.vec_step, 1)
                v.wait_ge(s.vec_step, own())
                diagonals(12)
                v.wait_ge(s.rows_ready, T["rows"].up())
                for j in range(HT):
                    v.wait_ge(s.h_ps, T["h_ps"].up())
                    v.tensor_tensor(hpad[j % 3][:, :, 1:S + 1], bank(2 + j % 2).rearrange("p (b t) -> p b t", b=BPC),
                                    rowscale.rearrange("p (b t) -> p b t", b=BPC), ALU.mult).then_inc(s.h_scaled, 1)
                    if j >= 1:
                        side_taps(j - 1)
                side_taps(HT - 1)
                v.wait_ge(s.silu_done, T["silu"].up(HT))
                v.tensor_reduce(hmax, hs.rearrange("p j t -> p t j"), AX, ALU.max, apply_absolute_value=True).then_inc(s.hmax_ready, 1)
                v.wait_ge(s.hmaxT_ps, T["hmaxT"].up())
                v.tensor_reduce(small[:, 16:20], bank(4).rearrange("p (k t) -> p k t", k=TPC), AX, ALU.max).then_inc(s.vec_step, 1)
                v.wait_ge(s.vec_step, own())
                v.tensor_scalar(small[:, 20:24], small[:, 16:20], 1e-5, None, ALU.max).then_inc(s.vec_step, 1)
                v.wait_ge(s.vec_step, own())
                v.reciprocal(small[:, 24:28], small[:, 20:24]).then_inc(s.vec_step, 1)
                v.wait_ge(s.vec_step, own())
                v.tensor_scalar(small[:, 28:32], small[:, 24:28], 127.0, None, ALU.mult).then_inc(s.vec_step, 1)
                v.tensor_scalar(small[:, 32:36], small[:, 20:24], small[:, 85:86], None, ALU.mult).then_inc(s.vec_step, 1)
                v.wait_ge(s.vec_step, T["step"].up(2))
                diagonals(28)
                v.wait_ge(s.rows_ready, T["rows"].up())
                for j in range(HT):
                    if j % 2:
                        v.wait_ge(s.odd_scaled, T["odd"].up())
                    else:
                        v.tensor_tensor(hs[:, j, :], hs[:, j, :], rowscale, ALU.mult).then_inc(s.vec_step, 1)
                        v.wait_ge(s.vec_step, own())
                    v.tensor_scalar(hq[:, j, :], hs[:, j, :], MAGIC, MAGIC, ALU.add, ALU.subtract).then_inc(s.hq_ready, 1)
                for k in range(TPC):
                    xk = x[:, bass.ds(c * TPC + k, 1), :].rearrange("p a n -> p (a n)")
                    v.wait_ge(s.o_ps, T["o"].up())
                    v.scalar_tensor_tensor(xk, bank(6 + k % 2, D), small[:, 32 + k:33 + k], xk, ALU.mult, ALU.add).then_inc(s.x_done, 1)
                T["x_done"].up(TPC)
                v.wait_ge(s.x_done, T["x_done"].now())
            leave("F", CHUNKS)

            def end_batch(b):
                v.wait_ge(s.den_ps, T["den"].up())
                v.reciprocal(weighed_sb[:, :], bank(7, 256)).then_inc(s.vec_step, 1)
                v.wait_ge(s.vec_step, own())
                v.tensor_tensor(weighed_sb[:, :], bank(4, 256), weighed_sb[:, :], ALU.mult).then_inc(s.vec_step, 1)
                v.wait_ge(s.vec_step, own())
                wv = weighed_sb[:, :].rearrange("p (g h q) -> p g h q", g=KT, h=2)
                mine = attn_ch[:, :, b * S:b * S + S]
                v.tensor_scalar(mine, wv[:, :, 0, :], parity[:, 0:1], None, ALU.mult).then_inc(s.vec_step, 1)
                v.wait_ge(s.vec_step, own())
                v.scalar_tensor_tensor(mine, wv[:, :, 1, :], parity[:, 1:2], mine, ALU.mult, ALU.add).then_inc(s.attn_ready, 1)

            def maxima(b, first):
                for u in range(MAX_UNITS):
                    pair, half = divmod(u, 2)
                    width = HALF if half == 0 else NK - HALF
                    at = 1024 * ((u + 1) % 2)
                    v.wait_ge(s.mx_ps, T["mx"].up())
                    v.tensor_reduce(mpart[:, pair, half:half + 1], PS[:, at:at + width], AX, ALU.max).then_inc(s.mx_red, 1)
                    if u == 2 and not (first and b == 0):
                        end_batch(1 - b)
                v.wait_ge(s.mx_red, T["mx"].now())
                v.tensor_reduce(m8[:, 0:PAIRS], mpart[:, :, :], AX, ALU.max).then_inc(s.vec_step, 1)
                v.wait_ge(s.vec_step, own())
                v.tensor_copy(m8[:, 32:32 + PAIRS], m8[:, 0:PAIRS]).then_inc(s.m8_ready, 1)
                v.wait_ge(s.m8T_ps, T["m8T"].up())
                v.tensor_scalar(sh8[:, 0, :], bank(2, P, slice(0, 40)), -1.0, None, ALU.mult).then_inc(s.vec_step, 1)
                v.wait_ge(s.vec_step, own())
                v.scalar_tensor_tensor(sh8[:, 1, :], bank(2, P, slice(0, 40)), -1.0, sh8[:, 0, :], ALU.mult, ALU.subtract)\
                 .then_inc(s.vec_step, 1)
                v.wait_ge(s.vec_step, own())
                for part, rows in enumerate((slice(0, PAIRS), slice(32, 32 + PAIRS))):
                    v.tensor_tensor(shift[rows, :].rearrange("p (h q) -> p h q", h=PAIRS),
                                    sh8[rows, part, None, :].broadcast_to([PAIRS, PAIRS, P]),
                                    ident[rows, rows, None].broadcast_to([PAIRS, PAIRS, P]), ALU.mult).then_inc(s.shift_ready, 1)

            def finish(g, xi):
                if g == 0:
                    v.wait_ge(s.po_ps, T["po"].up())
                    v.tensor_tensor(xi, bank(7, D), xi, ALU.add).then_inc(s.vec_step, 1)
                    v.wait_ge(s.vec_step, own())
                    v.tensor_tensor(xi, xi, bias_p[:, :], ALU.add).then_inc(s.x_done, 1)
                    v.wait_ge(s.x_done, T["x_done"].up())
                    v.tensor_copy(carrier_v[:, :], eps[:, :])
                    moments(xi)
                if g == 1:
                    normalize(xi).then_inc(s.xn_ready, 1)
                if g in (4, 6, 8, 10):
                    q = (g - 4) // 2
                    if q >= 2:
                        v.wait_ge(s.p4T_ps, T["p4T"].up())
                    v.wait_ge(s.s4_ps, T["s4"].up())
                    v.tensor_tensor(s4[q % 2], bank(6).rearrange("p (h t) -> p h t", h=HPQ),
                                    causal[:, None, :].broadcast_to([P, HPQ, P]), ALU.add).then_inc(s.vec_step, 1)
                    v.wait_ge(s.vec_step, own())
                    v.tensor_reduce(s4_max, s4[q % 2], AX, ALU.max).then_inc(s.vec_step, 1)
                    v.wait_ge(s.vec_step, own())
                    v.tensor_scalar(s4_nmax[q % 2], s4_max, -(HD ** -0.5), None, ALU.mult).then_inc(s.s4_masked, 1)
                if g in (7, 9, 11, 13):
                    q = (g - 7) // 2
                    v.wait_ge(s.p4_ready, T["p4"].up(HPQ))
                    v.reciprocal(s4_inv[q % 2], s4_sum[q % 2]).then_inc(s.vec_step, 1)
                    v.wait_ge(s.vec_step, own())
                    v.wait_ge(s.o4_ps, T["o4"].up())
                    v.tensor_tensor(cat[:, q * HPQ * HD:(q + 1) * HPQ * HD].rearrange("p (h e) -> p h e", h=HPQ),
                                    bank(5, HPQ * HD).rearrange("p (h e) -> p h e", h=HPQ),
                                    s4_inv[q % 2][:, :, None].broadcast_to([P, HPQ, HD]), ALU.mult).then_inc(s.cat_ready, 1)
                if g == 15:
                    T["p4T"].up(2)
                    v.wait_ge(s.wo_ps, T["wo"].up())
                    for b in range(2):
                        rows = slice(b * S, b * S + S)
                        v.tensor_tensor(xi[rows, :], bank(5 + b, D, rows), xi[rows, :], ALU.add).then_inc(s.x_done, 1)
                    T["x_done"].up(2)

            def prepare(g, xi):
                if g == 17:
                    moments(xi)
                if g == 18:
                    normalize(xi).then_inc(s.xn_ready, 1)

            def vec_pair(before, after):
                for b in range(2):
                    maxima(b, before is None)
                    for t in range(KEY_TILES):
                        rows = slice(0, keys_of(t))
                        v.wait_ge(s.pr_ready, T["pr"].up())
                        if t == 0:
                            v.tensor_copy(probs_sum[:, :], probs[:, 0, :]).then_inc(s.sum_done, 1)
                        else:
                            v.wait_ge(s.sum_done, T["pr"].now(less=1))
                            v.tensor_tensor(probs_sum[rows, :], probs_sum[rows, :], probs[rows, t % PROBS, :], ALU.add).then_inc(s.sum_done, 1)
                        if before is not None:
                            finish(b * KEY_TILES + t, before)
                        if after is not None:
                            prepare(b * KEY_TILES + t, after)

            prepare(17, x[:, 0, :])
            prepare(18, x[:, 0, :])
            v.wait_ge(s.wkv_hi_ready, 1)
            v.tensor_tensor(wkv_lo[:, :, :].rearrange("p k n -> p (k n)"), wkv_raw,
                            wkv_hi[:, :, :].bitcast(F32).rearrange("p k n -> p (k n)"), ALU.subtract).then_inc(s.wkv_lo_ready, 1)
            vec_pair(None, x[:, 1, :])
            with v.Fori(1, TILES - 1) as i:
                enter("B", i, 1)
                vec_pair(tile_of_x(i - 1), tile_of_x(i + 1))
            leave("B", TILES - 2, 1)
            vec_pair(x[:, TILES - 2, :], None)
            end_batch(1)
            for g in range(16):
                finish(g, x[:, TILES - 1, :])
            v.wait_ge(s.x_done, XDONE_B)

            moments_of([x[:, k, :] for k in range(TILES)], moments_m, mv_m)
            v.wait_ge(s.ln_rstd, T["rstd"].up())
            with v.Fori(0, CHUNKS) as c:
                enter("M", c)
                for n in range(TPC):
                    v.tensor_scalar(xn_m[n][:, :], x[:, bass.ds(c * TPC + n, 1), :].rearrange("p a n -> p (a n)"),
                                    mv_m[:, bass.ds(c * TPC + n, 1), 0:1].rearrange("p a n -> p (a n)"),
                                    rstd_m[:, 1, bass.ds(c * TPC + n, 1)], ALU.subtract, ALU.mult).then_inc(s.xn_ready, 1)
                for n in range(TPC):
                    v.wait_ge(s.logits_ps, T["logits"].up())
                    v.tensor_copy(logits[:, bass.ds(c * TPC + n, 1), :].rearrange("p a e -> p (a e)"), bank(4 + n, EXPERTS)).then_inc(s.logits_sb, 1)
                    v.wait_ge(s.xT_all, T["xT"].up())
                    tokens = bass.ds((c * TPC + n) * P, P)
                    v.tensor_tensor(xT_lo[:, :, tokens], xnT_m[n][:, :, :], xT_hi[:, :, tokens].bitcast(F32), ALU.subtract).then_inc(s.xT_lo_all, 1)
            leave("M", CHUNKS)
            v.wait_ge(s.logits_sb, TILES)

            def rows16(at):
                return small[:, at:at + TILES]

            def wide(a):
                return a[:, :, None].broadcast_to([P, TILES, EXPERTS])

            ranks = rank[:, None, :].broadcast_to([P, TILES, EXPERTS])
            v.tensor_reduce(rows16(0), logits, AX, ALU.max).then_inc(s.vec_step, 1)
            v.wait_ge(s.vec_step, own())
            v.tensor_tensor(logits, logits, wide(rows16(0)), ALU.subtract).then_inc(s.rexp_in, 1)
            v.wait_ge(s.rexp_out, 1)

            def first_of_largest(p, largest, hot):
                v.tensor_reduce(largest, p, AX, ALU.max).then_inc(s.vec_step, 1)
                v.wait_ge(s.vec_step, own())
                v.tensor_tensor(rc, p, wide(largest), ALU.is_equal).then_inc(s.vec_step, 1)
                v.wait_ge(s.vec_step, own())
                v.tensor_tensor(rc, rc, ranks, ALU.mult).then_inc(s.vec_step, 1)
                v.wait_ge(s.vec_step, own())
                v.tensor_reduce(rows16(32), rc, AX, ALU.max).then_inc(s.vec_step, 1)
                v.wait_ge(s.vec_step, own())
                v.tensor_tensor(hot, rc, wide(rows16(32)), ALU.is_equal).then_inc(s.vec_step, 1)
                v.wait_ge(s.vec_step, own())

            first_of_largest(rp, rows16(0), ro1)
            v.scalar_tensor_tensor(rp, ro1, -4.0, rp, ALU.mult, ALU.add).then_inc(s.vec_step, 1)
            v.wait_ge(s.vec_step, own())
            first_of_largest(rp, rows16(16), ro2)
            v.tensor_tensor(rows16(32), rows16(0), rows16(16), ALU.add).then_inc(s.vec_step, 1)
            v.wait_ge(s.vec_step, own())
            v.reciprocal(rows16(48), rows16(32)).then_inc(s.vec_step, 1)
            v.wait_ge(s.vec_step, own())
            v.tensor_tensor(rc, ro1, wide(rows16(0)), ALU.mult).then_inc(s.vec_step, 1)
            v.tensor_tensor(rp, ro2, wide(rows16(16)), ALU.mult).then_inc(s.vec_step, 1)
            v.tensor_tensor(ro1, ro1, ro2, ALU.add).then_inc(s.vec_step, 1)
            v.wait_ge(s.vec_step, T["step"].up(3))
            v.tensor_tensor(rc, rc, rp, ALU.add).then_inc(s.vec_step, 1)
            v.wait_ge(s.vec_step, own())
            v.tensor_tensor(rc, rc, wide(rows16(48)), ALU.mult).then_inc(s.vec_step, 1)
            v.wait_ge(s.vec_step, own())
            v.tensor_reduce(rsmall[:, 0:EXPERTS], rc.rearrange("p t e -> p e t"), AX, ALU.add).then_inc(s.vec_step, 1)
            v.tensor_reduce(rsmall[:, EXPERTS:2 * EXPERTS], ro1.rearrange("p t e -> p e t"), AX, ALU.add).then_inc(s.vec_step, 1)
            v.wait_ge(s.vec_step, T["step"].up(2))
            v.tensor_copy(rsmall[:, 40:56], rsmall[:, 0:16]).then_inc(s.rsum_ready, 1)
            v.wait_ge(s.rsum_ps, 1)
            v.tensor_scalar(rsmall[:, 16:24], bank(3, EXPERTS, at=EXPERTS), 1.0, None, ALU.max).then_inc(s.vec_step, 1)
            v.wait_ge(s.vec_step, own())
            v.reciprocal(rsmall[:, 24:32], rsmall[:, 16:24]).then_inc(s.vec_step, 1)
            v.wait_ge(s.vec_step, own())
            v.tensor_tensor(rsmall[:, 32:40], bank(3, EXPERTS), rsmall[:, 24:32], ALU.mult).then_inc(s.vec_step, 1)
            v.wait_ge(s.vec_step, own())
            v.tensor_tensor(gates[:, :, :], ro1, rsmall[:, None, 32:40].broadcast_to([P, TILES, EXPERTS]), ALU.mult).then_inc(s.gates_ready, 1)
            v.wait_ge(s.gates_ready, 1)

            def add_output(e, step):
                for k in range(TPC):
                    c = step % CHUNKS
                    v.wait_ge(s.eo_ps, e * (STEPS * TPC) + step * TPC + k + 1)
                    xk = x[:, c * TPC + k, :]
                    gate = gates[:, c * TPC + k, e:e + 1] if isinstance(e, int) else gates[:, c * TPC + k, bass.ds(e, 1)]
                    v.scalar_tensor_tensor(xk, bank(4 + k, D), gate, xk, ALU.mult, ALU.add).then_inc(s.eo_added, 1)

            def vec_expert(e, first):
                for step in range(STEPS):
                    for j in range(UJ):
                        m = step * UJ + j
                        v.wait_ge(s.silu_g_ready, e * (STEPS * UJ) + m + 1)
                        v.wait_ge(s.u_ps, e * (STEPS * UJ) + m + 1)
                        if m >= 2 or not first:
                            v.wait_ge(s.h_lo_ready, e * (STEPS * UJ) + m - 1)
                        v.tensor_tensor(hidden[m % 2][:, :], bank(2 + m % 2), silu_g[m % 2][:, :], ALU.mult).then_inc(s.hidden_ready, 1)
                    if step:
                        add_output(e, step - 1)
                    elif not first:
                        add_output(e - 1, STEPS - 1)

            vec_expert(0, True)
            with v.Fori(1, EXPERTS) as e:
                vec_expert(e, False)
            add_output(EXPERTS - 1, STEPS - 1)


def kernel(**inputs):
    import numpy as np
    import concourse.bacc as bacc
    from concourse import mybir as mb
    from concourse.bass_utils import run_bass_kernel_spmd

    a = {k: np.asarray(v) for k, v in inputs.items()}

    def rows(m):
        return np.ascontiguousarray(m.reshape(-1, P, m.shape[-1]).transpose(1, 0, 2))

    def by_head(m):
        out = np.zeros((P, KT, P), m.dtype)
        for h in range(HEADS):
            r = (h % HPT) * HD
            out[r:r + HD, h // HPT, r:r + HD] = m[h]
        return out

    ctx = a["ctx_1024"]
    ctxT = np.zeros((B, P, KT, NKP), ctx.dtype)
    ctxT[:, :, :, :NK] = ctx.transpose(0, 2, 1).reshape(B, KT, P, NK).transpose(0, 2, 1, 3)
    ctxN = np.zeros((B, KEY_TILES * P, D), ctx.dtype)
    ctxN[:, :NK] = ctx
    ctxN = ctxN.reshape(B, KEY_TILES, P, D).transpose(0, 2, 1, 3)

    def unit(e, half):
        mine = slice(half * HID // 2, (half + 1) * HID // 2)
        three = a["L1_ffn_gate_w"][e, mine].T, a["L1_ffn_up_w"][e, mine].T, a["L1_ffn_down_w"][e, :, mine].T
        return np.concatenate([rows(m).reshape(P, -1) for m in three], axis=1)

    wo = a["L1_attn_W_O"].reshape(4, 64, D).transpose(1, 0, 2)
    arrays = {
        "x": a["x"].reshape(TILES, P, D).transpose(1, 0, 2),
        "ctxT": ctxT.reshape(B, P, KT * NKP),
        "ctxN": ctxN.reshape(B, P, KEY_TILES * D),
        "w_xqT": rows(a["L0_xattn_Wq"].T), "w_xkT": rows(a["L0_xattn_Wk"].T), "w_xv": rows(a["L0_xattn_Wv"]),
        "w_sq": rows(a["L0_attn_Wq"]), "w_sk": rows(a["L0_attn_Wk"]), "w_sv": rows(a["L0_attn_Wv"]),
        "w1T": rows(a["L0_ffn_w1"].T).reshape(P, -1), "w2T": rows(a["L0_ffn_w2"].T).reshape(P, -1),
        "conv_w": rows(a["L0_ffn_conv_w"].reshape(HID, 3)), "conv_b": a["L0_ffn_conv_b"].reshape(HT, P).T,
        "w_kv": rows(a["L1_xattn_W_kv"]).reshape(P, -1), "w_cq": rows(a["L1_xattn_W_q"]), "w_cp": rows(a["L1_xattn_W_proj"]),
        "b_p": np.broadcast_to(a["L1_xattn_b_proj"], (P, D)),
        "w_hq": by_head(a["L1_attn_Wq"]), "w_hk": by_head(a["L1_attn_Wk"]), "w_hv": by_head(a["L1_attn_Wv"]),
        "w_o": np.concatenate([wo, wo]),
        "w_router": rows(a["L1_ffn_router_w"].T),
        "experts": np.stack([unit(e, half) for e in range(EXPERTS) for half in range(2)]),
    }
    nc = bacc.Bacc("TRN2", target_bir_lowering=False, num_devices=1)
    fed, io = {}, {}
    for name, m in arrays.items():
        fed[f"in_{name}"] = np.ascontiguousarray(m)
        io[name] = nc.dram_tensor(f"in_{name}", m.shape, mb.dt.from_np(m.dtype), kind="ExternalInput").ap()
    out = nc.dram_tensor("out", (P, TILES, D), F32, kind="ExternalOutput").ap()
    build(nc, io, out)
    got = run_bass_kernel_spmd(nc, [fed], core_ids=[0]).results[0]["out"]
    return np.ascontiguousarray(got.transpose(1, 0, 2)).reshape(B, S, D)
```
